# Optimizing a Trainium2 kernel written in Bass

```python
import numpy as np
import jax
import jax.numpy as jnp

def _softmax(x, axis=-1):
    return jax.nn.softmax(x, axis=axis)

def _gelu(x):
    return jax.nn.gelu(x, approximate=True)

def _silu(x):
    return jax.nn.silu(x)

def _sigmoid(x):
    return jax.nn.sigmoid(x)

def _layernorm(x, axis=-1, eps=1e-05):
    m = jnp.mean(x, axis=axis, keepdims=True)
    v = jnp.var(x, axis=axis, keepdims=True)
    return (x - m) / jnp.sqrt(v + eps)

def _scatter_add(tgt, idx, src, axis=0):
    return tgt.at[idx].add(src)

def _segment_sum(src, seg, n):
    return jax.ops.segment_sum(src, seg, n)
kernel_name = 'mk_seq_postln_d2_jaxref_r4_7ae0bc'

def setup_inputs(seed: int=0):
    np.random.seed(seed)
    _w = jnp.asarray

    def _L0_attn_setup():
        import jax, jax.numpy as jnp
        import numpy as np
        B, T, C, H = (4, 1024, 512, 16)
        Dh = C // H

        def _feature_map(x):
            return jax.nn.elu(x) + 1.0
        key = jax.random.key(seed)
        ks = jax.random.split(key, 7)
        s = 0.02
        return {'x': jax.random.normal(ks[0], (B, T, C), dtype=jnp.float32), 'cos': jax.random.uniform(ks[1], (T, Dh), dtype=jnp.float32), 'sin': jax.random.uniform(ks[2], (T, Dh), dtype=jnp.float32), 'Wq': jax.random.normal(ks[3], (C, C), dtype=jnp.float32) * s, 'Wk': jax.random.normal(ks[4], (C, C), dtype=jnp.float32) * s, 'Wv': jax.random.normal(ks[5], (C, C), dtype=jnp.float32) * s, 'Wo': jax.random.normal(ks[6], (C, C), dtype=jnp.float32) * s}
    _L0_attn_in = _L0_attn_setup()

    def _L0_ffn_setup():
        import jax, jax.numpy as jnp
        import numpy as np
        _FP4_LUT = jnp.array([0.0, 0.5, 1.0, 1.5, 2.0, 3.0, 4.0, 6.0, -0.0, -0.5, -1.0, -1.5, -2.0, -3.0, -4.0, -6.0], dtype=jnp.float32)
        GROUP_SIZE = 128
        EPS = 1e-06

        def _dequant_fp4(packed_i32, scales_f16, group_size):
            out_f, in_p = packed_i32.shape
            w = packed_i32.astype(jnp.uint32)
            shifts = jnp.arange(8, dtype=jnp.uint32) * 4
            nib = w[:, :, None] >> shifts & jnp.uint32(15)
            vals = _FP4_LUT[nib.astype(jnp.int32)].reshape(out_f, in_p * 8)
            s = scales_f16.astype(jnp.float32).T
            s_full = jnp.repeat(s, group_size, axis=1)
            return vals * s_full
        key = jax.random.key(seed)
        k1, k2, k3, k4, k5 = jax.random.split(key, 5)
        B, S, H, I = (4, 512, 512, 1408)
        x = jax.random.normal(k1, (B, S, H), dtype=jnp.float32)
        gate_up_packed = jax.random.randint(k2, (2 * I, H // 8), 0, 2147483647, dtype=jnp.int32)
        gate_up_scales = jax.random.uniform(k3, (H // GROUP_SIZE, 2 * I), dtype=jnp.float32).astype(jnp.float16)
        down_packed = jax.random.randint(k4, (H, I // 8), 0, 2147483647, dtype=jnp.int32)
        down_scales = jax.random.uniform(k5, (I // GROUP_SIZE, H), dtype=jnp.float32).astype(jnp.float16)
        return {'x': x, 'gate_up_packed': gate_up_packed, 'gate_up_scales': gate_up_scales, 'down_packed': down_packed, 'down_scales': down_scales}
    _L0_ffn_in = _L0_ffn_setup()

    def _L1_attn_setup():
        import jax, jax.numpy as jnp
        import numpy as np
        from jax import lax
        B, L, H = (2, 1024, 512)
        NH = 16
        DK = H // NH
        C = 64
        EPS = 1e-05
        N_LAYER = 24

        def _gla_chunk(q, k, v, gf):
            b, Ls, dk = q.shape
            dv = v.shape[-1]
            n = Ls // C
            qc = q.reshape(b, n, C, dk).transpose(1, 0, 2, 3)
            kc = k.reshape(b, n, C, dk).transpose(1, 0, 2, 3)
            vc = v.reshape(b, n, C, dv).transpose(1, 0, 2, 3)
            gc = gf.reshape(b, n, C, dk).transpose(1, 0, 2, 3)
            Bc = jnp.cumsum(gc, axis=2)
            tril = jnp.tril(jnp.ones((C, C), bool))

            def step(S, inp):
                qh, kh, vh, Bh = inp
                Blast = Bh[:, -1, :]
                D = Bh[:, :, None, :] - Bh[:, None, :, :]
                A = jnp.einsum('bid,bjd,bijd->bij', qh, kh, jnp.exp(D))
                A = jnp.where(tril, A, 0.0)
                o_intra = jnp.einsum('bij,bjv->biv', A, vh)
                o_inter = jnp.einsum('bid,bdv->biv', qh * jnp.exp(Bh), S)
                kd = kh * jnp.exp(Blast[:, None, :] - Bh)
                S_new = S * jnp.exp(Blast)[..., None] + jnp.einsum('bjd,bjv->bdv', kd, vh)
                return (S_new, o_intra + o_inter)
            S0 = jnp.zeros((b, dk, dv), q.dtype)
            _, o = lax.scan(step, S0, (qc, kc, vc, Bc))
            return o.transpose(1, 0, 2, 3).reshape(b, Ls, dv)
        key = jax.random.key(seed)
        ks = jax.random.split(key, 7)
        std = 0.02
        return {'hidden_states': jax.random.normal(ks[0], (B, L, H), jnp.float32), 'Wq': jax.random.normal(ks[1], (DK, H), jnp.float32) * std, 'Wk': jax.random.normal(ks[2], (DK, H), jnp.float32) * std, 'Wog': jax.random.normal(ks[3], (H, H), jnp.float32) * std, 'Wig': jax.random.normal(ks[4], (H, H), jnp.float32) * std, 'Wo': jax.random.normal(ks[5], (H, H), jnp.float32) * (std / np.sqrt(2 * N_LAYER)), 'g_norm_w': jnp.ones((H,), jnp.float32)}
    _L1_attn_in = _L1_attn_setup()

    def _L1_ffn_setup():
        import jax, jax.numpy as jnp
        import numpy as np
        B, S, D, DFF = (4, 1024, 512, 2048)
        CAPACITY_FACTOR = 0.5
        K = int(CAPACITY_FACTOR * S)
        key = jax.random.key(seed)
        ks = jax.random.split(key, 5)
        hidden_states = jax.random.normal(ks[0], (B, S, D), dtype=jnp.float32)
        router_weight = jax.random.normal(ks[1], (D,), dtype=jnp.float32) * 0.02
        router_bias = jnp.zeros((1,), dtype=jnp.float32)
        w1 = jax.random.normal(ks[2], (D, DFF), dtype=jnp.float32) * (1.0 / np.sqrt(D))
        b1 = jnp.zeros((DFF,), dtype=jnp.float32)
        w2 = jax.random.normal(ks[3], (DFF, D), dtype=jnp.float32) * (1.0 / np.sqrt(DFF))
        b2 = jnp.zeros((D,), dtype=jnp.float32)
        return {'hidden_states': hidden_states, 'router_weight': router_weight, 'router_bias': router_bias, 'w1': w1, 'b1': b1, 'w2': w2, 'b2': b2}
    _L1_ffn_in = _L1_ffn_setup()
    _d = {'L0_attn_x': _L0_attn_in['x'], 'L0_attn_cos': _L0_attn_in['cos'], 'L0_attn_sin': _L0_attn_in['sin'], 'L0_attn_Wq': _L0_attn_in['Wq'], 'L0_attn_Wk': _L0_attn_in['Wk'], 'L0_attn_Wv': _L0_attn_in['Wv'], 'L0_attn_Wo': _L0_attn_in['Wo'], 'L0_ffn_gate_up_packed': _L0_ffn_in['gate_up_packed'], 'L0_ffn_gate_up_scales': _L0_ffn_in['gate_up_scales'], 'L0_ffn_down_packed': _L0_ffn_in['down_packed'], 'L0_ffn_down_scales': _L0_ffn_in['down_scales'], 'L1_attn_Wq': _L1_attn_in['Wq'], 'L1_attn_Wk': _L1_attn_in['Wk'], 'L1_attn_Wog': _L1_attn_in['Wog'], 'L1_attn_Wig': _L1_attn_in['Wig'], 'L1_attn_Wo': _L1_attn_in['Wo'], 'L1_attn_g_norm_w': _L1_attn_in['g_norm_w'], 'L1_ffn_router_weight': _L1_ffn_in['router_weight'], 'L1_ffn_router_bias': _L1_ffn_in['router_bias'], 'L1_ffn_w1': _L1_ffn_in['w1'], 'L1_ffn_b1': _L1_ffn_in['b1'], 'L1_ffn_w2': _L1_ffn_in['w2'], 'L1_ffn_b2': _L1_ffn_in['b2']}
    _x0 = _d['L0_attn_x']
    _d['L0_attn_x'] = jax.random.normal(jax.random.fold_in(jax.random.key(seed), 1), (2, 1024, 512), dtype=_x0.dtype)
    del _x0
    return _d

def reference(L0_attn_x, L0_attn_cos, L0_attn_sin, L0_attn_Wq, L0_attn_Wk, L0_attn_Wv, L0_attn_Wo, L0_ffn_gate_up_packed, L0_ffn_gate_up_scales, L0_ffn_down_packed, L0_ffn_down_scales, L1_attn_Wq, L1_attn_Wk, L1_attn_Wog, L1_attn_Wig, L1_attn_Wo, L1_attn_g_norm_w, L1_ffn_router_weight, L1_ffn_router_bias, L1_ffn_w1, L1_ffn_b1, L1_ffn_w2, L1_ffn_b2):

    def _L0_attn_ref(x, cos, sin, Wq, Wk, Wv, Wo):
        import jax, jax.numpy as jnp
        import numpy as np
        B, T, C, H = (4, 1024, 512, 16)
        Dh = C // H

        def _feature_map(x):
            return jax.nn.elu(x) + 1.0
        b, t, c = x.shape
        h, dh = (H, c // H)

        def proj(W):
            y = jnp.einsum('btc,oc->bto', x, W)
            return y.reshape(b, t, h, dh).transpose(0, 2, 1, 3)
        q = _feature_map(proj(Wq))
        k = _feature_map(proj(Wk))
        v = proj(Wv)
        kv = jnp.einsum('bhtd,bhte->bhde', k, v)
        z = 1.0 / (jnp.einsum('bhtd,bhd->bht', q, k.sum(axis=2)) + 1e-06)
        out = jnp.einsum('bhtd,bhde,bht->bhte', q, kv, z)
        out = out.transpose(0, 2, 1, 3).reshape(b, t, c)
        return jnp.einsum('btc,oc->bto', out, Wo)

    def _L0_ffn_ref(x, gate_up_packed, gate_up_scales, down_packed, down_scales):
        import jax, jax.numpy as jnp
        import numpy as np
        _FP4_LUT = jnp.array([0.0, 0.5, 1.0, 1.5, 2.0, 3.0, 4.0, 6.0, -0.0, -0.5, -1.0, -1.5, -2.0, -3.0, -4.0, -6.0], dtype=jnp.float32)
        GROUP_SIZE = 128
        EPS = 1e-06

        def _dequant_fp4(packed_i32, scales_f16, group_size):
            out_f, in_p = packed_i32.shape
            w = packed_i32.astype(jnp.uint32)
            shifts = jnp.arange(8, dtype=jnp.uint32) * 4
            nib = w[:, :, None] >> shifts & jnp.uint32(15)
            vals = _FP4_LUT[nib.astype(jnp.int32)].reshape(out_f, in_p * 8)
            s = scales_f16.astype(jnp.float32).T
            s_full = jnp.repeat(s, group_size, axis=1)
            return vals * s_full
        I = gate_up_packed.shape[0] // 2
        w_gu = _dequant_fp4(gate_up_packed, gate_up_scales, GROUP_SIZE)
        w_down = _dequant_fp4(down_packed, down_scales, GROUP_SIZE)
        gate_up = jnp.einsum('bsh,oh->bso', x, w_gu)
        gate, up = (gate_up[..., :I], gate_up[..., I:])
        h = jax.nn.silu(gate) * up
        y = jnp.einsum('bsi,hi->bsh', h, w_down)
        rms = jnp.sqrt(jnp.mean(y * y, axis=-1, keepdims=True) + EPS)
        return y / rms

    def _L1_attn_ref(hidden_states, Wq, Wk, Wog, Wig, Wo, g_norm_w):
        import jax, jax.numpy as jnp
        import numpy as np
        from jax import lax
        B, L, H = (2, 1024, 512)
        NH = 16
        DK = H // NH
        C = 64
        EPS = 1e-05
        N_LAYER = 24

        def _gla_chunk(q, k, v, gf):
            b, Ls, dk = q.shape
            dv = v.shape[-1]
            n = Ls // C
            qc = q.reshape(b, n, C, dk).transpose(1, 0, 2, 3)
            kc = k.reshape(b, n, C, dk).transpose(1, 0, 2, 3)
            vc = v.reshape(b, n, C, dv).transpose(1, 0, 2, 3)
            gc = gf.reshape(b, n, C, dk).transpose(1, 0, 2, 3)
            Bc = jnp.cumsum(gc, axis=2)
            tril = jnp.tril(jnp.ones((C, C), bool))

            def step(S, inp):
                qh, kh, vh, Bh = inp
                Blast = Bh[:, -1, :]
                D = Bh[:, :, None, :] - Bh[:, None, :, :]
                A = jnp.einsum('bid,bjd,bijd->bij', qh, kh, jnp.exp(D))
                A = jnp.where(tril, A, 0.0)
                o_intra = jnp.einsum('bij,bjv->biv', A, vh)
                o_inter = jnp.einsum('bid,bdv->biv', qh * jnp.exp(Bh), S)
                kd = kh * jnp.exp(Blast[:, None, :] - Bh)
                S_new = S * jnp.exp(Blast)[..., None] + jnp.einsum('bjd,bjv->bdv', kd, vh)
                return (S_new, o_intra + o_inter)
            S0 = jnp.zeros((b, dk, dv), q.dtype)
            _, o = lax.scan(step, S0, (qc, kc, vc, Bc))
            return o.transpose(1, 0, 2, 3).reshape(b, Ls, dv)
        x = hidden_states
        q = jax.nn.softmax(x @ Wq.T, axis=-1)
        k = jax.nn.sigmoid(x @ Wk.T)
        v = x
        gf = jax.nn.log_sigmoid(-k)
        o = _gla_chunk(q, k, v, gf)
        go = o @ Wog.T + x @ Wig.T
        on = o * lax.rsqrt(jnp.mean(o * o, axis=-1, keepdims=True) + EPS) * g_norm_w
        o = on * (go * jax.nn.sigmoid(go))
        return o @ Wo.T

    def _L1_ffn_ref(hidden_states, router_weight, router_bias, w1, b1, w2, b2):
        import jax, jax.numpy as jnp
        import numpy as np
        B, S, D, DFF = (4, 1024, 512, 2048)
        CAPACITY_FACTOR = 0.5
        K = int(CAPACITY_FACTOR * S)
        b, s, d = hidden_states.shape
        scores = jnp.einsum('bsd,d->bs', hidden_states, router_weight) + router_bias[0]
        top_scores, indices = jax.lax.top_k(scores, K)
        weights = jax.nn.sigmoid(top_scores)
        selected = jnp.take_along_axis(hidden_states, indices[:, :, None], axis=1)
        h = jax.nn.gelu(jnp.einsum('bkd,df->bkf', selected, w1) + b1)
        processed = jnp.einsum('bkf,fd->bkd', h, w2) + b2
        weighted = processed * weights[:, :, None]
        flat = hidden_states.reshape(b * s, d)
        flat_idx = (indices + jnp.arange(b)[:, None] * s).reshape(-1)
        out = flat.at[flat_idx].add(weighted.reshape(b * K, d))
        return out.reshape(b, s, d)
    x = L0_attn_x
    x = _layernorm(x + _L0_attn_ref(x, L0_attn_cos, L0_attn_sin, L0_attn_Wq, L0_attn_Wk, L0_attn_Wv, L0_attn_Wo), axis=-1)
    x = _layernorm(x + _L0_ffn_ref(x, L0_ffn_gate_up_packed, L0_ffn_gate_up_scales, L0_ffn_down_packed, L0_ffn_down_scales), axis=-1)
    x = _layernorm(x + _L1_attn_ref(x, L1_attn_Wq, L1_attn_Wk, L1_attn_Wog, L1_attn_Wig, L1_attn_Wo, L1_attn_g_norm_w), axis=-1)
    x = _layernorm(x + _L1_ffn_ref(x, L1_ffn_router_weight, L1_ffn_router_bias, L1_ffn_w1, L1_ffn_b1, L1_ffn_w2, L1_ffn_b2), axis=-1)
    return x

_drawn_inputs = setup_inputs


def setup_inputs(seed=0):
    import zlib

    import numpy as np

    out = dict(_drawn_inputs(seed))
    spreads = {'L1_attn_g_norm_w': (1.0, 0.6), 'L1_ffn_b1': (0.0, 0.542), 'L1_ffn_b2': (0.0, 0.365)}
    factors = {'L0_attn_Wq': 8.0,
     'L0_attn_Wk': 8.0,
     'L0_attn_Wv': 6.115,
     'L0_attn_Wo': 6.081,
     'L1_attn_Wq': 8.0,
     'L1_attn_Wk': 8.0,
     'L1_attn_Wog': 4.808,
     'L1_attn_Wig': 2.831}
    for name, (base, spread) in spreads.items():
        noise = np.random.default_rng([zlib.crc32(name.encode()), seed]).standard_normal(out[name].shape)
        drawn = base * np.exp(spread * noise) if base else spread * noise
        out[name] = jnp.asarray(drawn.astype(out[name].dtype))
    for name, factor in factors.items():
        out[name] = (out[name] * factor).astype(out[name].dtype)
    return out
```

```python
from contextlib import ExitStack

import concourse.bass as bass
from concourse import mybir

F32 = mybir.dt.float32
F32R = mybir.dt.float32r
F16 = mybir.dt.float16
BF16 = mybir.dt.bfloat16
I32 = mybir.dt.int32
U16 = mybir.dt.uint16
ALU = mybir.AluOpType
ACT = mybir.ActivationFunctionType
AX = mybir.AxisListType
ds = bass.ds

P = 128
NB = 2
T = 1024
C = 512
KC = C // P
BLK = 512
TB = BLK // P
NBLK = NB * T // BLK
HEADS = 16
DH = C // HEADS
HG = P // DH
LN_EPS = 1e-5


class Steps:

    def __init__(self, engine, sem, per_turn):
        self.engine, self.sem, self.per_turn = engine, sem, per_turn

    def turn(self, it):
        self.base, self.k = it * self.per_turn, 0

    def done(self, ins):
        ins.then_inc(self.sem, 1)
        self.k += 1
        self.engine.wait_ge(self.sem, self.base + self.k)

    def end(self):
        assert self.k == self.per_turn, (self.k, self.per_turn)


def three_products(pe, out, lh, ll, rh, rl, first, last):
    pe.matmul(out, lh, rh, start=first, stop=False)
    pe.matmul(out, ll, rh, start=False, stop=False)
    return pe.matmul(out, lh, rl, start=False, stop=last)


def layer_norm_block(dve, n, r, st, mv, var, rstd, filler, s_r, s_st, s_ag, s_var, s_rstd, s_out):
    for t in range(TB):
        dve.wait_ge(s_r, TB * n + t + 1)
        dve.bn_stats(st[:, t, :], r[:, t, :]).then_inc(s_st, 1)
    dve.wait_ge(s_st, TB * n + TB)
    dve.memset(filler[:, :], 0.0)
    for t in range(TB):
        dve.bn_aggr(mv[:, t, :], st[:, t, :]).then_inc(s_ag, 1)
    dve.wait_ge(s_ag, TB * n + TB)
    dve.tensor_scalar(var[:, :], mv[:, :, 1], LN_EPS, None, ALU.add).then_inc(s_var, 1)
    dve.wait_ge(s_rstd, n + 1)
    for t in range(TB):
        dve.tensor_scalar(r[:, t, :], r[:, t, :], mv[:, t, 0:1], rstd[:, t:t + 1], ALU.subtract,
                          ALU.mult).then_inc(s_out, 1)


def clear_semaphores(nc, sems):
    nc.clear_and_free_semaphores(sems)
    nc.all_engine_barrier()


class Constants:

    def __init__(self, nc, ctx):
        def sb(name, shape, dt=F32):
            return ctx.enter_context(nc.sbuf_tensor(name, shape, dt))

        self.ident = sb("ident", [P, P])
        self.ones = sb("ones", [P, P])
        self.before = sb("before", [P, P])
        self.head_mask = sb("head_mask", [P, P])
        self.upto = sb("upto", [P, P])
        self.within = sb("within", [P, P])
        self.to_half = sb("to_half", [P, P])
        self.minus_half = sb("minus_half", [P, TB])
        s_set = ctx.enter_context(nc.semaphore("const_set"))
        s_mat = ctx.enter_context(nc.semaphore("const_matrices"))
        s_done = ctx.enter_context(nc.semaphore("const_done"))
        with nc.Block() as block:
            @block.gpsimd
            def _(pool):
                pool.memset(self.minus_half[:, :], -0.5)
                pool.memset(self.ones[:, :], 1.0)
                pool.memset(self.head_mask[:, :], 1.0).then_inc(s_set, 1)
                pool.wait_ge(s_set, 1)
                pool.affine_select(out=self.ident[:, :], in_=self.ones[:, :], compare_op=ALU.is_equal, fill=0.0,
                                   base=0, pattern=[[-1, P]], channel_multiplier=1)
                pool.affine_select(out=self.before[:, :], in_=self.ones[:, :], compare_op=ALU.is_gt, fill=0.0,
                                   base=0, pattern=[[-1, P]], channel_multiplier=1)
                for m in (self.upto, self.within):
                    pool.affine_select(out=m[:, :], in_=self.ones[:, :], compare_op=ALU.is_ge, fill=0.0,
                                       base=0, pattern=[[1, P]], channel_multiplier=-1)
                pool.memset(self.to_half[:, :], 0.0).then_inc(s_mat, 1)
                pool.wait_ge(s_mat, 1)
                h = P // 2
                pool.memset(self.within[0:h, h:P], 0.0).then_inc(s_mat, 1)
                pool.wait_ge(s_mat, 2)
                pool.tensor_copy(self.to_half[0:h, 0:h], self.before[0:h, 0:h]).then_inc(s_mat, 1)
                pool.wait_ge(s_mat, 3)
                pool.tensor_scalar(self.to_half[h:P, h:P], self.upto[h:P, h:P], -1.0, None, ALU.mult).then_inc(s_mat, 1)
                pool.wait_ge(s_mat, 4)
                v = self.head_mask[:, :].rearrange("p (h e) -> p h e", e=DH)
                pool.affine_select(out=v, in_=v, compare_op=ALU.is_ge, fill=0.0, base=0,
                                   pattern=[[-DH, HG], [0, DH]], channel_multiplier=1).then_inc(s_set, 1)
                pool.wait_ge(s_set, 2)
                pool.affine_select(out=v, in_=v, compare_op=ALU.is_ge, fill=0.0, base=DH - 1,
                                   pattern=[[DH, HG], [0, DH]], channel_multiplier=-1).then_inc(s_done, 1)
                pool.wait_ge(s_done, 1)




def linear_attention(nc, x, xT, wT, woT, x1, const):
    ctx, sems = ExitStack(), []
    ctx.callback(clear_semaphores, nc, sems)
    with ctx:
        def sb(name, shape, dt=F32):
            return ctx.enter_context(nc.sbuf_tensor(name, shape, dt))

        def sem(name):
            sems.append(nc.alloc_semaphore(name))
            return sems[-1]

        NW = 4
        NT = T // P
        w_raw = [sb(f"w_raw{i}", [P, KC, C]) for i in range(NW)]
        w_hi = [sb(f"w_hi{i}", [P, KC, C], F32R) for i in range(NW)]
        w_lo = [sb(f"w_lo{i}", [P, KC, C], F32R) for i in range(NW)]
        xt_raw = [sb(f"xt_raw{i}", [P, KC, BLK]) for i in range(2)]
        xt_hi = sb("xt_hi", [P, KC, BLK], F32R)
        xt_lo = sb("xt_lo", [P, KC, BLK], F32R)
        q = [sb(f"q{i}", [P, KC, BLK]) for i in range(2)]
        k = [sb(f"k{i}", [P, C]) for i in range(2)]
        v1 = [sb(f"v1_{i}", [P, KC, P + 1]) for i in range(2)]
        e_k = sb("e_k", [P, C])
        e_q = sb("e_q", [P, C])
        kvz = sb("kvz", [P, KC, P + HG])
        z = sb("z", [P, HEADS])
        zi = [sb(f"zi{i}", [P, HEADS]) for i in range(2)]
        att = [sb(f"att{i}", [P, C]) for i in range(2)]
        at_hi = [sb(f"at_hi{i}", [P, KC, P], F32R) for i in range(2)]
        at_lo = [sb(f"at_lo{i}", [P, KC, P], F32R) for i in range(2)]
        x_res = [sb(f"x_res{i}", [P, C]) for i in range(4)]
        r = [sb(f"r{i}", [P, C]) for i in range(3)]
        x_out = [sb(f"x_out{i}", [P, C]) for i in range(2)]
        st = [sb(f"st{i}", [P, 6]) for i in range(3)]
        mv = [sb(f"mv{i}", [P, 2]) for i in range(3)]
        filler = sb("filler", [P, 1])
        var = [sb(f"var{i}", [P, 1]) for i in range(2)]
        rstd = [sb(f"rstd{i}", [P, 1]) for i in range(2)]

        ps = ctx.enter_context(nc.psum_tensor("ps_attn", [P, 8, 512], F32))
        KV0, PROJ, QP, TP, YP = 0, 2, 6, 6, 0

        s_w = [sem(f"w_loaded{i}") for i in range(NW)]
        s_wh = sem("w_hi_done")
        s_wl = sem("w_lo_done")
        s_xt = [sem(f"xt_loaded{i}") for i in range(2)]
        s_xth = sem("xt_hi_done")
        s_xtl = sem("xt_lo_done")
        s_proj = sem("k_v_projected")
        s_ek = sem("k_exp_done")
        s_k = sem("k_ready")
        s_v = sem("v_ready")
        s_ones = sem("ones_ready")
        s_kvt = sem("kv_tile_added")
        s_q = sem("q_projected")
        s_eq = sem("q_exp_done")
        s_qr = sem("q_ready")
        s_kv = sem("kv_masked")
        s_num = sem("num_done")
        s_att = sem("att_ready")
        s_tp = sem("att_transposed")
        s_ath = sem("att_hi_done")
        s_atl = sem("att_lo_done")
        s_y = sem("out_projected")
        s_xr = [sem(f"x_res_loaded{i}") for i in range(4)]
        s_r = sem("residual_added")
        s_var = sem("var_ready")
        s_rstd = sem("rstd_ready")
        s_out = sem("x_out_ready")
        s_st = [sem(f"x_out_stored{i}") for i in range(2)]
        s_dve = sem("dve_step_attn")

        block = ctx.enter_context(nc.Block())

        @block.sync
        def _(sp):
            sp.dma_start(xt_raw[0][:, :, :], xT[:, :, 0:BLK]).then_inc(s_xt[0], 16)
            for i in range(NW):
                sp.dma_start(w_raw[i][:, :, :], (wT[i] if i < 3 else woT)).then_inc(s_w[i], 16)
            with sp.Fori(0, NB) as b:
                for h in range(2):
                    nxt = b * 2 + 1 if h == 0 else (b * 2 + 2) % (NB * 2)
                    sp.wait_ge(s_xth, 2 * b + h)
                    sp.wait_ge(s_xtl, 2 * b + h)
                    sp.dma_start(xt_raw[1 - h][:, :, :], xT[:, :, ds(nxt * BLK, BLK)]).then_inc(s_xt[1 - h], 16)
                for t in range(NT):
                    sp.wait_ge(s_r, b * NT + max(0, t - 3))
                    sp.dma_start(x_res[t % 4][:, :], x[b * NT + t, :, :]).then_inc(s_xr[t % 4], 16)

        @block.scalar
        def _(act):
            for i in range(NW):
                act.wait_ge(s_w[i], 16)
                act.activation(w_hi[i][:, :, :], w_raw[i][:, :, :], ACT.Copy).then_inc(s_wh, 1)
            with act.Fori(0, NB) as b:
                for h in range(2):
                    act.wait_ge(s_xt[h], 16 * (b + 1))
                    act.wait_ge(s_q, 8 * b + 4 * h)
                    act.activation(xt_hi[:, :, :], xt_raw[h][:, :, :], ACT.Copy).then_inc(s_xth, 1)
                    for t in range(TB):
                        n = TB * h + t
                        act.wait_ge(s_proj, NT * b + n + 1)
                        act.wait_ge(s_k, NT * b + n)
                        act.activation(e_k[:, :], ps[:, PROJ + 2 * (n % 2), :], ACT.Exp).then_inc(s_ek, 1)
                        act.wait_ge(s_kvt, NT * b + max(0, n - 1))
                        act.wait_ge(s_ones, 2)
                        act.activation(v1[n % 2][:, :, 0:P], ps[:, PROJ + 2 * (n % 2) + 1, :].rearrange("p (g e) -> p g e", g=KC),
                                       ACT.Copy).then_inc(s_v, 1)
                    for m in range(KC):
                        act.wait_ge(s_q, 8 * b + 4 * h + m + 1)
                        act.wait_ge(s_qr, 8 * b + 4 * h + m)
                        act.activation(e_q[:, :], ps[:, QP + m % 2, :], ACT.Exp).then_inc(s_eq, 1)
                for t in range(NT):
                    act.wait_ge(s_tp, NT * b + t + 1)
                    act.wait_ge(s_y, NT * b + max(0, t - 1))
                    act.activation(at_hi[t % 2][:, :, :], ps[:, TP + t % 2, :].rearrange("p (k n) -> p k n", k=KC),
                                   ACT.Copy).then_inc(s_ath, 1)

        @block.vector
        def _(dve):
            steps = Steps(dve, s_dve, NT + 2 * KC + 4 * NT)

            def normalise(u, b):
                dve.wait_ge(s_rstd, NT * b + u + 1)
                dve.wait_ge(s_st[u % 2], 16 * (NT // 2 * b + u // 2))
                dve.tensor_scalar(x_out[u % 2][:, :], r[u % 3][:, :], mv[u % 3][:, 0:1], rstd[u % 2][:, :],
                                  ALU.subtract, ALU.mult).then_inc(s_out, 1)

            for i in range(2):
                dve.memset(v1[i][:, :, P:P + 1], 1.0).then_inc(s_ones, 1)
            for i in range(NW):
                dve.wait_ge(s_wh, i + 1)
                dve.tensor_tensor(w_lo[i][:, :, :], w_raw[i][:, :, :], w_hi[i][:, :, :].bitcast(F32),
                                  ALU.subtract).then_inc(s_wl, 1)
            with dve.Fori(0, NB) as b:
                steps.turn(b)
                for h in range(2):
                    for t in range(TB):
                        n = TB * h + t
                        dve.wait_ge(s_ek, NT * b + n + 1)
                        dve.wait_ge(s_kvt, NT * b + max(0, n - 1))
                        steps.done(dve.tensor_scalar(e_k[:, :], e_k[:, :], 1.0, None, ALU.min))
                        dve.scalar_tensor_tensor(out=k[n % 2][:, :], in0=ps[:, PROJ + 2 * (n % 2), :], scalar=0.0,
                                                 in1=e_k[:, :], op0=ALU.max, op1=ALU.add).then_inc(s_k, 1)
                    for m in range(KC):
                        dve.wait_ge(s_eq, 8 * b + 4 * h + m + 1)
                        steps.done(dve.tensor_scalar(e_q[:, :], e_q[:, :], 1.0, None, ALU.min))
                        dve.scalar_tensor_tensor(out=q[h][:, m, :], in0=ps[:, QP + m % 2, :], scalar=0.0,
                                                 in1=e_q[:, :], op0=ALU.max, op1=ALU.add).then_inc(s_qr, 1)
                dve.wait_ge(s_kvt, NT * b + NT)
                kvp = ps[:, KV0:KV0 + 2, 0:2 * (P + 1)].rearrange("p a (g e) -> p a g e", g=2)
                for a in range(2):
                    dve.tensor_tensor(kvz[:, 2 * a:2 * a + 2, 0:P], kvp[:, a, :, 0:P],
                                      const.head_mask[:, :].unsqueeze(1).to_broadcast([P, 2, P]), ALU.mult)
                    ins = dve.tensor_tensor(kvz[:, 2 * a:2 * a + 2, P:P + HG],
                                            kvp[:, a, :, P:P + 1].to_broadcast([P, 2, HG]),
                                            const.head_mask[:, 0:P:DH].unsqueeze(1).to_broadcast([P, 2, HG]), ALU.mult)
                ins.then_inc(s_kv, 1)
                for t in range(NT + 2):
                    if t < NT:
                        num = ps[:, PROJ + 2 * (t % 2):PROJ + 2 * (t % 2) + 2, 0:2 * (P + HG)].rearrange("p a (g e) -> p a g e", g=2)
                        dve.wait_ge(s_num, NT * b + t + 1)
                        dve.wait_ge(s_tp, NT * b + max(0, t - 1))
                        for a in range(2):
                            ins = dve.tensor_scalar(z[:, 8 * a:8 * a + 8].rearrange("p (g h) -> p g h", g=2), num[:, a, :, P:P + HG], 1e-6, None, ALU.add)
                        steps.done(ins)
                        steps.done(dve.reciprocal(zi[t % 2][:, :], z[:, :]))
                        for a in range(2):
                            ins = dve.tensor_tensor(
                                att[t % 2][:, 256 * a:256 * a + 256].rearrange("p (g h e) -> p g h e", g=2, h=HG),
                                num[:, a, :, 0:P].rearrange("p g (h e) -> p g h e", h=HG),
                                zi[t % 2][:, 8 * a:8 * a + 8].rearrange("p (g h) -> p g h", g=2).unsqueeze(3).to_broadcast([P, 2, HG, DH]),
                                ALU.mult)
                        ins.then_inc(s_att, 1)
                    if 1 <= t <= NT:
                        u = t - 1
                        dve.wait_ge(s_ath, NT * b + u + 1)
                        dve.wait_ge(s_y, NT * b + max(0, u - 1))
                        dve.tensor_tensor(at_lo[u % 2][:, :, :], ps[:, TP + u % 2, :].rearrange("p (k n) -> p k n", k=KC),
                                          at_hi[u % 2][:, :, :].bitcast(F32), ALU.subtract).then_inc(s_atl, 1)
                    if 2 <= t:
                        u = t - 2
                        dve.wait_ge(s_y, NT * b + u + 1)
                        dve.wait_ge(s_xr[u % 4], 16 * (NT // 4 * b + u // 4 + 1))
                        dve.wait_ge(s_out, NT * b + max(0, u - 2))
                        dve.tensor_tensor(r[u % 3][:, :], ps[:, YP + u % 2, :], x_res[u % 4][:, :], ALU.add).then_inc(s_r, 1)
                        dve.wait_ge(s_r, NT * b + u + 1)
                        steps.done(dve.bn_stats(st[u % 3][:, :], r[u % 3][:, :]))
                        dve.memset(filler[:, :], 0.0)
                        steps.done(dve.bn_aggr(mv[u % 3][:, :], st[u % 3][:, :]))
                        dve.tensor_scalar(var[u % 2][:, :], mv[u % 3][:, 1:2], LN_EPS, None, ALU.add).then_inc(s_var, 1)
                    if 3 <= t:
                        normalise(t - 3, b)
                normalise(NT - 1, b)
                steps.end()

        @block.gpsimd
        def _(pool):
            with pool.Fori(0, NB) as b:
                for h in range(2):
                    pool.wait_ge(s_xth, 2 * b + h + 1)
                    pool.wait_ge(s_q, 8 * b + 4 * h)
                    pool.tensor_tensor(xt_lo[:, :, :], xt_raw[h][:, :, :], xt_hi[:, :, :].bitcast(F32),
                                       ALU.subtract).then_inc(s_xtl, 1)
                for t in range(NT):
                    pool.wait_ge(s_var, NT * b + t + 1)
                    pool.tensor_tensor(rstd[t % 2][:, :], var[t % 2][:, :], const.minus_half[:, 0:1], ALU.pow).then_inc(s_rstd, 1)
                    pool.wait_ge(s_out, NT * b + t + 1)
                    pool.dma_start(x1[b * NT + t, :, :], x_out[t % 2][:, :]).then_inc(s_st[t % 2], 16)
            for i in range(2):
                pool.wait_ge(s_st[i], 16 * NB * NT // 2)

        @block.tensor
        def _(pe):
            with pe.Fori(0, NB) as b:
                def add_kv(n):
                    pe.wait_ge(s_k, NT * b + n + 1)
                    pe.wait_ge(s_v, NT * b + n + 1)
                    if n == 0:
                        pe.wait_ge(s_r, NT * b)
                    for g in range(KC):
                        ins = pe.matmul(ps[:, KV0 + g // 2, (g % 2) * (P + 1):(g % 2 + 1) * (P + 1)],
                                        k[n % 2][:, g * P:(g + 1) * P], v1[n % 2][:, g, :],
                                        start=(n == 0 and g % 2 == 0), stop=(n == NT - 1), skip_group_check=True)
                    ins.then_inc(s_kvt, 1)

                for h in range(2):
                    pe.wait_ge(s_xth, 2 * b + h + 1)
                    pe.wait_ge(s_xtl, 2 * b + h + 1)
                    for t in range(TB):
                        n = TB * h + t
                        bank = PROJ + 2 * (n % 2)
                        if n < 2:
                            pe.wait_ge(s_att, NT * b)
                        else:
                            pe.wait_ge(s_k, NT * b + n - 1)
                            pe.wait_ge(s_v, NT * b + n - 1)
                        for i in range(2):
                            pe.wait_ge(s_wh, i + 1)
                            pe.wait_ge(s_wl, i + 1)
                            for c in range(KC):
                                ins = three_products(pe, ps[:, bank + i, :], xt_hi[:, c, t * P:(t + 1) * P],
                                                     xt_lo[:, c, t * P:(t + 1) * P], w_hi[i][:, c, :], w_lo[i][:, c, :],
                                                     c == 0, c == KC - 1)
                        ins.then_inc(s_proj, 1)
                        if n >= 1:
                            add_kv(n - 1)
                    for m in range(KC):
                        if m < 2 and h == 0:
                            pe.wait_ge(s_atl, NT * b)
                        else:
                            pe.wait_ge(s_qr, 8 * b + 4 * h + m - 1)
                        pe.wait_ge(s_wh, 3)
                        pe.wait_ge(s_wl, 3)
                        for c in range(KC):
                            ins = three_products(pe, ps[:, QP + m % 2, :], w_hi[2][:, c, m * P:(m + 1) * P],
                                                 w_lo[2][:, c, m * P:(m + 1) * P], xt_hi[:, c, :], xt_lo[:, c, :],
                                                 c == 0, c == KC - 1)
                        ins.then_inc(s_q, 1)
                        if h == 1 and m == 0:
                            add_kv(NT - 1)
                for t in range(NT + 2):
                    if t < NT:
                        h, col = t // TB, (t % TB) * P
                        if t == 0:
                            pe.wait_ge(s_kv, b + 1)
                        if t < 2:
                            pe.wait_ge(s_k, NT * b + NT)
                            pe.wait_ge(s_v, NT * b + NT)
                        else:
                            pe.wait_ge(s_att, NT * b + t - 1)
                        pe.wait_ge(s_qr, 8 * b + 4 * h + 4)
                        for g in range(KC):
                            ins = pe.matmul(ps[:, PROJ + 2 * (t % 2) + g // 2, (g % 2) * (P + HG):(g % 2 + 1) * (P + HG)],
                                            q[h][:, g, col:col + P], kvz[:, g, :], start=True, stop=True)
                        ins.then_inc(s_num, 1)
                    if 1 <= t <= NT:
                        u = t - 1
                        pe.wait_ge(s_att, NT * b + u + 1)
                        if u < 2:
                            pe.wait_ge(s_qr, 8 * b + 8)
                        else:
                            pe.wait_ge(s_atl, NT * b + u - 1)
                            pe.wait_ge(s_ath, NT * b + u - 1)
                        for m in range(KC):
                            ins = pe.transpose(ps[:, TP + u % 2, m * P:(m + 1) * P], att[u % 2][:, m * P:(m + 1) * P], const.ident[:, :])
                        ins.then_inc(s_tp, 1)
                    if t >= 2:
                        u = t - 2
                        pe.wait_ge(s_ath, NT * b + u + 1)
                        pe.wait_ge(s_atl, NT * b + u + 1)
                        if u < 2:
                            pe.wait_ge(s_kv, b + 1)
                        else:
                            pe.wait_ge(s_r, NT * b + u - 1)
                        pe.wait_ge(s_wl, 4)
                        for c in range(KC):
                            ins = three_products(pe, ps[:, YP + u % 2, :], at_hi[u % 2][:, c, :], at_lo[u % 2][:, c, :],
                                                 w_hi[3][:, c, :], w_lo[3][:, c, :], c == 0, c == KC - 1)
                        ins.then_inc(s_y, 1)


I_FF = 1408
IT = I_FF // P
NIB = 8
RMS_EPS = 1e-6
SIGN_AND_MAGNITUDE = -0x72000000
FP16_UNBIAS = 16384.0


def fp4_feed_forward(nc, x1, gu_packed, gu_scales, dn_packed, dn_scales, x2, const):
    ctx, sems = ExitStack(), []
    ctx.callback(clear_semaphores, nc, sems)
    with ctx:
        def sb(name, shape, dt=F32):
            return ctx.enter_context(nc.sbuf_tensor(name, shape, dt))

        def sem(name):
            sems.append(nc.alloc_semaphore(name))
            return sems[-1]

        gu_hi = sb("gu_hi", [P, 2 * IT, KC, P], F32R)
        gu_lo = sb("gu_lo", [P, 2 * IT, KC, P], F32R)
        dn_hi = sb("dn_hi", [P, IT, C], F32R)
        dn_lo = sb("dn_lo", [P, IT, C], F32R)
        packed = [sb(f"packed{i}", [P, C], I32) for i in range(2)]
        nib = [sb(f"nib{i}", [P, C], I32) for i in range(2)]
        scale = [sb(f"scale{i}", [P, C], F16) for i in range(2)]
        scale_hi = [sb(f"scale_hi{i}", [P, C], F16) for i in range(2)]
        scale_lo = [sb(f"scale_lo{i}", [P, C], F16) for i in range(2)]
        shift = sb("shift", [P, 1], I32)
        lane = sb("lane", [P, 1], I32)
        xs = sb("xs", [P, TB, C])
        xt_hi = sb("fxt_hi", [P, KC, BLK], F32R)
        xt_lo = sb("fxt_lo", [P, KC, BLK], F32R)
        sg = [sb(f"sg{i}", [P, BLK]) for i in range(2)]
        h = [sb(f"h{i}", [P, BLK]) for i in range(2)]
        h_hi = [sb(f"h_hi{i}", [P, BLK], F32R) for i in range(2)]
        h_lo = [sb(f"h_lo{i}", [P, BLK], F32R) for i in range(2)]
        ss = sb("ss", [P, TB])
        rms = sb("rms", [P, TB])
        r = sb("fr", [P, TB, C])
        st = sb("fst", [P, TB, 6])
        mv = sb("fmv", [P, TB, 2])
        filler = sb("ffiller", [P, 1])
        var = sb("fvar", [P, TB])
        rstd = sb("frstd", [P, TB])

        ps = ctx.enter_context(nc.psum_tensor("ps_fp4", [P, 8, 512], F32))
        Y, G = 0, 4

        NCH = 3 * IT
        s_ln = sem("lane_ready")
        s_sh = sem("shift_ready")
        s_pk = [sem(f"packed_loaded{i}") for i in range(2)]
        s_sc = [sem(f"scale_loaded{i}") for i in range(2)]
        s_n1 = sem("nibble_shifted")
        s_n2 = sem("nibble_masked")
        s_s1 = sem("scale_hi_done")
        s_s2 = sem("scale_lo_done")
        s_wh = sem("fw_hi_done")
        s_wl = sem("fw_lo_done")
        s_x = sem("xs_loaded")
        s_tp = sem("x_transposed")
        s_xth = sem("fxt_hi_done")
        s_xtl = sem("fxt_lo_done")
        s_gu = sem("gate_up_projected")
        s_sg = sem("silu_done")
        s_h = sem("h_ready")
        s_hh = sem("h_hi_done")
        s_hl = sem("h_lo_done")
        s_dn = sem("down_added")
        s_ss = sem("squares_summed")
        s_ms = sem("mean_square_ready")
        s_rms = sem("rms_ready")
        s_y = sem("y_taken")
        s_r = sem("fresidual_added")
        s_st = sem("fstats_done")
        s_ag = sem("faggregated")
        s_var = sem("fvar_ready")
        s_rstd = sem("frstd_ready")
        s_out = sem("fx_out_ready")
        s_sto = sem("fx_out_stored")

        block = ctx.enter_context(nc.Block())

        def chunk(n):
            j, part = n // 3, n % 3
            if part < 2:
                o = part * IT + j
                return (gu_packed[:, :, o * P:(o + 1) * P], gu_scales[:, o * P:(o + 1) * P],
                        gu_hi[:, o, :, :], gu_lo[:, o, :, :], KC)
            return dn_packed[j * (P // NIB):(j + 1) * (P // NIB), :], dn_scales[j:j + 1, :], dn_hi[:, j, :], dn_lo[:, j, :], 1

        @block.sync
        def _(sp):
            for n in range(NCH):
                words, scales, _, _, k = chunk(n)
                if n >= 2:
                    sp.wait_ge(s_n1, n - 1)
                    sp.wait_ge(s_s2, n - 1)
                if k == 1:
                    sp.dma_start(packed[n % 2][:, :], words.unsqueeze(1).to_broadcast([P // NIB, NIB, C])).then_inc(s_pk[n % 2], 16)
                    sp.dma_start(scale[n % 2][:, :], scales.to_broadcast([P, C])).then_inc(s_sc[n % 2], 16)
                else:
                    for kk in range(KC):
                        sp.dma_start(packed[n % 2][:, kk * P:(kk + 1) * P],
                                     words[:, kk, :].unsqueeze(1).to_broadcast([P // NIB, NIB, P])).then_inc(s_pk[n % 2], 16)
                    sp.dma_start(scale[n % 2][:, :].rearrange("p (k o) -> p k o", k=KC),
                                 scales.unsqueeze(0).to_broadcast([P, KC, P])).then_inc(s_sc[n % 2], 16)
                if n == 0:
                    sp.dma_start(xs[:, :, :], x1[0:TB, :, :].rearrange("t p c -> p t c")).then_inc(s_x, 16)
            with sp.Fori(0, NBLK) as b:
                sp.wait_ge(s_out, TB * b + TB)
                sp.dma_start(x2[ds(TB * b, TB), :, :].rearrange("t p c -> p t c"), r[:, :, :]).then_inc(s_sto, 16)
                sp.dma_start(xs[:, :, :], x1[ds((b + 1) % NBLK * TB, TB), :, :].rearrange("t p c -> p t c")).then_inc(s_x, 16)
            sp.wait_ge(s_sto, 16 * NBLK)
            sp.wait_ge(s_x, 16 * (NBLK + 1))

        @block.scalar
        def _(act):
            with act.Fori(0, NBLK) as b:
                for c in range(KC):
                    act.wait_ge(s_tp, KC * b + c + 1)
                    act.activation(xt_hi[:, c, :], ps[:, G + c, :], ACT.Copy).then_inc(s_xth, 1)

                def h_high(j):
                    act.wait_ge(s_h, IT * b + j + 1)
                    act.wait_ge(s_dn, IT * b + max(0, j - 1))
                    act.activation(h_hi[j % 2][:, :], h[j % 2][:, :], ACT.Copy).then_inc(s_hh, 1)

                for j in range(IT):
                    act.wait_ge(s_gu, IT * b + j + 1)
                    act.wait_ge(s_h, IT * b + max(0, j - 1))
                    act.activation(sg[j % 2][:, :], ps[:, G + 2 * (j % 2), :], ACT.Silu).then_inc(s_sg, 1)
                    h_high(j)
                act.wait_ge(s_dn, IT * b + IT)
                act.wait_ge(s_sto, 16 * b)
                for t in range(TB):
                    act.activation(r[:, t, :], ps[:, Y + t, :], ACT.Square, accum_out=ss[:, t:t + 1]).then_inc(s_ss, 1)

        @block.vector
        def _(dve):
            dve.wait_ge(s_ln, 1)
            dve.tensor_scalar(lane[:, :], lane[:, :], NIB - 1, 2, ALU.bitwise_and, ALU.logical_shift_left).then_inc(s_sh, 1)
            dve.wait_ge(s_sh, 1)
            dve.tensor_scalar(shift[:, :], lane[:, :], -1.0, 28.0, ALU.mult, ALU.add).then_inc(s_sh, 1)
            dve.wait_ge(s_sh, 2)
            for n in range(NCH):
                _, _, hi, lo, k = chunk(n)
                i = n % 2
                dve.wait_ge(s_pk[i], 16 * sum(chunk(m)[4] for m in range(i, n + 1, 2)))
                if n >= 2:
                    dve.wait_ge(s_wh, n - 1)
                    dve.wait_ge(s_wl, n - 1)
                dve.tensor_scalar(nib[i][:, :], packed[i][:, :], shift[:, 0:1], 3, ALU.logical_shift_left,
                                  ALU.arith_shift_right).then_inc(s_n1, 1)
                dve.wait_ge(s_sc[i], 16 * (n // 2 + 1))
                dve.tensor_scalar(scale_hi[i][:, :].bitcast(U16), scale[i][:, :].bitcast(U16), 0xFFFE, None,
                                  ALU.bitwise_and).then_inc(s_s1, 1)
                dve.wait_ge(s_n1, n + 1)
                dve.tensor_scalar(nib[i][:, :], nib[i][:, :], SIGN_AND_MAGNITUDE, None, ALU.bitwise_and).then_inc(s_n2, 1)
                dve.wait_ge(s_s1, n + 1)
                dve.tensor_tensor(scale_lo[i][:, :], scale[i][:, :], scale_hi[i][:, :], ALU.subtract).then_inc(s_s2, 1)
                dve.wait_ge(s_n2, n + 1)
                value = nib[i][:, :].bitcast(F16)[:, 1:2 * C:2]
                shaped = (lambda a: a.rearrange("p (k o) -> p k o", k=KC)) if k == KC else (lambda a: a)
                dve.scalar_tensor_tensor(out=hi, in0=shaped(value), scalar=FP16_UNBIAS, in1=shaped(scale_hi[i][:, :]),
                                         op0=ALU.mult, op1=ALU.mult).then_inc(s_wh, 1)
                dve.wait_ge(s_s2, n + 1)
                dve.scalar_tensor_tensor(out=lo, in0=shaped(value), scalar=FP16_UNBIAS, in1=shaped(scale_lo[i][:, :]),
                                         op0=ALU.mult, op1=ALU.mult).then_inc(s_wl, 1)
            with dve.Fori(0, NBLK) as b:
                for c in range(KC):
                    dve.wait_ge(s_xth, KC * b + c + 1)
                    dve.tensor_tensor(xt_lo[:, c, :], ps[:, G + c, :], xt_hi[:, c, :].bitcast(F32), ALU.subtract).then_inc(s_xtl, 1)
                for j in range(IT):
                    dve.wait_ge(s_sg, IT * b + j + 1)
                    dve.wait_ge(s_hl, IT * b + max(0, j - 1))
                    dve.wait_ge(s_hh, IT * b + max(0, j - 1))
                    dve.tensor_tensor(h[j % 2][:, :], sg[j % 2][:, :], ps[:, G + 2 * (j % 2) + 1, :], ALU.mult).then_inc(s_h, 1)
                dve.wait_ge(s_ss, TB * b + TB)
                dve.tensor_scalar(ss[:, :], ss[:, :], 1.0 / C, RMS_EPS, ALU.mult, ALU.add).then_inc(s_ms, 1)
                dve.wait_ge(s_rms, b + 1)
                dve.wait_ge(s_x, 16 * (b + 1))
                for t in range(TB):
                    dve.scalar_tensor_tensor(out=r[:, t, :], in0=ps[:, Y + t, :], scalar=rms[:, t:t + 1], in1=xs[:, t, :],
                                             op0=ALU.mult, op1=ALU.add).then_inc(s_r, 1)
                layer_norm_block(dve, b, r, st, mv, var, rstd, filler, s_r, s_st, s_ag, s_var, s_rstd, s_out)

        @block.gpsimd
        def _(pool):
            pool.iota(lane[:, :], pattern=[[0, 1]], base=0, channel_multiplier=1).then_inc(s_ln, 1)
            with pool.Fori(0, NBLK) as b:
                for j in range(IT):
                    pool.wait_ge(s_hh, IT * b + j + 1)
                    pool.tensor_tensor(h_lo[j % 2][:, :], h[j % 2][:, :], h_hi[j % 2][:, :].bitcast(F32), ALU.subtract).then_inc(s_hl, 1)
                pool.wait_ge(s_ms, b + 1)
                pool.tensor_tensor(rms[:, :], ss[:, :], const.minus_half[:, :], ALU.pow).then_inc(s_rms, 1)
                pool.wait_ge(s_var, b + 1)
                pool.tensor_tensor(rstd[:, :], var[:, :], const.minus_half[:, :], ALU.pow).then_inc(s_rstd, 1)

        @block.tensor
        def _(pe):
            with pe.Fori(0, NBLK) as b:
                def gate_up(j):
                    if j < 2:
                        pe.wait_ge(s_h, IT * b)
                        pe.wait_ge(s_xtl, KC * b + KC)
                    else:
                        pe.wait_ge(s_h, IT * b + j - 1)
                    for part in range(2):
                        pe.wait_ge(s_wh, 3 * j + part + 1)
                        pe.wait_ge(s_wl, 3 * j + part + 1)
                        o = part * IT + j
                        for c in range(KC):
                            ins = three_products(pe, ps[:, G + 2 * (j % 2) + part, :], gu_hi[:, o, c, :], gu_lo[:, o, c, :],
                                                 xt_hi[:, c, :], xt_lo[:, c, :], c == 0, c == KC - 1)
                    ins.then_inc(s_gu, 1)

                def down(j):
                    pe.wait_ge(s_hh, IT * b + j + 1)
                    pe.wait_ge(s_hl, IT * b + j + 1)
                    pe.wait_ge(s_wh, 3 * j + 3)
                    pe.wait_ge(s_wl, 3 * j + 3)
                    if j == 0:
                        pe.wait_ge(s_r, TB * b)
                    for t in range(TB):
                        ins = three_products(pe, ps[:, Y + t, :], h_hi[j % 2][:, t * P:(t + 1) * P], h_lo[j % 2][:, t * P:(t + 1) * P],
                                             dn_hi[:, j, :], dn_lo[:, j, :], j == 0, j == IT - 1)
                    ins.then_inc(s_dn, 1)

                pe.wait_ge(s_x, 16 * (b + 1))
                pe.wait_ge(s_h, IT * b)
                for c in range(KC):
                    for t in range(TB):
                        ins = pe.transpose(ps[:, G + c, t * P:(t + 1) * P], xs[:, t, c * P:(c + 1) * P], const.ident[:, :])
                    ins.then_inc(s_tp, 1)
                gate_up(0)
                for j in range(1, IT):
                    gate_up(j)
                    down(j - 1)
                down(IT - 1)


HALF = 64
DK = 32
GLA_EPS = 1e-5


def gated_linear_attention(nc, x2, wqkT, wogT, wigT, woT, norm_w, x3, const):
    ctx, sems = ExitStack(), []
    ctx.callback(clear_semaphores, nc, sems)
    with ctx:
        def sb(name, shape, dt=F32):
            return ctx.enter_context(nc.sbuf_tensor(name, shape, dt))

        def sem(name):
            sems.append(nc.alloc_semaphore(name))
            return sems[-1]

        WQK, WIG, WOG, WO = range(4)
        NW = 4
        w_cols = [P, C, C, C]
        w_raw = [sb(f"gw_raw{i}", [P, KC, w_cols[i]]) for i in range(NW)]
        w_hi = [sb(f"gw_hi{i}", [P, KC, w_cols[i]], F32R) for i in range(NW)]
        w_lo = [sb(f"gw_lo{i}", [P, KC, w_cols[i]], F32R) for i in range(NW)]
        nw = sb("norm_w_sb", [P, KC])
        xs = [sb(f"gxs{i}", [P, TB, C]) for i in range(2)]
        xt_hi = sb("gxt_hi", [P, KC, BLK], F32R)
        xt_lo = sb("gxt_lo", [P, KC, BLK], F32R)
        qk_f = sb("qk_f", [P, BLK])
        q_max = sb("q_max", [P, TB])
        q_sum = sb("q_sum", [P, TB])
        q_inv = sb("q_inv", [P, TB])
        qx = sb("qx", [P, TB, DK])
        qs = sb("qs", [P, TB, DK])
        kx = sb("kx", [P, TB, DK])
        ks = sb("ks", [P, TB, DK])
        sp = sb("sp", [P, TB, DK])
        decay = sb("decay", [P, 4, TB, DK])
        grow = sb("grow", [P, TB, DK])
        QH, QT, KA, KB = range(4)
        feats = sb("feats", [P, 4, TB, DK])
        k_end = sb("k_end", [P, TB, DK])
        ft = [sb(f"ft{i}", [DK, 4, P]) for i in range(2)]
        at = [sb(f"gat{i}", [P, P]) for i in range(2)]
        state = sb("state", [DK, C])
        dec = sb("dec", [DK, TB])
        o_f = sb("o_f", [P, KC, BLK])
        o_hi = sb("o_hi", [P, KC, BLK], F32R)
        o_lo = sb("o_lo", [P, KC, BLK], F32R)
        sq = sb("sq", [P, KC, P])
        sg = [sb(f"gsg{i}", [P, BLK]) for i in range(2)]
        p_hi = sb("p_hi", [P, KC, BLK], F32R)
        p_lo = sb("p_lo", [P, KC, BLK], F32R)
        ms = sb("ms", [P, TB])
        rms = sb("grms", [P, TB])
        r = sb("gr", [P, TB, C])
        st = sb("gst", [P, TB, 6])
        mv = sb("gmv", [P, TB, 2])
        var = sb("gvar", [P, TB])
        rstd = sb("grstd", [P, TB])
        filler = sb("gfiller", [P, 1])

        ps = ctx.enter_context(nc.psum_tensor("ps_gla", [P, 8, 512], F32))
        F, A, S, O, GO = 0, 1, 2, 3, 4
        D_COL, SS_COL = 128, 132

        s_nw = sem("norm_w_loaded")
        s_w = [sem(f"gw_loaded{i}") for i in range(NW)]
        s_fold = sem("norm_w_folded")
        s_wh = sem("gw_hi_done")
        s_wl = sem("gw_lo_done")
        s_x = [sem(f"gx_loaded{i}") for i in range(2)]
        s_tp = sem("gx_transposed")
        s_xth = sem("gxt_hi_done")
        s_xtl = sem("gxt_lo_done")
        s_qk = sem("qk_projected")
        s_qkf = sem("qk_taken")
        s_tok = sem("qk_transposed")
        s_qx = sem("q_shifted")
        s_qe = sem("q_exp_done_gla")
        s_ke = sem("k_exp_done_gla")
        s_ks = sem("k_sigmoid_done")
        s_k2 = sem("k_exp2_done")
        s_sp = sem("softplus_done")
        s_sum = sem("gate_sums_done")
        s_dec = sem("decays_done")
        s_ft = sem("feats_ready")
        s_ftt = sem("feats_transposed")
        s_fts = sem("feats_taken")
        s_a = sem("scores_done")
        s_at = sem("scores_masked")
        s_su = sem("state_update_done")
        s_dexp = sem("state_decay_ready")
        s_s = sem("state_ready")
        s_o = sem("o_done")
        s_of = sem("o_copied")
        s_sq = sem("o_squared")
        s_oh = sem("o_hi_done")
        s_ol = sem("o_lo_done")
        s_ss = sem("o_squares_summed")
        s_go = sem("go_done")
        s_sg = sem("gsilu_done")
        s_p = sem("p_ready")
        s_ph = sem("p_hi_done")
        s_pl = sem("p_lo_done")
        s_y = sem("gy_done")
        s_ms = sem("gmean_square_ready")
        s_rms = sem("grms_ready")
        s_r = sem("gresidual_added")
        s_st = sem("gstats_done")
        s_ag = sem("gaggregated")
        s_var = sem("gvar_ready")
        s_rstd = sem("grstd_ready")
        s_out = sem("gx_out_ready")
        s_sto = sem("gx_out_stored")
        s_dve = sem("dve_step_gla")

        block = ctx.enter_context(nc.Block())

        @block.sync
        def _(sp_):
            sp_.dma_start(xs[0][:, :, :], x2[0:TB, :, :].rearrange("t p c -> p t c")).then_inc(s_x[0], 16)
            sp_.dma_start(w_raw[WQK][:, :, 0:2 * DK], wqkT).then_inc(s_w[WQK], 16)
            sp_.dma_start(w_raw[WQK][:, :, 2 * DK:P], wqkT).then_inc(s_w[WQK], 16)
            sp_.dma_start(w_raw[WIG][:, :, :], wigT).then_inc(s_w[WIG], 16)
            sp_.dma_start(w_raw[WOG][:, :, :], wogT).then_inc(s_w[WOG], 16)
            sp_.dma_start(w_raw[WO][:, :, :], woT).then_inc(s_w[WO], 16)
            sp_.dma_start(nw[:, :], norm_w).then_inc(s_nw, 16)
            with sp_.Fori(0, NB) as b:
                for h in range(2):
                    n = 2 * b + h
                    sp_.wait_ge(s_r, TB * n)
                    sp_.dma_start(xs[1 - h][:, :, :], x2[ds((n + 1) % NBLK * TB, TB), :, :].rearrange("t p c -> p t c")).then_inc(s_x[1 - h], 16)
                    sp_.wait_ge(s_out, TB * n + TB)
                    sp_.dma_start(x3[ds(TB * n, TB), :, :].rearrange("t p c -> p t c"), r[:, :, :]).then_inc(s_sto, 16)
            sp_.wait_ge(s_sto, 16 * NBLK)
            sp_.wait_ge(s_x[0], 16 * (NB + 1))

        @block.scalar
        def _(act):
            for i in range(NW):
                act.wait_ge(s_w[i], 32 if i == WQK else 16)
                if i == WO:
                    act.wait_ge(s_fold, KC)
                act.activation(w_hi[i][:, :, :], w_raw[i][:, :, :], ACT.Copy).then_inc(s_wh, 1)
            with act.Fori(0, NB) as b:
                for h in range(2):
                    n = 2 * b + h
                    for c in range(KC):
                        act.wait_ge(s_tp, KC * n + c + 1)
                        act.activation(xt_hi[:, c, :], ps[:, GO + c, :], ACT.Copy).then_inc(s_xth, 1)
                    act.wait_ge(s_qk, n + 1)
                    act.activation(qk_f[:, :], ps[:, F, :], ACT.Copy).then_inc(s_qkf, 1)
                    tok = ps[:, A, :].rearrange("p (t f) -> p t f", t=TB)
                    act.wait_ge(s_qx, n + 1)
                    act.activation(kx[:, :, :], tok[:, :, DK:2 * DK], ACT.Exp, scale=-1.0).then_inc(s_ke, 1)
                    act.activation(qx[:, :, :], qx[:, :, :], ACT.Exp).then_inc(s_qe, 1)
                    act.wait_ge(s_ks, n + 1)
                    act.activation(kx[:, :, :], ks[:, :, :], ACT.Exp).then_inc(s_k2, 1)
                    act.wait_ge(s_k2, n + 1)
                    act.activation(sp[:, :, :], kx[:, :, :], ACT.Ln, bias=1.0).then_inc(s_sp, 1)
                    act.wait_ge(s_sum, n + 1)
                    sums = ps[:, F, :].rearrange("p (a t d) -> p a t d", a=4, t=TB)
                    act.wait_ge(s_ft, 5 * n)
                    act.activation(decay[:, :, :, :].rearrange("p a t d -> p (a t d)"), ps[:, F, :], ACT.Exp, scale=-1.0).then_inc(s_dec, 1)
                    act.activation(grow[:, :, :].rearrange("p t d -> p (t d)"), ps[:, F, 0:P], ACT.Exp).then_inc(s_dec, 1)
                    act.wait_ge(s_s, 2 * TB * b + TB * h + b + 1)
                    act.activation(dec[:, :], ps[0:DK, A, D_COL:D_COL + TB], ACT.Exp, scale=-1.0).then_inc(s_dexp, 1)
                    for t in range(TB):
                        i = TB * n + t
                        act.wait_ge(s_ftt, i + 1)
                        act.activation(ft[t % 2][:, :, :].rearrange("d a n -> d (a n)"), ps[0:DK, F, :], ACT.Copy).then_inc(s_fts, 1)
                        act.wait_ge(s_o, i + 1)
                        o = ps[:, O, :].rearrange("p (m n) -> p m n", m=KC)
                        o_t = o_f[:, :, t * P:(t + 1) * P]
                        act.activation(o_t, o, ACT.Copy).then_inc(s_of, 1)
                        act.wait_ge(s_of, i + 1)
                        act.wait_ge(s_ss, i)
                        act.activation(sq[:, :, :], o_t, ACT.Square).then_inc(s_sq, 1)
                        act.activation(o_hi[:, :, t * P:(t + 1) * P], o_t, ACT.Copy).then_inc(s_oh, 1)
                    for m in range(KC):
                        act.wait_ge(s_go, KC * n + m + 1)
                        act.wait_ge(s_pl, KC * n + max(0, m - 1))
                        act.activation(sg[m % 2][:, :], ps[:, GO + m, :], ACT.Silu).then_inc(s_sg, 1)
                        act.wait_ge(s_p, KC * n + m + 1)
                        act.activation(p_hi[:, m, :], sg[m % 2][:, :], ACT.Copy).then_inc(s_ph, 1)

        @block.vector
        def _(dve):
            steps = Steps(dve, s_dve, 2 * 5)
            dve.wait_ge(s_nw, 16)
            dve.wait_ge(s_w[WO], 16)
            for c in range(KC):
                dve.tensor_scalar(w_raw[WO][:, c, :], w_raw[WO][:, c, :], nw[:, c:c + 1], None, ALU.mult).then_inc(s_fold, 1)
            dve.wait_ge(s_fold, KC)
            for i in range(NW):
                dve.wait_ge(s_wh, i + 1)
                dve.tensor_tensor(w_lo[i][:, :, :], w_raw[i][:, :, :], w_hi[i][:, :, :].bitcast(F32), ALU.subtract).then_inc(s_wl, 1)
            with dve.Fori(0, NB) as b:
                steps.turn(b)
                dve.wait_ge(s_o, 2 * TB * b)
                dve.memset(state[:, :], 0.0).then_inc(s_s, 1)
                for h in range(2):
                    n = 2 * b + h
                    for c in range(KC):
                        dve.wait_ge(s_xth, KC * n + c + 1)
                        dve.tensor_tensor(xt_lo[:, c, :], ps[:, GO + c, :], xt_hi[:, c, :].bitcast(F32), ALU.subtract).then_inc(s_xtl, 1)
                    dve.wait_ge(s_tok, n + 1)
                    tok = ps[:, A, :].rearrange("p (t f) -> p t f", t=TB)
                    steps.done(dve.tensor_reduce(q_max[:, :], tok[:, :, 0:DK], AX.X, ALU.max))
                    dve.tensor_tensor(qx[:, :, :], tok[:, :, 0:DK], q_max[:, :].unsqueeze(2).to_broadcast([P, TB, DK]),
                                      ALU.subtract).then_inc(s_qx, 1)
                    dve.wait_ge(s_ke, n + 1)
                    steps.done(dve.tensor_scalar(kx[:, :, :], kx[:, :, :], 1.0, None, ALU.add))
                    dve.reciprocal(ks[:, :, :], kx[:, :, :]).then_inc(s_ks, 1)
                    dve.wait_ge(s_qe, n + 1)
                    steps.done(dve.tensor_reduce(q_sum[:, :], qx[:, :, :], AX.X, ALU.add))
                    steps.done(dve.reciprocal(q_inv[:, :], q_sum[:, :]))
                    steps.done(dve.tensor_tensor(qs[:, :, :], qx[:, :, :], q_inv[:, :].unsqueeze(2).to_broadcast([P, TB, DK]), ALU.mult))
                    dve.wait_ge(s_dec, 2 * n + 2)
                    dve.wait_ge(s_su, TB * n)
                    dve.wait_ge(s_ks, n + 1)
                    dve.tensor_tensor(feats[:, QH, :, :], qs[:, :, :], decay[:, 0, :, :], ALU.mult).then_inc(s_ft, 1)
                    dve.tensor_tensor(feats[:, KA, :, :], ks[:, :, :], grow[:, :, :], ALU.mult).then_inc(s_ft, 1)
                    dve.tensor_tensor(feats[:, KB, :, :], ks[:, :, :], decay[:, 1, :, :], ALU.mult).then_inc(s_ft, 1)
                    dve.tensor_tensor(feats[:, QT, :, :], qs[:, :, :], decay[:, 2, :, :], ALU.mult).then_inc(s_ft, 1)
                    dve.tensor_tensor(k_end[:, :, :], ks[:, :, :], decay[:, 3, :, :], ALU.mult).then_inc(s_ft, 1)
                    for t in range(TB):
                        i = TB * n + t
                        dve.wait_ge(s_a, i + 1)
                        dve.tensor_tensor(at[t % 2][:, :], ps[:, A, 0:P], const.upto[:, :], ALU.mult).then_inc(s_at, 1)
                        dve.wait_ge(s_dexp, n + 1)
                        dve.wait_ge(s_su, i + 1)
                        dve.wait_ge(s_o, i + 1)
                        dve.scalar_tensor_tensor(out=state[:, :], in0=state[:, :], scalar=dec[:, t:t + 1],
                                                 in1=ps[0:DK, S, :], op0=ALU.mult, op1=ALU.add).then_inc(s_s, 1)
                        dve.wait_ge(s_oh, i + 1)
                        dve.tensor_tensor(o_lo[:, :, t * P:(t + 1) * P], o_f[:, :, t * P:(t + 1) * P],
                                          o_hi[:, :, t * P:(t + 1) * P].bitcast(F32), ALU.subtract).then_inc(s_ol, 1)
                    dve.wait_ge(s_ss, TB * n + TB)
                    dve.tensor_scalar(ms[:, :], ps[:, A, SS_COL:SS_COL + TB], 1.0 / C, GLA_EPS, ALU.mult, ALU.add).then_inc(s_ms, 1)
                    for m in range(KC):
                        dve.wait_ge(s_sg, KC * n + m + 1)
                        dve.tensor_tensor(sg[m % 2][:, :], sg[m % 2][:, :], o_f[:, m, :], ALU.mult).then_inc(s_p, 1)
                    dve.wait_ge(s_rms, n + 1)
                    dve.wait_ge(s_sto, 16 * n)
                    for t in range(TB):
                        dve.wait_ge(s_y, TB * n + t + 1)
                        dve.scalar_tensor_tensor(out=r[:, t, :], in0=ps[:, t, :], scalar=rms[:, t:t + 1], in1=xs[h][:, t, :],
                                                 op0=ALU.mult, op1=ALU.add).then_inc(s_r, 1)
                    layer_norm_block(dve, n, r, st, mv, var, rstd, filler, s_r, s_st, s_ag, s_var, s_rstd, s_out)
                steps.end()

        @block.gpsimd
        def _(pool):
            with pool.Fori(0, NB) as b:
                for h in range(2):
                    n = 2 * b + h
                    pool.wait_ge(s_ms, n + 1)
                    pool.tensor_tensor(rms[:, :], ms[:, :], const.minus_half[:, :], ALU.pow).then_inc(s_rms, 1)
                    for m in range(KC):
                        pool.wait_ge(s_ph, KC * n + m + 1)
                        pool.tensor_tensor(p_lo[:, m, :], sg[m % 2][:, :], p_hi[:, m, :].bitcast(F32), ALU.subtract).then_inc(s_pl, 1)
                    pool.wait_ge(s_var, n + 1)
                    pool.tensor_tensor(rstd[:, :], var[:, :], const.minus_half[:, :], ALU.pow).then_inc(s_rstd, 1)

        @block.tensor
        def _(pe):
            with pe.Fori(0, NB) as b:
                for h in range(2):
                    n = 2 * b + h
                    x_in = xs[h]

                    def gate(m, half, last):
                        w, hi, lo = ((WIG, xt_hi, xt_lo), (WOG, o_hi, o_lo))[half]
                        for c in range(KC):
                            ins = three_products(pe, ps[:, GO + m, :], w_hi[w][:, c, m * P:(m + 1) * P], w_lo[w][:, c, m * P:(m + 1) * P],
                                                 hi[:, c, :], lo[:, c, :], half == 0 and c == 0, last and c == KC - 1)
                        return ins

                    pe.wait_ge(s_x[h], 16 * (b + 1))
                    pe.wait_ge(s_sg, KC * n)
                    for c in range(KC):
                        for t in range(TB):
                            ins = pe.transpose(ps[:, GO + c, t * P:(t + 1) * P], x_in[:, t, c * P:(c + 1) * P], const.ident[:, :])
                        ins.then_inc(s_tp, 1)
                    pe.wait_ge(s_xtl, KC * n + KC)
                    pe.wait_ge(s_r, TB * n)
                    pe.wait_ge(s_wl, 1)
                    for c in range(KC):
                        ins = three_products(pe, ps[:, F, :], w_hi[WQK][:, c, :], w_lo[WQK][:, c, :], xt_hi[:, c, :], xt_lo[:, c, :],
                                             c == 0, c == KC - 1)
                    ins.then_inc(s_qk, 1)
                    pe.wait_ge(s_wl, 2)
                    gate(0, 0, False)
                    pe.wait_ge(s_qkf, n + 1)
                    pe.wait_ge(s_ms, n)
                    for t in range(TB):
                        ins = pe.transpose(ps[:, A, t * P:(t + 1) * P], qk_f[:, t * P:(t + 1) * P], const.ident[:, :])
                    ins.then_inc(s_tok, 1)
                    gate(1, 0, False)
                    pe.wait_ge(s_sp, n + 1)
                    for a, m in enumerate((const.within, const.to_half, const.upto, const.before)):
                        ins = pe.matmul(ps[:, F, a * P:(a + 1) * P], m[:, :], sp[:, :, :].rearrange("p t d -> p (t d)"), start=True, stop=True)
                    for t in range(TB):
                        ins = pe.matmul(ps[0:DK, A, D_COL + t:D_COL + t + 1], sp[:, t, :], const.ones[:, 0:1], start=True, stop=True)
                    ins.then_inc(s_sum, 1)
                    gate(2, 0, False)
                    for t in range(TB):
                        i = TB * n + t
                        pe.wait_ge(s_ft, 5 * n + 5)
                        pe.wait_ge(s_dec, 2 * n + 2)
                        pe.wait_ge(s_fts, i)
                        for a in range(4):
                            ins = pe.transpose(ps[0:DK, F, a * P:(a + 1) * P], feats[:, a, t, :], const.ident[:, :])
                        ins.then_inc(s_ftt, 1)
                        pe.wait_ge(s_s, i + b + 1)
                        pe.wait_ge(s_at, i)
                        pe.matmul(ps[0:DK, S, :], k_end[:, t, :], x_in[:, t, :], start=True, stop=True).then_inc(s_su, 1)
                        if t == 0:
                            gate(3, 0, False)
                        pe.wait_ge(s_dexp, n + 1)
                        pe.wait_ge(s_fts, i + 1)
                        f = ft[t % 2]
                        pe.matmul(ps[:, A, 0:HALF], f[:, KA, :], f[:, QH, 0:HALF], start=True, stop=True)
                        pe.matmul(ps[:, A, HALF:P], f[:, KB, :], f[:, QH, HALF:P], start=True, stop=True).then_inc(s_a, 1)
                        pe.wait_ge(s_at, i + 1)
                        pe.wait_ge(s_of, i)
                        for m in range(KC):
                            o = ps[:, O, m * P:(m + 1) * P]
                            pe.matmul(o, x_in[:, t, m * P:(m + 1) * P], at[t % 2][:, :], start=True, stop=False)
                            ins = pe.matmul(o, state[:, m * P:(m + 1) * P], f[:, QT, :], start=False, stop=True)
                        ins.then_inc(s_o, 1)
                        pe.wait_ge(s_sq, i + 1)
                        for m in range(KC):
                            ins = pe.matmul(ps[:, A, SS_COL + t:SS_COL + t + 1], sq[:, m, :], const.ones[:, 0:1],
                                            start=(m == 0), stop=(m == KC - 1))
                        ins.then_inc(s_ss, 1)
                    pe.wait_ge(s_ol, TB * n + TB)
                    pe.wait_ge(s_wl, 3)
                    for m in range(KC):
                        gate(m, 1, True).then_inc(s_go, 1)
                    pe.wait_ge(s_ph, KC * n + KC)
                    pe.wait_ge(s_pl, KC * n + KC)
                    pe.wait_ge(s_ms, n + 1)
                    pe.wait_ge(s_of, TB * n + TB)
                    pe.wait_ge(s_s, TB * n + TB + b + 1)
                    pe.wait_ge(s_wl, 4)
                    for t in range(TB):
                        for c in range(KC):
                            ins = three_products(pe, ps[:, t, :], p_hi[:, c, t * P:(t + 1) * P], p_lo[:, c, t * P:(t + 1) * P],
                                                 w_hi[WO][:, c, :], w_lo[WO][:, c, :], c == 0, c == KC - 1)
                        ins.then_inc(s_y, 1)


D_FF = 2048
FT = D_FF // P
TOP = T // 2
NT8 = T // P
ID_COL, WEIGHT_COL, ROW = C, C + 1, C + 2


def routed_feed_forward(nc, x3, router_w, router_b, w1, b1, w2, b2, rows, out, const):
    ctx, sems = ExitStack(), []
    ctx.callback(clear_semaphores, nc, sems)
    with ctx:
        def sb(name, shape, dt=F32):
            return ctx.enter_context(nc.sbuf_tensor(name, shape, dt))

        def sem(name):
            sems.append(nc.alloc_semaphore(name))
            return sems[-1]

        NCH = 8
        w1_hi = sb("w1_hi", [P, KC, D_FF], F32R)
        w1_lo = sb("w1_lo", [P, KC, D_FF], F32R)
        w2_hi = sb("w2_hi", [P, FT, C], F32R)
        w2_lo = sb("w2_lo", [P, FT, C], F32R)
        w_raw = [sb(f"mw_raw{i}", [P, 4, 512]) for i in range(2)]
        b1_sb = sb("b1_sb", [P, FT])
        b2_sb = sb("b2_sb", [P, C])
        rw_sb = sb("rw_sb", [P, C])
        rb_sb = sb("rb_sb", [P, 1])
        token = sb("token", [P, NB * NT8], I32)
        base = sb("base", [P, NB])
        big = sb("big", [P, NT8, ROW])
        score = sb("score", [P, NT8])
        counts = sb("counts", [P, 3, NT8])
        rank = sb("rank", [P, NT8])
        row = sb("row", [P, NT8], I32)
        xt_hi = sb("mxt_hi", [P, KC, BLK], F32R)
        xt_lo = sb("mxt_lo", [P, KC, BLK], F32R)
        h = [sb(f"mh{i}", [P, BLK]) for i in range(2)]
        h_hi = [sb(f"mh_hi{i}", [P, BLK], F32R) for i in range(2)]
        h_lo = [sb(f"mh_lo{i}", [P, BLK], F32R) for i in range(2)]
        r = sb("mr", [P, TB, C])
        scores = r[:, 0:2, :].rearrange("p a n -> p (a n)")
        work = r[:, 2:4, :].rearrange("p a (b n) -> p (a b) n", n=P)
        where = sb("where", [P, TB], I32)
        st = sb("mst", [P, TB, 6])
        mv = sb("mmv", [P, TB, 2])
        var = sb("mvar", [P, TB])
        rstd = sb("mrstd", [P, TB])
        filler = sb("mfiller", [P, 1])
        pool_filler = sb("pool_filler", [P, 1])

        ps = ctx.enter_context(nc.psum_tensor("ps_moe", [P, 8, 512], F32))
        Y, H = 0, 4

        s_c = sem("m_small_loaded")
        s_w = [sem(f"mw_loaded{i}") for i in range(2)]
        s_wh = sem("mw_hi_done")
        s_wl = sem("mw_lo_done")
        s_id = sem("ids_ready")
        s_x = sem("mx_loaded")
        s_dot = sem("score_dot_done")
        s_sc = sem("score_ready")
        s_sig = sem("weight_ready")
        s_tok = sem("token_index_set")
        s_diag = sem("score_diagonals_ready")
        s_bc = sem("scores_broadcast")
        s_sb = sem("scores_taken")
        s_cnt = sem("counted")
        s_rk = sem("rank_ready")
        s_row = sem("row_ready")
        s_scat = sem("rows_scattered")
        s_r = sem("mresidual_added")
        s_st = sem("mstats_done")
        s_ag = sem("maggregated")
        s_var = sem("mvar_ready")
        s_rstd = sem("mrstd_ready")
        s_out = sem("mx_out_ready")
        s_all = sem("plain_rows_stored")
        s_sel = sem("selected_loaded")
        s_tp = sem("mx_transposed")
        s_xth = sem("mxt_hi_done")
        s_xtl = sem("mxt_lo_done")
        s_h1 = sem("mh_projected")
        s_g = sem("gelu_done")
        s_hh = sem("mh_hi_done")
        s_hl = sem("mh_lo_done")
        s_y = sem("my_added")
        s_b2 = sem("b2_weighted")
        s_wr = sem("where_ready")
        s_fin = sem("selected_stored")
        s_dve = sem("dve_step_moe")

        block = ctx.enter_context(nc.Block())

        @block.sync
        def _(sp):
            sp.dma_start(big[:, :, 0:C], x3[0:NT8, :, :].rearrange("t p c -> p t c")).then_inc(s_x, 16)
            sp.dma_start(rw_sb[:, :], router_w.to_broadcast([P, C])).then_inc(s_c, 16)
            sp.dma_start(rb_sb[:, :], router_b.to_broadcast([P, 1])).then_inc(s_c, 16)
            sp.dma_start(b2_sb[:, :], b2.to_broadcast([P, C])).then_inc(s_c, 16)
            sp.dma_start(b1_sb[:, :], b1).then_inc(s_c, 16)

            def load_weights(n):
                src = w1[:, :, n * 512:(n + 1) * 512] if n < 4 else w2[:, (n - 4) * 4:(n - 3) * 4, :]
                sp.dma_start(w_raw[n % 2][:, :, :], src).then_inc(s_w[n % 2], 16)

            for n in range(2):
                load_weights(n)
            with sp.Fori(0, NB) as b:
                for g in range(2):
                    sp.wait_ge(s_out, 2 * TB * b + TB * g + TB)
                    sp.dma_start(out[ds(2 * TB * b + TB * g, TB), :, :].rearrange("t p c -> p t c"), r[:, :, :]).then_inc(s_all, 16)
                sp.wait_ge(s_scat, 16 * NT8 * (b + 1))
                sp.dma_start(big[:, :, 0:C], x3[ds((b + 1) % NB * NT8, NT8), :, :].rearrange("t p c -> p t c")).then_inc(s_x, 16)
            for n in range(2, NCH):
                sp.wait_ge(s_wl, n - 1)
                load_weights(n)
            sp.wait_ge(s_x, 16 * (NB + 1))
            sp.wait_ge(s_all, 16 * 2 * NB)
            sp.wait_ge(s_scat, 16 * NT8 * NB)
            with sp.Fori(0, NB) as b:
                sp.wait_ge(s_r, TB * (2 * NB + b))
                sp.wait_ge(s_wr, b)
                sp.dma_start(big[:, 0:TB, :], rows[ds(NT8 * b, TB), :, :].rearrange("t p c -> p t c")).then_inc(s_sel, 16)

        @block.scalar
        def _(act):
            with act.Fori(0, NB) as b:
                act.wait_ge(s_sc, b + 1)
                act.activation(big[:, :, WEIGHT_COL], score[:, :], ACT.Sigmoid).then_inc(s_sig, 1)
                act.wait_ge(s_bc, b + 1)
                act.wait_ge(s_all, 16 * 2 * b)
                act.activation(r[:, 0:2, :], ps[:, H:H + 2, :], ACT.Copy).then_inc(s_sb, 1)
            for n in range(NCH):
                hi = w1_hi[:, :, n * 512:(n + 1) * 512] if n < 4 else w2_hi[:, (n - 4) * 4:(n - 3) * 4, :]
                act.wait_ge(s_w[n % 2], 16 * (n // 2 + 1))
                act.activation(hi, w_raw[n % 2][:, :, :], ACT.Copy).then_inc(s_wh, 1)
            with act.Fori(0, NB) as b:
                for c in range(KC):
                    act.wait_ge(s_tp, KC * b + c + 1)
                    act.activation(xt_hi[:, c, :], ps[:, H + c, :], ACT.Copy).then_inc(s_xth, 1)
                for j in range(FT):
                    act.wait_ge(s_h1, FT * b + j + 1)
                    act.wait_ge(s_hl, FT * b + max(0, j - 1))
                    act.activation(h[j % 2][:, :], ps[:, H + j % 4, :], ACT.Gelu_apprx_tanh, bias=b1_sb[:, j:j + 1]).then_inc(s_g, 1)
                    act.wait_ge(s_g, FT * b + j + 1)
                    act.wait_ge(s_y, FT * b + max(0, j - 1))
                    act.activation(h_hi[j % 2][:, :], h[j % 2][:, :], ACT.Copy).then_inc(s_hh, 1)

        @block.vector
        def _(dve):
            steps = Steps(dve, s_dve, 2)
            dve.wait_ge(s_c, 64)
            dve.wait_ge(s_id, 2)
            with dve.Fori(0, NB) as b:
                steps.turn(b)
                dve.wait_ge(s_x, 16 * (b + 1))
                dve.wait_ge(s_all, 16 * 2 * b)
                for t in range(NT8):
                    ins = dve.tensor_tensor_reduce(out=work[:, 0:4, :].rearrange("p a n -> p (a n)"), in0=big[:, t, 0:C], in1=rw_sb[:, :],
                                                   scale=1.0, scalar=0.0, op0=ALU.mult, op1=ALU.add, accum_out=score[:, t:t + 1])
                    ins.then_inc(s_dot, 1)
                    dve.wait_ge(s_dot, NT8 * b + t + 1)
                dve.tensor_scalar(score[:, :], score[:, :], rb_sb[:, 0:1], None, ALU.add).then_inc(s_sc, 1)
                dve.tensor_copy(big[:, :, ID_COL].bitcast(I32), token[:, ds(b * NT8, NT8)]).then_inc(s_tok, 1)
                dve.wait_ge(s_sc, b + 1)
                dve.tensor_tensor(work[:, :, :], const.ident[:, :].unsqueeze(1).to_broadcast([P, NT8, P]),
                                  score[:, :].unsqueeze(2).to_broadcast([P, NT8, P]), ALU.mult).then_inc(s_diag, 1)
                dve.wait_ge(s_sb, b + 1)
                junk = work[:, :, :].rearrange("p a n -> p (a n)")
                k = 0
                for t in range(NT8):
                    s_t = score[:, t:t + 1]
                    todo = [(0, t * P, ALU.is_ge), (t * P, T, ALU.is_gt)] if t else [(0, T, ALU.is_gt)]
                    for a, (lo, hi, op) in enumerate(todo):
                        dve.tensor_scalar(junk[:, 0:hi - lo], scores[:, lo:hi], s_t, None, op, ALU.add,
                                          accum_out=counts[:, 1 - a if t else 0, t:t + 1]).then_inc(s_cnt, 1)
                        k += 1
                        dve.wait_ge(s_cnt, (3 * NT8 - 1) * b + k)
                    dve.scalar_tensor_tensor(out=junk[:, 0:P], in0=scores[:, t * P:(t + 1) * P], scalar=s_t, in1=const.before[:, :],
                                             op0=ALU.is_equal, op1=ALU.mult, accum_out=counts[:, 2, t:t + 1]).then_inc(s_cnt, 1)
                    k += 1
                    dve.wait_ge(s_cnt, (3 * NT8 - 1) * b + k)
                steps.done(dve.tensor_tensor(rank[:, :], counts[:, 0, :], counts[:, 2, :], ALU.add))
                steps.done(dve.tensor_tensor(rank[:, 1:NT8], rank[:, 1:NT8], counts[:, 1, 1:NT8], ALU.add))
                dve.wait_ge(s_scat, 16 * NT8 * b)
                dve.tensor_tensor(row[:, :], rank[:, :], base[:, ds(b, 1)].to_broadcast([P, NT8]), ALU.add).then_inc(s_row, 1)
                for g in range(2):
                    n = 2 * b + g
                    dve.wait_ge(s_all, 16 * n)
                    for t in range(TB):
                        dve.tensor_scalar(r[:, t, :], big[:, TB * g + t, 0:C], 2.0, None, ALU.mult).then_inc(s_r, 1)
                    layer_norm_block(dve, n, r, st, mv, var, rstd, filler, s_r, s_st, s_ag, s_var, s_rstd, s_out)
            for n in range(NCH):
                hi = w1_hi[:, :, n * 512:(n + 1) * 512] if n < 4 else w2_hi[:, (n - 4) * 4:(n - 3) * 4, :]
                lo = w1_lo[:, :, n * 512:(n + 1) * 512] if n < 4 else w2_lo[:, (n - 4) * 4:(n - 3) * 4, :]
                dve.wait_ge(s_wh, n + 1)
                dve.tensor_tensor(lo, w_raw[n % 2][:, :, :], hi.bitcast(F32), ALU.subtract).then_inc(s_wl, 1)
            with dve.Fori(0, NB) as b:
                for c in range(KC):
                    dve.wait_ge(s_xth, KC * b + c + 1)
                    dve.tensor_tensor(xt_lo[:, c, :], ps[:, H + c, :], xt_hi[:, c, :].bitcast(F32), ALU.subtract).then_inc(s_xtl, 1)
                dve.wait_ge(s_fin, 16 * TB * b)
                dve.wait_ge(s_all, 16 * 2 * NB)
                dve.tensor_copy(where[:, :], big[:, 0:TB, ID_COL].bitcast(I32)).then_inc(s_wr, 1)
                for t in range(TB):
                    weight = big[:, t, WEIGHT_COL:WEIGHT_COL + 1]
                    dve.tensor_scalar(r[:, t, :], b2_sb[:, :], weight, None, ALU.mult).then_inc(s_b2, 1)
                for t in range(TB):
                    dve.wait_ge(s_b2, 2 * TB * b + t + 1)
                    dve.scalar_tensor_tensor(out=r[:, t, :], in0=big[:, t, 0:C], scalar=2.0, in1=r[:, t, :], op0=ALU.mult,
                                             op1=ALU.add).then_inc(s_b2, 1)
                for t in range(TB):
                    weight = big[:, t, WEIGHT_COL:WEIGHT_COL + 1]
                    dve.wait_ge(s_b2, 2 * TB * b + TB + t + 1)
                    dve.wait_ge(s_y, FT * b + FT)
                    dve.scalar_tensor_tensor(out=r[:, t, :], in0=ps[:, Y + t, :], scalar=weight, in1=r[:, t, :],
                                             op0=ALU.mult, op1=ALU.add).then_inc(s_r, 1)
                layer_norm_block(dve, 2 * NB + b, r, st, mv, var, rstd, filler, s_r, s_st, s_ag, s_var, s_rstd, s_out)

        @block.gpsimd
        def _(pool):
            pool.memset(pool_filler[:, :], 1.0)
            pool.iota(token[:, :], pattern=[[P, NB * NT8]], base=0, channel_multiplier=1).then_inc(s_id, 1)
            pool.iota(base[:, :], pattern=[[T, NB]], base=0, channel_multiplier=0,
                      allow_small_or_imprecise_dtypes=True).then_inc(s_id, 1)
            with pool.Fori(0, NB) as b:
                pool.wait_ge(s_row, b + 1)
                pool.wait_ge(s_sig, b + 1)
                pool.wait_ge(s_tok, b + 1)
                settle(pool, pool_filler)
                for t in range(NT8):
                    pool.indirect_dma_start(rows_flat(rows), bass.IndirectOffsetOnAxis(ap=row[:, t:t + 1], axis=0),
                                            big[:, t, :], None).then_inc(s_scat, 16)
                for g in range(2):
                    pool.wait_ge(s_var, 2 * b + g + 1)
                    pool.tensor_tensor(rstd[:, :], var[:, :], const.minus_half[:, :], ALU.pow).then_inc(s_rstd, 1)
            pool.wait_ge(s_all, 16 * 2 * NB)
            with pool.Fori(0, NB) as b:
                for j in range(FT):
                    pool.wait_ge(s_hh, FT * b + j + 1)
                    pool.wait_ge(s_y, FT * b + max(0, j - 1))
                    pool.tensor_tensor(h_lo[j % 2][:, :], h[j % 2][:, :], h_hi[j % 2][:, :].bitcast(F32), ALU.subtract).then_inc(s_hl, 1)
                pool.wait_ge(s_var, 2 * NB + b + 1)
                pool.tensor_tensor(rstd[:, :], var[:, :], const.minus_half[:, :], ALU.pow).then_inc(s_rstd, 1)
                pool.wait_ge(s_wr, b + 1)
                pool.wait_ge(s_out, TB * (2 * NB + b) + TB)
                settle(pool, pool_filler)
                for t in range(TB):
                    pool.indirect_dma_start(rows_flat(out), bass.IndirectOffsetOnAxis(ap=where[:, t:t + 1], axis=0),
                                            r[:, t, :], None).then_inc(s_fin, 16)
            pool.wait_ge(s_fin, 16 * TB * NB)

        @block.tensor
        def _(pe):
            with pe.Fori(0, NB) as b:
                pe.wait_ge(s_diag, b + 1)
                pe.wait_ge(s_sb, b)
                for a in range(2):
                    ins = pe.matmul(ps[:, H + a, :], const.ones[:, :], work[:, 4 * a:4 * a + 4, :].rearrange("p a n -> p (a n)"), start=True, stop=True)
                ins.then_inc(s_bc, 1)
            pe.wait_ge(s_sb, NB)
            with pe.Fori(0, NB) as b:
                def up(j):
                    if j < 4:
                        pe.wait_ge(s_xtl, KC * b + KC)
                    pe.wait_ge(s_g, FT * b + max(0, j - 3))
                    pe.wait_ge(s_wl, j // 4 + 1)
                    for c in range(KC):
                        ins = three_products(pe, ps[:, H + j % 4, :], w1_hi[:, c, j * P:(j + 1) * P], w1_lo[:, c, j * P:(j + 1) * P],
                                             xt_hi[:, c, :], xt_lo[:, c, :], c == 0, c == KC - 1)
                    ins.then_inc(s_h1, 1)

                def down(j):
                    pe.wait_ge(s_hh, FT * b + j + 1)
                    pe.wait_ge(s_hl, FT * b + j + 1)
                    pe.wait_ge(s_wl, 4 + j // 4 + 1)
                    if j == 0:
                        pe.wait_ge(s_r, TB * (2 * NB + b))
                    for t in range(TB):
                        ins = three_products(pe, ps[:, Y + t, :], h_hi[j % 2][:, t * P:(t + 1) * P], h_lo[j % 2][:, t * P:(t + 1) * P],
                                             w2_hi[:, j, :], w2_lo[:, j, :], j == 0, j == FT - 1)
                    ins.then_inc(s_y, 1)

                pe.wait_ge(s_sel, 16 * (b + 1))
                pe.wait_ge(s_g, FT * b)
                for c in range(KC):
                    for t in range(TB):
                        ins = pe.transpose(ps[:, H + c, t * P:(t + 1) * P], big[:, t, c * P:(c + 1) * P], const.ident[:, :])
                    ins.then_inc(s_tp, 1)
                up(0)
                for j in range(1, FT):
                    up(j)
                    down(j - 1)
                down(FT - 1)


def rows_flat(a):
    return a.rearrange("n p c -> (n p) c")


def settle(pool, filler):
    pool.tensor_tensor(filler[:, :], filler[:, :], filler[:, :], ALU.mult)


def transformer_two_layers(nc, x, xT, wqT, wkT, wvT, woT, gu_packed, gu_scales, dn_packed, dn_scales,
                           wqkT, wogT, wigT, wo1T, norm_w, router_w, router_b, w1, b1, w2, b2, out):
    def tiles(a):
        return a.rearrange("(n p) c -> n p c", p=P)

    def contracted(a):
        return a.rearrange("(k p) n -> p k n", p=P)

    x1, x2, x3 = (tiles(nc.dram_tensor(name, [NB * T, C], F32).ap()) for name in ("x1", "x2", "x3"))
    rows = tiles(nc.dram_tensor("routed_rows", [NB * T, ROW], F32).ap())
    with ExitStack() as ctx:
        const = Constants(nc, ctx)
        linear_attention(nc, tiles(x), contracted(xT), [contracted(wkT), contracted(wvT), contracted(wqT)],
                         contracted(woT), x1, const)
        fp4_feed_forward(nc, x1, gu_packed.rearrange("(k w) o -> w k o", w=P // NIB), gu_scales, dn_packed, dn_scales,
                         x2, const)
        gated_linear_attention(nc, x2, contracted(wqkT), contracted(wogT), contracted(wigT), contracted(wo1T), norm_w,
                               x3, const)
        routed_feed_forward(nc, x3, router_w, router_b, contracted(w1), b1, contracted(w2), b2, rows, tiles(out), const)


def kernel(**inputs):
    import numpy as np
    import concourse.bacc as bacc
    from concourse.bass_utils import run_bass_kernel_spmd

    a = {name: np.asarray(value) for name, value in inputs.items()}
    x = a["L0_attn_x"].reshape(NB * T, C)
    laid_out = {
        "x": x,
        "xT": x.T,
        "wqT": a["L0_attn_Wq"].T,
        "wkT": a["L0_attn_Wk"].T,
        "wvT": a["L0_attn_Wv"].T,
        "woT": a["L0_attn_Wo"].T,
        "gate_up_packed": a["L0_ffn_gate_up_packed"].T,
        "gate_up_scales": a["L0_ffn_gate_up_scales"],
        "down_packed": a["L0_ffn_down_packed"].T,
        "down_scales": a["L0_ffn_down_scales"],
        "gla_wqkT": np.concatenate([a["L1_attn_Wq"], a["L1_attn_Wk"]]).T,
        "gla_wogT": a["L1_attn_Wog"].T,
        "gla_wigT": a["L1_attn_Wig"].T,
        "gla_woT": a["L1_attn_Wo"].T,
        "gla_norm_w": a["L1_attn_g_norm_w"].reshape(KC, P).T,
        "router_w": a["L1_ffn_router_weight"].reshape(1, C),
        "router_b": a["L1_ffn_router_bias"].reshape(1, 1),
        "w1": a["L1_ffn_w1"],
        "b1": a["L1_ffn_b1"].reshape(FT, P).T,
        "w2": a["L1_ffn_w2"],
        "b2": a["L1_ffn_b2"].reshape(1, C),
    }
    nc = bacc.Bacc("TRN2", target_bir_lowering=False, num_devices=1)
    arrays, args = {}, []
    for name, value in laid_out.items():
        arrays[f"in_{name}"] = np.ascontiguousarray(value)
        args.append(nc.dram_tensor(f"in_{name}", value.shape, mybir.dt.from_np(value.dtype), kind="ExternalInput").ap())
    args.append(nc.dram_tensor("out", (NB * T, C), F32, kind="ExternalOutput").ap())
    transformer_two_layers(nc, *args)
    result = run_bass_kernel_spmd(nc, [arrays], core_ids=[0])
    return result.results[0]["out"].reshape(NB, T, C)
```

```python
from contextlib import ExitStack

import concourse.bass as bass
from concourse import mybir

F32 = mybir.dt.float32
F32R = mybir.dt.float32r
F16 = mybir.dt.float16
BF16 = mybir.dt.bfloat16
I32 = mybir.dt.int32
U16 = mybir.dt.uint16
ALU = mybir.AluOpType
ACT = mybir.ActivationFunctionType
AX = mybir.AxisListType
ds = bass.ds

P = 128
NB = 2
T = 1024
C = 512
KC = C // P
BLK = 512
TB = BLK // P
NBLK = NB * T // BLK
HEADS = 16
DH = C // HEADS
HG = P // DH
LN_EPS = 1e-5
START = 1


class Steps:

    def __init__(self, engine, sem, per_turn):
        self.engine, self.sem, self.per_turn = engine, sem, per_turn

    def turn(self, it):
        self.base, self.k = it * self.per_turn, 0

    def done(self, ins):
        ins.then_inc(self.sem, 1)
        self.k += 1
        self.engine.wait_ge(self.sem, START + self.base + self.k)

    def end(self):
        assert self.k == self.per_turn, (self.k, self.per_turn)


def three_products(pe, out, lh, ll, rh, rl, first, last):
    pe.matmul(out, lh, rh, start=first, stop=False)
    pe.matmul(out, ll, rh, start=False, stop=False)
    return pe.matmul(out, lh, rl, start=False, stop=last)


def layer_norm_block(dve, n, r, st, mv, var, rstd, filler, s_r, s_st, s_ag, s_var, s_rstd, s_out):
    for t in range(TB):
        dve.wait_ge(s_r, START + TB * n + t + 1)
        dve.bn_stats(st[:, t, :], r[:, t, :]).then_inc(s_st, 1)
    dve.wait_ge(s_st, START + TB * n + TB)
    dve.memset(filler[:, :], 0.0)
    for t in range(TB):
        dve.bn_aggr(mv[:, t, :], st[:, t, :]).then_inc(s_ag, 1)
    dve.wait_ge(s_ag, START + TB * n + TB)
    dve.tensor_scalar(var[:, :], mv[:, :, 1], LN_EPS, None, ALU.add).then_inc(s_var, 1)
    dve.wait_ge(s_rstd, START + n + 1)
    for t in range(TB):
        dve.tensor_scalar(r[:, t, :], r[:, t, :], mv[:, t, 0:1], rstd[:, t:t + 1], ALU.subtract,
                          ALU.mult).then_inc(s_out, 1)


def start_semaphores(nc, sems):
    for sem in sems:
        nc.gpsimd.nop().then_inc(sem, START)
    nc.all_engine_barrier()


def clear_semaphores(nc, sems):
    nc.clear_and_free_semaphores(sems)
    nc.all_engine_barrier()


class Constants:

    def __init__(self, nc, ctx):
        def sb(name, shape, dt=F32):
            return ctx.enter_context(nc.sbuf_tensor(name, shape, dt))

        self.ident = sb("ident", [P, P])
        self.ones = sb("ones", [P, P])
        self.before = sb("before", [P, P])
        self.head_mask = sb("head_mask", [P, P])
        self.upto = sb("upto", [P, P])
        self.within = sb("within", [P, P])
        self.to_half = sb("to_half", [P, P])
        self.minus_half = sb("minus_half", [P, TB])
        s_set = ctx.enter_context(nc.semaphore("const_set"))
        s_mat = ctx.enter_context(nc.semaphore("const_matrices"))
        s_done = ctx.enter_context(nc.semaphore("const_done"))
        with nc.Block() as block:
            @block.gpsimd
            def _(pool):
                pool.memset(self.minus_half[:, :], -0.5)
                pool.memset(self.ones[:, :], 1.0)
                pool.memset(self.head_mask[:, :], 1.0).then_inc(s_set, 1)
                pool.wait_ge(s_set, 1)
                pool.affine_select(out=self.ident[:, :], in_=self.ones[:, :], compare_op=ALU.is_equal, fill=0.0,
                                   base=0, pattern=[[-1, P]], channel_multiplier=1)
                pool.affine_select(out=self.before[:, :], in_=self.ones[:, :], compare_op=ALU.is_gt, fill=0.0,
                                   base=0, pattern=[[-1, P]], channel_multiplier=1)
                for m in (self.upto, self.within):
                    pool.affine_select(out=m[:, :], in_=self.ones[:, :], compare_op=ALU.is_ge, fill=0.0,
                                       base=0, pattern=[[1, P]], channel_multiplier=-1)
                pool.memset(self.to_half[:, :], 0.0).then_inc(s_mat, 1)
                pool.wait_ge(s_mat, 1)
                h = P // 2
                pool.memset(self.within[0:h, h:P], 0.0).then_inc(s_mat, 1)
                pool.wait_ge(s_mat, 2)
                pool.tensor_copy(self.to_half[0:h, 0:h], self.before[0:h, 0:h]).then_inc(s_mat, 1)
                pool.wait_ge(s_mat, 3)
                pool.tensor_scalar(self.to_half[h:P, h:P], self.upto[h:P, h:P], -1.0, None, ALU.mult).then_inc(s_mat, 1)
                pool.wait_ge(s_mat, 4)
                v = self.head_mask[:, :].rearrange("p (h e) -> p h e", e=DH)
                pool.affine_select(out=v, in_=v, compare_op=ALU.is_ge, fill=0.0, base=0,
                                   pattern=[[-DH, HG], [0, DH]], channel_multiplier=1).then_inc(s_set, 1)
                pool.wait_ge(s_set, 2)
                pool.affine_select(out=v, in_=v, compare_op=ALU.is_ge, fill=0.0, base=DH - 1,
                                   pattern=[[DH, HG], [0, DH]], channel_multiplier=-1).then_inc(s_done, 1)
                pool.wait_ge(s_done, 1)




def linear_attention(nc, x, xT, wT, woT, x1, const):
    ctx, sems = ExitStack(), []
    ctx.callback(clear_semaphores, nc, sems)
    with ctx:
        def sb(name, shape, dt=F32):
            return ctx.enter_context(nc.sbuf_tensor(name, shape, dt))

        def sem(name):
            sems.append(nc.alloc_semaphore(name))
            return sems[-1]

        NW = 4
        NT = T // P
        w_raw = [sb(f"w_raw{i}", [P, KC, C]) for i in range(NW)]
        w_hi = [sb(f"w_hi{i}", [P, KC, C], F32R) for i in range(NW)]
        w_lo = [sb(f"w_lo{i}", [P, KC, C], F32R) for i in range(NW)]
        xt_raw = [sb(f"xt_raw{i}", [P, KC, BLK]) for i in range(2)]
        xt_hi = sb("xt_hi", [P, KC, BLK], F32R)
        xt_lo = sb("xt_lo", [P, KC, BLK], F32R)
        q = [sb(f"q{i}", [P, KC, BLK]) for i in range(2)]
        k = [sb(f"k{i}", [P, C]) for i in range(2)]
        v1 = [sb(f"v1_{i}", [P, KC, P + 1]) for i in range(2)]
        e_k = sb("e_k", [P, C])
        e_q = sb("e_q", [P, C])
        kvz = sb("kvz", [P, KC, P + HG])
        z = sb("z", [P, HEADS])
        zi = [sb(f"zi{i}", [P, HEADS]) for i in range(2)]
        att = [sb(f"att{i}", [P, C]) for i in range(2)]
        at_hi = [sb(f"at_hi{i}", [P, KC, P], F32R) for i in range(2)]
        at_lo = [sb(f"at_lo{i}", [P, KC, P], F32R) for i in range(2)]
        x_res = [sb(f"x_res{i}", [P, C]) for i in range(4)]
        r = [sb(f"r{i}", [P, C]) for i in range(3)]
        x_out = [sb(f"x_out{i}", [P, C]) for i in range(2)]
        st = [sb(f"st{i}", [P, 6]) for i in range(3)]
        mv = [sb(f"mv{i}", [P, 2]) for i in range(3)]
        filler = sb("filler", [P, 1])
        var = [sb(f"var{i}", [P, 1]) for i in range(2)]
        rstd = [sb(f"rstd{i}", [P, 1]) for i in range(2)]

        ps = ctx.enter_context(nc.psum_tensor("ps_attn", [P, 8, 512], F32))
        KV0, PROJ, QP, TP, YP = 0, 2, 6, 6, 0

        s_w = [sem(f"w_loaded{i}") for i in range(NW)]
        s_wh = sem("w_hi_done")
        s_wl = sem("w_lo_done")
        s_xt = [sem(f"xt_loaded{i}") for i in range(2)]
        s_xth = sem("xt_hi_done")
        s_xtl = sem("xt_lo_done")
        s_proj = sem("k_v_projected")
        s_ek = sem("k_exp_done")
        s_k = sem("k_ready")
        s_v = sem("v_ready")
        s_ones = sem("ones_ready")
        s_kvt = sem("kv_tile_added")
        s_q = sem("q_projected")
        s_eq = sem("q_exp_done")
        s_qr = sem("q_ready")
        s_kv = sem("kv_masked")
        s_num = sem("num_done")
        s_att = sem("att_ready")
        s_tp = sem("att_transposed")
        s_ath = sem("att_hi_done")
        s_atl = sem("att_lo_done")
        s_y = sem("out_projected")
        s_xr = [sem(f"x_res_loaded{i}") for i in range(4)]
        s_r = sem("residual_added")
        s_var = sem("var_ready")
        s_rstd = sem("rstd_ready")
        s_out = sem("x_out_ready")
        s_st = [sem(f"x_out_stored{i}") for i in range(2)]
        s_dve = sem("dve_step_attn")

        start_semaphores(nc, sems)
        block = ctx.enter_context(nc.Block())

        @block.sync
        def _(sp):
            sp.dma_start(xt_raw[0][:, :, :], xT[:, :, 0:BLK]).then_inc(s_xt[0], 16)
            for i in range(NW):
                sp.dma_start(w_raw[i][:, :, :], (wT[i] if i < 3 else woT)).then_inc(s_w[i], 16)
            with sp.Fori(0, NB) as b:
                for h in range(2):
                    nxt = b * 2 + 1 if h == 0 else (b * 2 + 2) % (NB * 2)
                    sp.wait_ge(s_xth, START + 2 * b + h)
                    sp.wait_ge(s_xtl, START + 2 * b + h)
                    sp.dma_start(xt_raw[1 - h][:, :, :], xT[:, :, ds(nxt * BLK, BLK)]).then_inc(s_xt[1 - h], 16)
                for t in range(NT + 3):
                    if t < NT:
                        sp.wait_ge(s_r, START + b * NT + max(0, t - 3))
                        sp.dma_start(x_res[t % 4][:, :], x[b * NT + t, :, :]).then_inc(s_xr[t % 4], 16)
                    if t >= 3:
                        u = t - 3
                        sp.wait_ge(s_out, START + NT * b + u + 1)
                        sp.dma_start(x1[b * NT + u, :, :], x_out[u % 2][:, :]).then_inc(s_st[u % 2], 16)
            for i in range(2):
                sp.wait_ge(s_st[i], START + 16 * NB * NT // 2)

        @block.scalar
        def _(act):
            for i in range(NW):
                act.wait_ge(s_w[i], START + 16)
                act.activation(w_hi[i][:, :, :], w_raw[i][:, :, :], ACT.Copy).then_inc(s_wh, 1)
            with act.Fori(0, NB) as b:
                for h in range(2):
                    act.wait_ge(s_xt[h], START + 16 * (b + 1))
                    act.wait_ge(s_q, START + 8 * b + 4 * h)
                    act.activation(xt_hi[:, :, :], xt_raw[h][:, :, :], ACT.Copy).then_inc(s_xth, 1)
                    for t in range(TB):
                        n = TB * h + t
                        act.wait_ge(s_proj, START + NT * b + n + 1)
                        act.wait_ge(s_k, START + NT * b + n)
                        act.activation(e_k[:, :], ps[:, PROJ + 2 * (n % 2), :], ACT.Exp).then_inc(s_ek, 1)
                        act.wait_ge(s_kvt, START + NT * b + max(0, n - 1))
                        act.wait_ge(s_ones, START + 2)
                        act.activation(v1[n % 2][:, :, 0:P], ps[:, PROJ + 2 * (n % 2) + 1, :].rearrange("p (g e) -> p g e", g=KC),
                                       ACT.Copy).then_inc(s_v, 1)
                    for m in range(KC):
                        act.wait_ge(s_q, START + 8 * b + 4 * h + m + 1)
                        act.wait_ge(s_qr, START + 8 * b + 4 * h + m)
                        act.activation(e_q[:, :], ps[:, QP + m % 2, :], ACT.Exp).then_inc(s_eq, 1)
                for t in range(NT):
                    act.wait_ge(s_tp, START + NT * b + t + 1)
                    act.wait_ge(s_y, START + NT * b + max(0, t - 1))
                    act.activation(at_hi[t % 2][:, :, :], ps[:, TP + t % 2, :].rearrange("p (k n) -> p k n", k=KC),
                                   ACT.Copy).then_inc(s_ath, 1)

        @block.vector
        def _(dve):
            steps = Steps(dve, s_dve, NT + 2 * KC + 4 * NT)

            def normalise(u, b):
                dve.wait_ge(s_rstd, START + NT * b + u + 1)
                dve.wait_ge(s_st[u % 2], START + 16 * (NT // 2 * b + u // 2))
                dve.tensor_scalar(x_out[u % 2][:, :], r[u % 3][:, :], mv[u % 3][:, 0:1], rstd[u % 2][:, :],
                                  ALU.subtract, ALU.mult).then_inc(s_out, 1)

            for i in range(2):
                dve.memset(v1[i][:, :, P:P + 1], 1.0).then_inc(s_ones, 1)
            for i in range(NW):
                dve.wait_ge(s_wh, START + i + 1)
                dve.tensor_tensor(w_lo[i][:, :, :], w_raw[i][:, :, :], w_hi[i][:, :, :].bitcast(F32),
                                  ALU.subtract).then_inc(s_wl, 1)
            with dve.Fori(0, NB) as b:
                steps.turn(b)
                for h in range(2):
                    for t in range(TB):
                        n = TB * h + t
                        dve.wait_ge(s_ek, START + NT * b + n + 1)
                        dve.wait_ge(s_kvt, START + NT * b + max(0, n - 1))
                        steps.done(dve.tensor_scalar(e_k[:, :], e_k[:, :], 1.0, None, ALU.min))
                        dve.scalar_tensor_tensor(out=k[n % 2][:, :], in0=ps[:, PROJ + 2 * (n % 2), :], scalar=0.0,
                                                 in1=e_k[:, :], op0=ALU.max, op1=ALU.add).then_inc(s_k, 1)
                    for m in range(KC):
                        dve.wait_ge(s_eq, START + 8 * b + 4 * h + m + 1)
                        steps.done(dve.tensor_scalar(e_q[:, :], e_q[:, :], 1.0, None, ALU.min))
                        dve.scalar_tensor_tensor(out=q[h][:, m, :], in0=ps[:, QP + m % 2, :], scalar=0.0,
                                                 in1=e_q[:, :], op0=ALU.max, op1=ALU.add).then_inc(s_qr, 1)
                dve.wait_ge(s_kvt, START + NT * b + NT)
                kvp = ps[:, KV0:KV0 + 2, 0:2 * (P + 1)].rearrange("p a (g e) -> p a g e", g=2)
                for a in range(2):
                    dve.tensor_tensor(kvz[:, 2 * a:2 * a + 2, 0:P], kvp[:, a, :, 0:P],
                                      const.head_mask[:, :].unsqueeze(1).to_broadcast([P, 2, P]), ALU.mult)
                    ins = dve.tensor_tensor(kvz[:, 2 * a:2 * a + 2, P:P + HG],
                                            kvp[:, a, :, P:P + 1].to_broadcast([P, 2, HG]),
                                            const.head_mask[:, 0:P:DH].unsqueeze(1).to_broadcast([P, 2, HG]), ALU.mult)
                ins.then_inc(s_kv, 1)
                for t in range(NT + 2):
                    if t < NT:
                        num = ps[:, PROJ + 2 * (t % 2):PROJ + 2 * (t % 2) + 2, 0:2 * (P + HG)].rearrange("p a (g e) -> p a g e", g=2)
                        dve.wait_ge(s_num, START + NT * b + t + 1)
                        dve.wait_ge(s_tp, START + NT * b + max(0, t - 1))
                        for a in range(2):
                            ins = dve.tensor_scalar(z[:, 8 * a:8 * a + 8].rearrange("p (g h) -> p g h", g=2), num[:, a, :, P:P + HG], 1e-6, None, ALU.add)
                        steps.done(ins)
                        steps.done(dve.reciprocal(zi[t % 2][:, :], z[:, :]))
                        for a in range(2):
                            ins = dve.tensor_tensor(
                                att[t % 2][:, 256 * a:256 * a + 256].rearrange("p (g h e) -> p g h e", g=2, h=HG),
                                num[:, a, :, 0:P].rearrange("p g (h e) -> p g h e", h=HG),
                                zi[t % 2][:, 8 * a:8 * a + 8].rearrange("p (g h) -> p g h", g=2).unsqueeze(3).to_broadcast([P, 2, HG, DH]),
                                ALU.mult)
                        ins.then_inc(s_att, 1)
                    if 1 <= t <= NT:
                        u = t - 1
                        dve.wait_ge(s_ath, START + NT * b + u + 1)
                        dve.wait_ge(s_y, START + NT * b + max(0, u - 1))
                        dve.tensor_tensor(at_lo[u % 2][:, :, :], ps[:, TP + u % 2, :].rearrange("p (k n) -> p k n", k=KC),
                                          at_hi[u % 2][:, :, :].bitcast(F32), ALU.subtract).then_inc(s_atl, 1)
                    if 2 <= t:
                        u = t - 2
                        dve.wait_ge(s_y, START + NT * b + u + 1)
                        dve.wait_ge(s_xr[u % 4], START + 16 * (NT // 4 * b + u // 4 + 1))
                        dve.wait_ge(s_out, START + NT * b + max(0, u - 2))
                        dve.tensor_tensor(r[u % 3][:, :], ps[:, YP + u % 2, :], x_res[u % 4][:, :], ALU.add).then_inc(s_r, 1)
                        dve.wait_ge(s_r, START + NT * b + u + 1)
                        steps.done(dve.bn_stats(st[u % 3][:, :], r[u % 3][:, :]))
                        dve.memset(filler[:, :], 0.0)
                        steps.done(dve.bn_aggr(mv[u % 3][:, :], st[u % 3][:, :]))
                        dve.tensor_scalar(var[u % 2][:, :], mv[u % 3][:, 1:2], LN_EPS, None, ALU.add).then_inc(s_var, 1)
                    if 3 <= t:
                        normalise(t - 3, b)
                normalise(NT - 1, b)
                steps.end()

        @block.gpsimd
        def _(pool):
            with pool.Fori(0, NB) as b:
                for h in range(2):
                    pool.wait_ge(s_xth, START + 2 * b + h + 1)
                    pool.wait_ge(s_q, START + 8 * b + 4 * h)
                    pool.tensor_tensor(xt_lo[:, :, :], xt_raw[h][:, :, :], xt_hi[:, :, :].bitcast(F32),
                                       ALU.subtract).then_inc(s_xtl, 1)
                for t in range(NT):
                    pool.wait_ge(s_var, START + NT * b + t + 1)
                    pool.tensor_tensor(rstd[t % 2][:, :], var[t % 2][:, :], const.minus_half[:, 0:1], ALU.pow).then_inc(s_rstd, 1)

        @block.tensor
        def _(pe):
            with pe.Fori(0, NB) as b:
                def add_kv(n):
                    pe.wait_ge(s_k, START + NT * b + n + 1)
                    pe.wait_ge(s_v, START + NT * b + n + 1)
                    if n == 0:
                        pe.wait_ge(s_r, START + NT * b)
                    for g in range(KC):
                        ins = pe.matmul(ps[:, KV0 + g // 2, (g % 2) * (P + 1):(g % 2 + 1) * (P + 1)],
                                        k[n % 2][:, g * P:(g + 1) * P], v1[n % 2][:, g, :],
                                        start=(n == 0 and g % 2 == 0), stop=(n == NT - 1), skip_group_check=True)
                    ins.then_inc(s_kvt, 1)

                for h in range(2):
                    pe.wait_ge(s_xth, START + 2 * b + h + 1)
                    pe.wait_ge(s_xtl, START + 2 * b + h + 1)
                    for t in range(TB):
                        n = TB * h + t
                        bank = PROJ + 2 * (n % 2)
                        if n < 2:
                            pe.wait_ge(s_att, START + NT * b)
                        else:
                            pe.wait_ge(s_k, START + NT * b + n - 1)
                            pe.wait_ge(s_v, START + NT * b + n - 1)
                        for i in range(2):
                            pe.wait_ge(s_wh, START + i + 1)
                            pe.wait_ge(s_wl, START + i + 1)
                            for c in range(KC):
                                ins = three_products(pe, ps[:, bank + i, :], xt_hi[:, c, t * P:(t + 1) * P],
                                                     xt_lo[:, c, t * P:(t + 1) * P], w_hi[i][:, c, :], w_lo[i][:, c, :],
                                                     c == 0, c == KC - 1)
                        ins.then_inc(s_proj, 1)
                        if n >= 1:
                            add_kv(n - 1)
                    for m in range(KC):
                        if m < 2 and h == 0:
                            pe.wait_ge(s_atl, START + NT * b)
                        else:
                            pe.wait_ge(s_qr, START + 8 * b + 4 * h + m - 1)
                        pe.wait_ge(s_wh, START + 3)
                        pe.wait_ge(s_wl, START + 3)
                        for c in range(KC):
                            ins = three_products(pe, ps[:, QP + m % 2, :], w_hi[2][:, c, m * P:(m + 1) * P],
                                                 w_lo[2][:, c, m * P:(m + 1) * P], xt_hi[:, c, :], xt_lo[:, c, :],
                                                 c == 0, c == KC - 1)
                        ins.then_inc(s_q, 1)
                        if h == 1 and m == 0:
                            add_kv(NT - 1)
                for t in range(NT + 2):
                    if t < NT:
                        h, col = t // TB, (t % TB) * P
                        if t == 0:
                            pe.wait_ge(s_kv, START + b + 1)
                        if t < 2:
                            pe.wait_ge(s_k, START + NT * b + NT)
                            pe.wait_ge(s_v, START + NT * b + NT)
                        else:
                            pe.wait_ge(s_att, START + NT * b + t - 1)
                        pe.wait_ge(s_qr, START + 8 * b + 4 * h + 4)
                        for g in range(KC):
                            ins = pe.matmul(ps[:, PROJ + 2 * (t % 2) + g // 2, (g % 2) * (P + HG):(g % 2 + 1) * (P + HG)],
                                            q[h][:, g, col:col + P], kvz[:, g, :], start=True, stop=True)
                        ins.then_inc(s_num, 1)
                    if 1 <= t <= NT:
                        u = t - 1
                        pe.wait_ge(s_att, START + NT * b + u + 1)
                        if u < 2:
                            pe.wait_ge(s_qr, START + 8 * b + 8)
                        else:
                            pe.wait_ge(s_atl, START + NT * b + u - 1)
                            pe.wait_ge(s_ath, START + NT * b + u - 1)
                        for m in range(KC):
                            ins = pe.transpose(ps[:, TP + u % 2, m * P:(m + 1) * P], att[u % 2][:, m * P:(m + 1) * P], const.ident[:, :])
                        ins.then_inc(s_tp, 1)
                    if t >= 2:
                        u = t - 2
                        pe.wait_ge(s_ath, START + NT * b + u + 1)
                        pe.wait_ge(s_atl, START + NT * b + u + 1)
                        if u < 2:
                            pe.wait_ge(s_kv, START + b + 1)
                        else:
                            pe.wait_ge(s_r, START + NT * b + u - 1)
                        pe.wait_ge(s_wl, START + 4)
                        for c in range(KC):
                            ins = three_products(pe, ps[:, YP + u % 2, :], at_hi[u % 2][:, c, :], at_lo[u % 2][:, c, :],
                                                 w_hi[3][:, c, :], w_lo[3][:, c, :], c == 0, c == KC - 1)
                        ins.then_inc(s_y, 1)


I_FF = 1408
IT = I_FF // P
NIB = 8
RMS_EPS = 1e-6
SIGN_AND_MAGNITUDE = -0x72000000
FP16_UNBIAS = 16384.0


def fp4_feed_forward(nc, x1, gu_packed, gu_scales, dn_packed, dn_scales, x2, const):
    ctx, sems = ExitStack(), []
    ctx.callback(clear_semaphores, nc, sems)
    with ctx:
        def sb(name, shape, dt=F32):
            return ctx.enter_context(nc.sbuf_tensor(name, shape, dt))

        def sem(name):
            sems.append(nc.alloc_semaphore(name))
            return sems[-1]

        SLOTS = 3
        gu_val = sb("gu_val", [P, 2 * IT, KC, P], F32R)
        dn_hi = sb("dn_hi", [P, IT, C], F32R)
        dn_lo = sb("dn_lo", [P, IT, C], F32R)
        gu_scale16 = sb("gu_scale16", [P, 2 * IT, KC], F16)
        gu_scale = sb("gu_scale", [P, 2 * IT, KC])
        packed = [sb(f"packed{i}", [P, C], I32) for i in range(SLOTS)]
        nib = [sb(f"nib{i}", [P, C], I32) for i in range(SLOTS)]
        scale = [sb(f"scale{i}", [P, C], F16) for i in range(2)]
        scale_hi = [sb(f"scale_hi{i}", [P, C], F16) for i in range(2)]
        scale_lo = [sb(f"scale_lo{i}", [P, C], F16) for i in range(2)]
        dn_val = [sb(f"dn_val{i}", [P, C]) for i in range(2)]
        shift = sb("shift", [P, 1], I32)
        lane = sb("lane", [P, 1], I32)
        xs = sb("xs", [P, TB, C])
        x_res = sb("fx_res", [P, TB, C])
        xt_hi = sb("fxt_hi", [P, KC, BLK], F32R)
        xt_lo = sb("fxt_lo", [P, KC, BLK], F32R)
        acc = [[sb(f"acc{part}_{i}", [P, BLK]) for i in range(2)] for part in range(2)]
        sg = [sb(f"sg{i}", [P, BLK]) for i in range(2)]
        h = [sb(f"h{i}", [P, BLK]) for i in range(2)]
        HS = 3
        h_hi = [sb(f"h_hi{i}", [P, BLK], F32R) for i in range(HS)]
        h_lo = [sb(f"h_lo{i}", [P, BLK], F32R) for i in range(HS)]
        y_sb = sb("y_sb", [P, TB, C])
        ss = sb("ss", [P, TB])
        ms = sb("fms", [P, TB])
        rms = sb("rms", [P, TB])
        r = sb("fr", [P, TB, C])
        st = sb("fst", [P, TB, 6])
        mv = sb("fmv", [P, TB, 2])
        filler = sb("ffiller", [P, 1])
        var = sb("fvar", [P, TB])
        rstd = sb("frstd", [P, TB])

        ps = ctx.enter_context(nc.psum_tensor("ps_fp4", [P, 8, 512], F32))
        Y, G = 0, 4

        s_ln = sem("lane_ready")
        s_sh = sem("shift_ready")
        s_gs = sem("gu_scales_loaded")
        s_gsc = sem("gu_scales_widened")
        s_pk = [sem(f"packed_loaded{i}") for i in range(SLOTS)]
        s_sc = [sem(f"scale_loaded{i}") for i in range(2)]
        s_n1 = sem("nibble_shifted")
        s_n2 = sem("nibble_masked")
        s_s1 = sem("scale_hi_done")
        s_s2 = sem("scale_lo_done")
        s_v = sem("gate_up_values_done")
        s_dv = sem("down_values_done")
        s_dh = sem("down_hi_done")
        s_dl = sem("down_lo_done")
        s_x = sem("xs_loaded")
        s_xr = sem("fx_res_loaded")
        s_tp = sem("x_transposed")
        s_xth = sem("fxt_hi_done")
        s_xtl = sem("fxt_lo_done")
        s_gu = sem("group_projected")
        s_g0 = sem("first_group_scaled")
        s_acc = sem("group_added")
        s_sg = sem("silu_done")
        s_h = sem("h_ready")
        s_hh = sem("h_hi_done")
        s_hl = sem("h_lo_done")
        s_dn = sem("down_added")
        s_ye = sem("y_copied")
        s_ss = sem("squares_summed")
        s_ms = sem("mean_square_ready")
        s_rms = sem("rms_ready")
        s_r = sem("fresidual_added")
        s_st = sem("fstats_done")
        s_ag = sem("faggregated")
        s_var = sem("fvar_ready")
        s_rstd = sem("frstd_ready")
        s_out = sem("fx_out_ready")
        s_sto = sem("fx_out_stored")

        start_semaphores(nc, sems)
        block = ctx.enter_context(nc.Block())

        DOWN = 2
        chunks = [(0, 0), (0, 1)]
        for j in range(IT):
            chunks += [(j + 1, 0), (j + 1, 1)] if j + 1 < IT else []
            chunks.append((j, DOWN))
        NCH = len(chunks)

        def loads(n):
            return 1 if chunks[n][1] == DOWN else KC

        @block.sync
        def _(sp):
            sp.dma_start(xs[:, :, :], x1[0:TB, :, :].rearrange("t p c -> p t c")).then_inc(s_x, 16)
            sp.dma_start(gu_scale16[:, :, :], gu_scales).then_inc(s_gs, 16)
            for n in range(NCH):
                j, part = chunks[n]
                if n >= SLOTS:
                    sp.wait_ge(s_n1, START + n - SLOTS + 1)
                if part == DOWN:
                    if j >= 2:
                        sp.wait_ge(s_s2, START + j - 1)
                    sp.dma_start(packed[n % SLOTS][:, :], dn_packed[j * (P // NIB):(j + 1) * (P // NIB), :].unsqueeze(1)
                                 .to_broadcast([P // NIB, NIB, C])).then_inc(s_pk[n % SLOTS], 16)
                    sp.dma_start(scale[j % 2][:, :], dn_scales[j:j + 1, :].to_broadcast([P, C])).then_inc(s_sc[j % 2], 16)
                else:
                    o = part * IT + j
                    for kk in range(KC):
                        sp.dma_start(packed[n % SLOTS][:, kk * P:(kk + 1) * P], gu_packed[:, kk, o * P:(o + 1) * P]
                                     .unsqueeze(1).to_broadcast([P // NIB, NIB, P])).then_inc(s_pk[n % SLOTS], 16)

            def load(b, nxt):
                sp.wait_ge(s_tp, START + KC * b + KC)
                sp.dma_start(xs[:, :, :], x1[ds(nxt * TB, TB), :, :].rearrange("t p c -> p t c")).then_inc(s_x, 16)

            def load_residual(b):
                sp.dma_start(x_res[:, :, :], x1[ds(b * TB, TB), :, :].rearrange("t p c -> p t c")).then_inc(s_xr, 16)

            def store(b):
                sp.wait_ge(s_out, START + TB * b + TB)
                sp.dma_start(x2[ds(TB * b, TB), :, :].rearrange("t p c -> p t c"), r[:, :, :]).then_inc(s_sto, 16)

            load(0, 1)
            load_residual(0)
            with sp.Fori(1, NBLK) as b:
                load(b, (b + 1) % NBLK)
                store(b - 1)
                load_residual(b)
            store(NBLK - 1)
            sp.wait_ge(s_sto, START + 16 * NBLK)
            sp.wait_ge(s_x, START + 16 * (NBLK + 1))

        @block.scalar
        def _(act):
            act.wait_ge(s_gs, START + 16)
            act.activation(gu_scale[:, :, :], gu_scale16[:, :, :], ACT.Copy).then_inc(s_gsc, 1)
            act.wait_ge(s_gsc, START + 1)

            def x_high(n):
                for c in range(KC):
                    act.wait_ge(s_tp, START + KC * n + c + 1)
                    act.activation(xt_hi[:, c, :], ps[:, G + c, :], ACT.Copy).then_inc(s_xth, 1)

            def values(j, part):
                n = chunks.index((j, part))
                act.wait_ge(s_n2, START + n + 1)
                act.activation(gu_val[:, part * IT + j, :, :].rearrange("p k o -> p (k o)"),
                               nib[n % SLOTS][:, :].bitcast(F16)[:, 1:2 * C:2], ACT.Copy, scale=FP16_UNBIAS).then_inc(s_v, 1)

            def down_values(j):
                n = chunks.index((j, DOWN))
                act.wait_ge(s_n2, START + n + 1)
                if j >= 2:
                    act.wait_ge(s_dh, START + j - 1)
                    act.wait_ge(s_dl, START + j - 1)
                act.activation(dn_val[j % 2][:, :], nib[n % SLOTS][:, :].bitcast(F16)[:, 1:2 * C:2], ACT.Copy,
                               scale=FP16_UNBIAS).then_inc(s_dv, 1)

            def first_group(b, j, part):
                u = 2 * (IT * b + j) + part
                act.wait_ge(s_gu, START + KC * u + 1)
                if part == 0:
                    act.wait_ge(s_sg, START + IT * b + max(0, j - 1))
                else:
                    act.wait_ge(s_h, START + IT * b + max(0, j - 1))
                act.activation(acc[part][j % 2][:, :], ps[:, G, :], ACT.Copy,
                               scale=gu_scale[:, part * IT + j, 0:1]).then_inc(s_g0, 1)

            def silu(b, j):
                act.wait_ge(s_acc, START + 3 * (2 * (IT * b + j)) + 3)
                act.wait_ge(s_h, START + IT * b + max(0, j - 1))
                act.activation(sg[j % 2][:, :], acc[0][j % 2][:, :], ACT.Silu).then_inc(s_sg, 1)

            def h_high(b, j):
                act.wait_ge(s_h, START + IT * b + j + 1)
                act.wait_ge(s_dn, START + IT * b + max(0, j - HS + 1))
                act.activation(h_hi[j % HS][:, :], h[j % 2][:, :], ACT.Copy).then_inc(s_hh, 1)

            def squares(b):
                act.wait_ge(s_sto, START + 16 * b)
                act.wait_ge(s_ye, START + TB * b + TB)
                for t in range(TB):
                    act.activation(r[:, t, :], y_sb[:, t, :], ACT.Square, accum_out=ss[:, t:t + 1]).then_inc(s_ss, 1)

            def run(b, first):
                for j in range(IT):
                    first_group(b, j, 0)
                    if first and j + 1 < IT:
                        values(j + 1, 0)
                    if j:
                        h_high(b, j - 1)
                    first_group(b, j, 1)
                    silu(b, j)
                    if first and j + 1 < IT:
                        values(j + 1, 1)
                    if first:
                        down_values(j)
                    if not first and j == 0:
                        squares(b - 1)
                h_high(b, IT - 1)
                x_high(b + 1)
                act.wait_ge(s_dn, START + IT * b + IT)
                act.wait_ge(s_r, START + TB * b)
                for t in range(TB):
                    act.activation(y_sb[:, t, :], ps[:, Y + t, :], ACT.Copy).then_inc(s_ye, 1)

            x_high(0)
            values(0, 0)
            values(0, 1)
            run(0, True)
            with act.Fori(1, NBLK) as b:
                run(b, False)
            squares(NBLK - 1)

        @block.vector
        def _(dve):
            dve.wait_ge(s_ln, START + 1)
            dve.tensor_scalar(lane[:, :], lane[:, :], NIB - 1, 2, ALU.bitwise_and, ALU.logical_shift_left).then_inc(s_sh, 1)
            dve.wait_ge(s_sh, START + 1)
            dve.tensor_scalar(shift[:, :], lane[:, :], -1.0, 28.0, ALU.mult, ALU.add).then_inc(s_sh, 1)
            dve.wait_ge(s_sh, START + 2)

            def nibbles(n):
                j, part = chunks[n]
                i = n % SLOTS
                dve.wait_ge(s_pk[i], START + 16 * sum(loads(m) for m in range(i, n + 1, SLOTS)))
                if n >= SLOTS:
                    held, held_part = chunks[n - SLOTS]
                    if held_part == DOWN:
                        dve.wait_ge(s_dv, START + held + 1)
                    else:
                        dve.wait_ge(s_v, START + 2 * held + held_part + 1)
                dve.tensor_scalar(nib[i][:, :], packed[i][:, :], shift[:, 0:1], 3, ALU.logical_shift_left,
                                  ALU.arith_shift_right).then_inc(s_n1, 1)
                dve.wait_ge(s_n1, START + n + 1)
                dve.tensor_scalar(nib[i][:, :], nib[i][:, :], SIGN_AND_MAGNITUDE, None, ALU.bitwise_and).then_inc(s_n2, 1)

            def down_scales(j):
                i = j % 2
                dve.wait_ge(s_sc[i], START + 16 * (j // 2 + 1))
                if j >= 2:
                    dve.wait_ge(s_s2, START + j - 1)
                    dve.wait_ge(s_dh, START + j - 1)
                dve.tensor_scalar(scale_hi[i][:, :].bitcast(U16), scale[i][:, :].bitcast(U16), 0xFFFE, None,
                                  ALU.bitwise_and).then_inc(s_s1, 1)

            def down_high(j):
                dve.wait_ge(s_dv, START + j + 1)
                dve.wait_ge(s_s1, START + j + 1)
                dve.tensor_tensor(dn_hi[:, j, :], dn_val[j % 2][:, :], scale_hi[j % 2][:, :], ALU.mult).then_inc(s_dh, 1)

            def x_low(n):
                for c in range(KC):
                    dve.wait_ge(s_xth, START + KC * n + c + 1)
                    dve.tensor_tensor(xt_lo[:, c, :], ps[:, G + c, :], xt_hi[:, c, :].bitcast(F32), ALU.subtract).then_inc(s_xtl, 1)

            def groups(b, j, part):
                u = 2 * (IT * b + j) + part
                a = acc[part][j % 2]
                for c in range(1, KC):
                    dve.wait_ge(s_gu, START + KC * u + c + 1)
                    if c == 1:
                        dve.wait_ge(s_g0, START + u + 1)
                    else:
                        dve.wait_ge(s_acc, START + 3 * u + c - 1)
                    dve.scalar_tensor_tensor(out=a[:, :], in0=ps[:, G + c, :], scalar=gu_scale[:, part * IT + j, c:c + 1],
                                             in1=a[:, :], op0=ALU.mult, op1=ALU.add).then_inc(s_acc, 1)

            def mean_square(b):
                dve.wait_ge(s_ss, START + TB * b + TB)
                dve.tensor_scalar(ms[:, :], ss[:, :], 1.0 / C, RMS_EPS, ALU.mult, ALU.add).then_inc(s_ms, 1)

            def finish_rows(b, t):
                if t == 0:
                    dve.wait_ge(s_rms, START + b + 1)
                    dve.wait_ge(s_xr, START + 16 * (b + 1))
                dve.scalar_tensor_tensor(out=r[:, t, :], in0=y_sb[:, t, :], scalar=rms[:, t:t + 1], in1=x_res[:, t, :],
                                         op0=ALU.mult, op1=ALU.add).then_inc(s_r, 1)
                dve.wait_ge(s_r, START + TB * b + t + 1)
                dve.memset(filler[:, :], 0.0)
                dve.bn_stats(st[:, t, :], r[:, t, :]).then_inc(s_st, 1)

            def variance(b):
                dve.wait_ge(s_st, START + TB * b + TB)
                dve.memset(filler[:, :], 0.0)
                for t in range(TB):
                    dve.bn_aggr(mv[:, t, :], st[:, t, :]).then_inc(s_ag, 1)
                dve.wait_ge(s_ag, START + TB * b + TB)
                dve.tensor_scalar(var[:, :], mv[:, :, 1], LN_EPS, None, ALU.add).then_inc(s_var, 1)

            def normalise(b, t):
                if t == 0:
                    dve.wait_ge(s_rstd, START + b + 1)
                dve.tensor_scalar(r[:, t, :], r[:, t, :], mv[:, t, 0:1], rstd[:, t:t + 1], ALU.subtract,
                                  ALU.mult).then_inc(s_out, 1)

            def run(b, first):
                for j in range(IT):
                    groups(b, j, 0)
                    if first and j + 1 < IT:
                        nibbles(chunks.index((j + 1, 0)))
                    if first and j >= 1:
                        down_high(j - 1)
                    groups(b, j, 1)
                    if first:
                        if j + 1 < IT:
                            nibbles(chunks.index((j + 1, 1)))
                        down_scales(j)
                        nibbles(chunks.index((j, DOWN)))
                    elif j == 1:
                        mean_square(b - 1)
                    elif 2 <= j < 2 + TB:
                        finish_rows(b - 1, j - 2)
                    elif j == 2 + TB:
                        variance(b - 1)
                    elif j >= IT - TB:
                        normalise(b - 1, j - (IT - TB))
                if first:
                    down_high(IT - 1)
                x_low(b + 1)

            nibbles(0)
            nibbles(1)
            x_low(0)
            dve.wait_ge(s_gsc, START + 1)
            run(0, True)
            with dve.Fori(1, NBLK) as b:
                run(b, False)
            mean_square(NBLK - 1)
            for t in range(TB):
                finish_rows(NBLK - 1, t)
            variance(NBLK - 1)
            for t in range(TB):
                normalise(NBLK - 1, t)

        @block.gpsimd
        def _(pool):
            pool.iota(lane[:, :], pattern=[[0, 1]], base=0, channel_multiplier=1).then_inc(s_ln, 1)

            def down_low(j):
                i = j % 2
                pool.wait_ge(s_s1, START + j + 1)
                pool.tensor_tensor(scale_lo[i][:, :], scale[i][:, :], scale_hi[i][:, :], ALU.subtract).then_inc(s_s2, 1)
                pool.wait_ge(s_dv, START + j + 1)
                pool.wait_ge(s_s2, START + j + 1)
                pool.tensor_tensor(dn_lo[:, j, :], dn_val[i][:, :], scale_lo[i][:, :], ALU.mult).then_inc(s_dl, 1)

            def product(b, j):
                pool.wait_ge(s_sg, START + IT * b + j + 1)
                pool.wait_ge(s_acc, START + 3 * (2 * (IT * b + j) + 1) + 3)
                pool.wait_ge(s_hl, START + IT * b + max(0, j - 1))
                pool.wait_ge(s_hh, START + IT * b + max(0, j - 1))
                pool.tensor_tensor(h[j % 2][:, :], sg[j % 2][:, :], acc[1][j % 2][:, :], ALU.mult).then_inc(s_h, 1)

            def h_low(b, j):
                pool.wait_ge(s_hh, START + IT * b + j + 1)
                pool.wait_ge(s_dn, START + IT * b + max(0, j - HS + 1))
                pool.tensor_tensor(h_lo[j % HS][:, :], h[j % 2][:, :], h_hi[j % HS][:, :].bitcast(F32), ALU.subtract).then_inc(s_hl, 1)

            def inverse_rms(b):
                pool.wait_ge(s_ms, START + b + 1)
                pool.tensor_tensor(rms[:, :], ms[:, :], const.minus_half[:, :], ALU.pow).then_inc(s_rms, 1)

            def inverse_std(b):
                pool.wait_ge(s_var, START + b + 1)
                pool.tensor_tensor(rstd[:, :], var[:, :], const.minus_half[:, :], ALU.pow).then_inc(s_rstd, 1)

            for j in range(IT):
                product(0, j)
                down_low(j)
                h_low(0, j)
            with pool.Fori(1, NBLK) as b:
                for j in range(IT):
                    product(b, j)
                    h_low(b, j)
                    if j == 1:
                        inverse_rms(b - 1)
                    if j == 2 + TB:
                        inverse_std(b - 1)
            inverse_rms(NBLK - 1)
            inverse_std(NBLK - 1)

        @block.tensor
        def _(pe):
            def bank_left(u, c):
                if c == 0:
                    pe.wait_ge(s_g0, START + u)
                else:
                    pe.wait_ge(s_acc, START + 3 * (u - 1) + c)

            def transposes(n, first=False):
                pe.wait_ge(s_x, START + 16 * (n + 1))
                for c in range(KC):
                    if not first:
                        bank_left(2 * IT * n, c)
                    for t in range(TB):
                        ins = pe.transpose(ps[:, G + c, t * P:(t + 1) * P], xs[:, t, c * P:(c + 1) * P], const.ident[:, :])
                    ins.then_inc(s_tp, 1)

            def project(b, j, part, first):
                u = 2 * (IT * b + j) + part
                o = part * IT + j
                if first:
                    pe.wait_ge(s_v, START + 2 * j + part + 1)
                for c in range(KC):
                    if j == 0 and part == 0:
                        pe.wait_ge(s_xtl, START + KC * b + c + 1)
                    else:
                        bank_left(u, c)
                    pe.matmul(ps[:, G + c, :], gu_val[:, o, c, :], xt_hi[:, c, :], start=True, stop=False)
                    pe.matmul(ps[:, G + c, :], gu_val[:, o, c, :], xt_lo[:, c, :], start=False, stop=True).then_inc(s_gu, 1)

            def down(b, j, half, first):
                if half == 0:
                    pe.wait_ge(s_hh, START + IT * b + j + 1)
                    pe.wait_ge(s_hl, START + IT * b + j + 1)
                    if first:
                        pe.wait_ge(s_dh, START + j + 1)
                        pe.wait_ge(s_dl, START + j + 1)
                for t in range(2 * half, 2 * half + 2):
                    if j == 0 and not first:
                        pe.wait_ge(s_ye, START + TB * (b - 1) + t + 1)
                    ins = three_products(pe, ps[:, Y + t, :], h_hi[j % HS][:, t * P:(t + 1) * P], h_lo[j % HS][:, t * P:(t + 1) * P],
                                         dn_hi[:, j, :], dn_lo[:, j, :], j == 0, j == IT - 1)
                if half == 1:
                    ins.then_inc(s_dn, 1)

            def run(b, first):
                for j in range(IT):
                    project(b, j, 0, first)
                    if j >= 2:
                        down(b, j - 2, 0, first)
                    project(b, j, 1, first)
                    if j >= 2:
                        down(b, j - 2, 1, first)
                down(b, IT - 2, 0, first)
                down(b, IT - 2, 1, first)
                transposes(b + 1)
                down(b, IT - 1, 0, first)
                down(b, IT - 1, 1, first)

            transposes(0, first=True)
            run(0, True)
            with pe.Fori(1, NBLK) as b:
                run(b, False)


HALF = 64
DK = 32
GLA_EPS = 1e-5


def gated_linear_attention(nc, x2, wqkT, wogT, wigT, woT, norm_w, router_w, x3, score, const):
    ctx, sems = ExitStack(), []
    ctx.callback(clear_semaphores, nc, sems)
    with ctx:
        def sb(name, shape, dt=F32):
            return ctx.enter_context(nc.sbuf_tensor(name, shape, dt))

        def sem(name):
            sems.append(nc.alloc_semaphore(name))
            return sems[-1]

        WQK, WIG, WOG, WO = range(4)
        NW = 4
        w_cols = [P, C, C, C]
        w_raw = [sb(f"gw_raw{i}", [P, KC, w_cols[i]]) for i in range(NW)]
        w_hi = [sb(f"gw_hi{i}", [P, KC, w_cols[i]], F32R) for i in range(NW)]
        w_lo = [sb(f"gw_lo{i}", [P, KC, w_cols[i]], F32R) for i in range(NW)]
        nw = sb("norm_w_sb", [P, KC])
        xs = [sb(f"gxs{i}", [P, TB, C]) for i in range(2)]
        xt_hi = sb("gxt_hi", [P, KC, BLK], F32R)
        xt_lo = sb("gxt_lo", [P, KC, BLK], F32R)
        qk_f = sb("qk_f", [P, BLK])
        q_max = sb("q_max", [P, TB])
        q_sum = sb("q_sum", [P, TB])
        q_inv = sb("q_inv", [P, TB])
        qx = sb("qx", [P, TB, DK])
        qs = sb("qs", [P, TB, DK])
        kx = sb("kx", [P, TB, DK])
        ks = sb("ks", [P, TB, DK])
        sp = sb("sp", [P, TB, DK])
        decay = sb("decay", [P, 4, TB, DK])
        grow = sb("grow", [P, TB, DK])
        QH, QT, KA, KB = range(4)
        feats = sb("feats", [P, 4, TB, DK])
        k_end = sb("k_end", [P, TB, DK])
        ft = [sb(f"ft{i}", [DK, 4, P]) for i in range(2)]
        at = [sb(f"gat{i}", [P, P]) for i in range(2)]
        state = sb("state", [DK, C])
        dec = sb("dec", [DK, TB])
        o_f = sb("o_f", [P, KC, BLK])
        o_hi = sb("o_hi", [P, KC, BLK], F32R)
        o_lo = sb("o_lo", [P, KC, BLK], F32R)
        sq = sb("sq", [P, KC, P])
        sg = [sb(f"gsg{i}", [P, BLK]) for i in range(2)]
        p_hi = sb("p_hi", [P, KC, BLK], F32R)
        p_lo = sb("p_lo", [P, KC, BLK], F32R)
        ms = sb("ms", [P, TB])
        rms = sb("grms", [P, TB])
        r = sb("gr", [P, TB, C])
        st = sb("gst", [P, TB, 6])
        mv = sb("gmv", [P, TB, 2])
        var = sb("gvar", [P, TB])
        rstd = sb("grstd", [P, TB])
        filler = sb("gfiller", [P, 1])
        rw_sb = sb("rw_sb", [P, C])
        junk = sb("gjunk", [P, C])
        dot = sb("dot", [P, TB])

        ps = ctx.enter_context(nc.psum_tensor("ps_gla", [P, 8, 512], F32))
        F, A, S, O, GO = 0, 1, 2, 3, 4
        D_COL, SS_COL = 128, 132

        s_nw = sem("norm_w_loaded")
        s_w = [sem(f"gw_loaded{i}") for i in range(NW)]
        s_fold = sem("norm_w_folded")
        s_wh = sem("gw_hi_done")
        s_wl = sem("gw_lo_done_by_dve")
        s_wlp = sem("gw_lo_done_by_pool")
        s_zero = sem("rows_zeroed")
        s_x = [sem(f"gx_loaded{i}") for i in range(2)]
        s_tp = sem("gx_transposed")
        s_xth = sem("gxt_hi_done")
        s_xtl = sem("gxt_lo_done")
        s_qk = sem("qk_projected")
        s_qkf = sem("qk_taken")
        s_tok = sem("qk_transposed")
        s_qx = sem("q_shifted")
        s_qe = sem("q_exp_done_gla")
        s_ke = sem("k_exp_done_gla")
        s_ks = sem("k_sigmoid_done")
        s_k2 = sem("k_exp2_done")
        s_sp = sem("softplus_done")
        s_sum = sem("gate_sums_done")
        s_dec = sem("decays_done")
        s_ft = sem("feats_ready")
        s_ftt = sem("feats_transposed")
        s_fts = sem("feats_taken")
        s_a = sem("scores_done")
        s_at = sem("scores_masked")
        s_su = sem("state_update_done")
        s_dexp = sem("state_decay_ready")
        s_s = sem("state_ready")
        s_o = sem("o_done")
        s_of = sem("o_copied")
        s_sq = sem("o_squared")
        s_oh = sem("o_hi_done")
        s_ol = sem("o_lo_done")
        s_ss = sem("o_squares_summed")
        s_go = sem("go_done")
        s_sg = sem("gsilu_done")
        s_p = sem("p_ready")
        s_ph = sem("p_hi_done")
        s_pl = sem("p_lo_done")
        s_y = sem("gy_done")
        s_ms = sem("gmean_square_ready")
        s_rms = sem("grms_ready")
        s_r = sem("gresidual_added")
        s_st = sem("gstats_done")
        s_ag = sem("gaggregated")
        s_var = sem("gvar_ready")
        s_rstd = sem("grstd_ready")
        s_out = sem("gx_out_ready")
        s_sto = sem("gx_out_stored")
        s_rw = sem("router_w_loaded")
        s_sc = sem("scores_kept")
        s_dot = sem("score_dot_done")
        s_dve = sem("dve_step_gla")

        start_semaphores(nc, sems)
        block = ctx.enter_context(nc.Block())

        @block.sync
        def _(sp_):
            sp_.dma_start(w_raw[WQK][:, :, 0:2 * DK], wqkT).then_inc(s_w[WQK], 16)
            sp_.dma_start(w_raw[WQK][:, :, 2 * DK:P], wqkT).then_inc(s_w[WQK], 16)
            sp_.dma_start(xs[0][:, :, :], x2[0:TB, :, :].rearrange("t p c -> p t c")).then_inc(s_x[0], 16)
            sp_.dma_start(w_raw[WIG][:, :, :], wigT).then_inc(s_w[WIG], 16)
            sp_.dma_start(w_raw[WOG][:, :, :], wogT).then_inc(s_w[WOG], 16)
            sp_.dma_start(w_raw[WO][:, :, :], woT).then_inc(s_w[WO], 16)
            sp_.dma_start(nw[:, :], norm_w).then_inc(s_nw, 16)
            sp_.dma_start(rw_sb[:, :], router_w.to_broadcast([P, C])).then_inc(s_rw, 16)
            with sp_.Fori(0, NB) as b:
                for h in range(2):
                    n = 2 * b + h
                    sp_.wait_ge(s_r, START + TB * n)
                    sp_.dma_start(xs[1 - h][:, :, :], x2[ds((n + 1) % NBLK * TB, TB), :, :].rearrange("t p c -> p t c")).then_inc(s_x[1 - h], 16)
                    sp_.wait_ge(s_out, START + TB * n + TB)
                    sp_.dma_start(x3[ds(TB * n, TB), :, :].rearrange("t p c -> p t c"), r[:, :, :]).then_inc(s_sto, 16)
            sp_.wait_ge(s_sto, START + 16 * NBLK)
            sp_.wait_ge(s_x[0], START + 16 * (NB + 1))

        @block.scalar
        def _(act):
            def weight_high(i):
                act.wait_ge(s_w[i], START + (32 if i == WQK else 16))
                if i == WO:
                    act.wait_ge(s_fold, START + KC)
                act.activation(w_hi[i][:, :, :], w_raw[i][:, :, :], ACT.Copy).then_inc(s_wh, 1)

            def x_high(n):
                for c in range(KC):
                    act.wait_ge(s_tp, START + KC * n + c + 1)
                    act.activation(xt_hi[:, c, :], ps[:, GO + c, :], ACT.Copy).then_inc(s_xth, 1)

            weight_high(WQK)
            x_high(0)
            weight_high(WIG)
            weight_high(WOG)
            weight_high(WO)
            with act.Fori(0, NB) as b:
                for h in range(2):
                    n = 2 * b + h
                    act.wait_ge(s_qk, START + n + 1)
                    act.activation(qk_f[:, :], ps[:, F, :], ACT.Copy).then_inc(s_qkf, 1)
                    tok = ps[:, A, :].rearrange("p (t f) -> p t f", t=TB)
                    act.wait_ge(s_qx, START + n + 1)
                    act.activation(kx[:, :, :], tok[:, :, DK:2 * DK], ACT.Exp, scale=-1.0).then_inc(s_ke, 1)
                    act.activation(qx[:, :, :], qx[:, :, :], ACT.Exp).then_inc(s_qe, 1)
                    act.wait_ge(s_ks, START + n + 1)
                    act.activation(kx[:, :, :], ks[:, :, :], ACT.Exp).then_inc(s_k2, 1)
                    act.wait_ge(s_k2, START + n + 1)
                    act.activation(sp[:, :, :], kx[:, :, :], ACT.Ln, bias=1.0).then_inc(s_sp, 1)
                    act.wait_ge(s_sum, START + n + 1)
                    act.wait_ge(s_ft, START + 5 * n)
                    act.activation(decay[:, :, :, :].rearrange("p a t d -> p (a t d)"), ps[:, F, :], ACT.Exp, scale=-1.0).then_inc(s_dec, 1)
                    act.activation(grow[:, :, :].rearrange("p t d -> p (t d)"), ps[:, F, 0:P], ACT.Exp).then_inc(s_dec, 1)
                    act.wait_ge(s_s, START + 2 * TB * b + TB * h + b + 1)
                    act.activation(dec[:, :], ps[0:DK, A, D_COL:D_COL + TB], ACT.Exp, scale=-1.0).then_inc(s_dexp, 1)

                    def take_feats(t):
                        i = TB * n + t
                        act.wait_ge(s_ftt, START + i + 1)
                        act.wait_ge(s_o, START + TB * n + max(0, t - 1))
                        act.activation(ft[t % 2][:, :, :].rearrange("d a n -> d (a n)"), ps[0:DK, F, :], ACT.Copy).then_inc(s_fts, 1)

                    take_feats(0)
                    for t in range(TB):
                        i = TB * n + t
                        if t + 1 < TB:
                            take_feats(t + 1)
                        act.wait_ge(s_o, START + i + 1)
                        o = ps[:, O, :].rearrange("p (m n) -> p m n", m=KC)
                        o_t = o_f[:, :, t * P:(t + 1) * P]
                        act.activation(o_t, o, ACT.Copy).then_inc(s_of, 1)
                        act.wait_ge(s_of, START + i + 1)
                        act.wait_ge(s_ss, START + i)
                        act.activation(sq[:, :, :], o_t, ACT.Square).then_inc(s_sq, 1)
                        act.activation(o_hi[:, :, t * P:(t + 1) * P], o_t, ACT.Copy).then_inc(s_oh, 1)
                    for m in range(KC):
                        act.wait_ge(s_go, START + KC * n + m + 1)
                        act.wait_ge(s_pl, START + KC * n + max(0, m - 1))
                        act.activation(sg[m % 2][:, :], ps[:, GO + m, :], ACT.Silu).then_inc(s_sg, 1)
                        act.wait_ge(s_p, START + KC * n + m + 1)
                        act.activation(p_hi[:, m, :], sg[m % 2][:, :], ACT.Copy).then_inc(s_ph, 1)
                    x_high(n + 1)

        @block.vector
        def _(dve):
            def x_low(n):
                for c in range(KC):
                    dve.wait_ge(s_xth, START + KC * n + c + 1)
                    dve.tensor_tensor(xt_lo[:, c, :], ps[:, GO + c, :], xt_hi[:, c, :].bitcast(F32), ALU.subtract).then_inc(s_xtl, 1)

            def weight_low(i):
                dve.wait_ge(s_wh, START + i + 1)
                dve.tensor_tensor(w_lo[i][:, :, :], w_raw[i][:, :, :], w_hi[i][:, :, :].bitcast(F32), ALU.subtract).then_inc(s_wl, 1)

            def score_tile(n, t):
                dve.wait_ge(s_out, START + TB * n)
                dve.wait_ge(s_dot, START + TB * n + t)
                dve.tensor_tensor_reduce(out=junk[:, :], in0=r[:, t, :], in1=rw_sb[:, :], scale=1.0, scalar=0.0,
                                         op0=ALU.mult, op1=ALU.add, accum_out=dot[:, t:t + 1]).then_inc(s_dot, 1)

            def keep_scores(n):
                dve.wait_ge(s_dot, START + TB * n + TB)
                dve.tensor_copy(score[:, ds(TB * n, TB)], dot[:, :]).then_inc(s_sc, 1)

            steps = Steps(dve, s_dve, 2 * 5)
            dve.memset(r[:, :, :], 0.0).then_inc(s_zero, 1)
            weight_low(WQK)
            x_low(0)
            weight_low(WIG)
            dve.wait_ge(s_nw, START + 16)
            dve.wait_ge(s_rw, START + 16)
            dve.wait_ge(s_w[WO], START + 16)
            for c in range(KC):
                dve.tensor_scalar(w_raw[WO][:, c, :], w_raw[WO][:, c, :], nw[:, c:c + 1], None, ALU.mult).then_inc(s_fold, 1)
            dve.wait_ge(s_zero, START + 1)
            with dve.Fori(0, NB) as b:
                steps.turn(b)
                dve.wait_ge(s_o, START + 2 * TB * b)
                dve.memset(state[:, :], 0.0).then_inc(s_s, 1)
                for h in range(2):
                    n = 2 * b + h
                    dve.wait_ge(s_tok, START + n + 1)
                    tok = ps[:, A, :].rearrange("p (t f) -> p t f", t=TB)
                    steps.done(dve.tensor_reduce(q_max[:, :], tok[:, :, 0:DK], AX.X, ALU.max))
                    dve.tensor_tensor(qx[:, :, :], tok[:, :, 0:DK], q_max[:, :].unsqueeze(2).to_broadcast([P, TB, DK]),
                                      ALU.subtract).then_inc(s_qx, 1)
                    dve.wait_ge(s_ke, START + n + 1)
                    steps.done(dve.tensor_scalar(kx[:, :, :], kx[:, :, :], 1.0, None, ALU.add))
                    dve.reciprocal(ks[:, :, :], kx[:, :, :]).then_inc(s_ks, 1)
                    dve.wait_ge(s_qe, START + n + 1)
                    steps.done(dve.tensor_reduce(q_sum[:, :], qx[:, :, :], AX.X, ALU.add))
                    steps.done(dve.reciprocal(q_inv[:, :], q_sum[:, :]))
                    steps.done(dve.tensor_tensor(qs[:, :, :], qx[:, :, :], q_inv[:, :].unsqueeze(2).to_broadcast([P, TB, DK]), ALU.mult))
                    dve.wait_ge(s_dec, START + 2 * n + 2)
                    dve.wait_ge(s_su, START + TB * n)
                    dve.wait_ge(s_ks, START + n + 1)
                    dve.tensor_tensor(feats[:, QH, :, :], qs[:, :, :], decay[:, 0, :, :], ALU.mult).then_inc(s_ft, 1)
                    dve.tensor_tensor(feats[:, KA, :, :], ks[:, :, :], grow[:, :, :], ALU.mult).then_inc(s_ft, 1)
                    dve.tensor_tensor(feats[:, KB, :, :], ks[:, :, :], decay[:, 1, :, :], ALU.mult).then_inc(s_ft, 1)
                    dve.tensor_tensor(feats[:, QT, :, :], qs[:, :, :], decay[:, 2, :, :], ALU.mult).then_inc(s_ft, 1)
                    dve.tensor_tensor(k_end[:, :, :], ks[:, :, :], decay[:, 3, :, :], ALU.mult).then_inc(s_ft, 1)

                    def mask(t):
                        i = TB * n + t
                        dve.wait_ge(s_a, START + i + 1)
                        dve.tensor_tensor(at[t % 2][:, :], ps[:, A, 0:P], const.upto[:, :], ALU.mult).then_inc(s_at, 1)

                    mask(0)
                    dve.wait_ge(s_sc, START + n)
                    for t in range(TB):
                        i = TB * n + t
                        dve.wait_ge(s_dexp, START + n + 1)
                        dve.wait_ge(s_su, START + i + 1)
                        dve.wait_ge(s_o, START + i + 1)
                        dve.scalar_tensor_tensor(out=state[:, :], in0=state[:, :], scalar=dec[:, t:t + 1],
                                                 in1=ps[0:DK, S, :], op0=ALU.mult, op1=ALU.add).then_inc(s_s, 1)
                        if t + 1 < TB:
                            mask(t + 1)
                        dve.wait_ge(s_oh, START + i + 1)
                        dve.tensor_tensor(o_lo[:, :, t * P:(t + 1) * P], o_f[:, :, t * P:(t + 1) * P],
                                          o_hi[:, :, t * P:(t + 1) * P].bitcast(F32), ALU.subtract).then_inc(s_ol, 1)
                        score_tile(n, t)
                    keep_scores(n)
                    dve.wait_ge(s_ss, START + TB * n + TB)
                    dve.tensor_scalar(ms[:, :], ps[:, A, SS_COL:SS_COL + TB], 1.0 / C, GLA_EPS, ALU.mult, ALU.add).then_inc(s_ms, 1)
                    for m in range(KC):
                        dve.wait_ge(s_sg, START + KC * n + m + 1)
                        dve.tensor_tensor(sg[m % 2][:, :], sg[m % 2][:, :], o_f[:, m, :], ALU.mult).then_inc(s_p, 1)
                    x_low(n + 1)
                    dve.wait_ge(s_rms, START + n + 1)
                    dve.wait_ge(s_sto, START + 16 * n)
                    dve.wait_ge(s_dot, START + TB * n + TB)
                    for t in range(TB):
                        dve.wait_ge(s_y, START + TB * n + t + 1)
                        dve.scalar_tensor_tensor(out=r[:, t, :], in0=ps[:, t, :], scalar=rms[:, t:t + 1], in1=xs[h][:, t, :],
                                                 op0=ALU.mult, op1=ALU.add).then_inc(s_r, 1)
                        dve.wait_ge(s_r, START + TB * n + t + 1)
                        dve.memset(filler[:, :], 0.0)
                        dve.bn_stats(st[:, t, :], r[:, t, :]).then_inc(s_st, 1)
                    dve.wait_ge(s_st, START + TB * n + TB)
                    dve.memset(filler[:, :], 0.0)
                    for t in range(TB):
                        dve.bn_aggr(mv[:, t, :], st[:, t, :]).then_inc(s_ag, 1)
                    dve.wait_ge(s_ag, START + TB * n + TB)
                    dve.tensor_scalar(var[:, :], mv[:, :, 1], LN_EPS, None, ALU.add).then_inc(s_var, 1)
                    dve.wait_ge(s_rstd, START + n + 1)
                    for t in range(TB):
                        dve.tensor_scalar(r[:, t, :], r[:, t, :], mv[:, t, 0:1], rstd[:, t:t + 1], ALU.subtract,
                                          ALU.mult).then_inc(s_out, 1)
                steps.end()
            dve.wait_ge(s_out, START + TB * NBLK)
            dve.wait_ge(s_sc, START + NBLK)
            for t in range(TB):
                score_tile(NBLK, t)
            keep_scores(NBLK)

        @block.gpsimd
        def _(pool):
            for i in (WOG, WO):
                pool.wait_ge(s_wh, START + i + 1)
                pool.tensor_tensor(w_lo[i][:, :, :], w_raw[i][:, :, :], w_hi[i][:, :, :].bitcast(F32), ALU.subtract).then_inc(s_wlp, 1)
            with pool.Fori(0, NB) as b:
                for h in range(2):
                    n = 2 * b + h
                    pool.wait_ge(s_ms, START + n + 1)
                    pool.tensor_tensor(rms[:, :], ms[:, :], const.minus_half[:, :], ALU.pow).then_inc(s_rms, 1)
                    for m in range(KC):
                        pool.wait_ge(s_ph, START + KC * n + m + 1)
                        pool.tensor_tensor(p_lo[:, m, :], sg[m % 2][:, :], p_hi[:, m, :].bitcast(F32), ALU.subtract).then_inc(s_pl, 1)
                    pool.wait_ge(s_var, START + n + 1)
                    pool.tensor_tensor(rstd[:, :], var[:, :], const.minus_half[:, :], ALU.pow).then_inc(s_rstd, 1)

        @block.tensor
        def _(pe):
            def transposes(x_in):
                for c in range(KC):
                    for t in range(TB):
                        ins = pe.transpose(ps[:, GO + c, t * P:(t + 1) * P], x_in[:, t, c * P:(c + 1) * P], const.ident[:, :])
                    ins.then_inc(s_tp, 1)

            pe.wait_ge(s_x[0], START + 16)
            transposes(xs[0])
            with pe.Fori(0, NB) as b:
                for h in range(2):
                    n = 2 * b + h
                    x_in = xs[h]

                    def gate(m, half, last):
                        w, hi, lo = ((WIG, xt_hi, xt_lo), (WOG, o_hi, o_lo))[half]
                        for c in range(KC):
                            ins = three_products(pe, ps[:, GO + m, :], w_hi[w][:, c, m * P:(m + 1) * P], w_lo[w][:, c, m * P:(m + 1) * P],
                                                 hi[:, c, :], lo[:, c, :], half == 0 and c == 0, last and c == KC - 1)
                        return ins

                    pe.wait_ge(s_xtl, START + KC * n + KC)
                    pe.wait_ge(s_r, START + TB * n)
                    pe.wait_ge(s_wl, START + 1)
                    for c in range(KC):
                        ins = three_products(pe, ps[:, F, :], w_hi[WQK][:, c, :], w_lo[WQK][:, c, :], xt_hi[:, c, :], xt_lo[:, c, :],
                                             c == 0, c == KC - 1)
                    ins.then_inc(s_qk, 1)
                    pe.wait_ge(s_wl, START + 2)
                    gate(0, 0, False)
                    pe.wait_ge(s_qkf, START + n + 1)
                    pe.wait_ge(s_ms, START + n)
                    for t in range(TB):
                        ins = pe.transpose(ps[:, A, t * P:(t + 1) * P], qk_f[:, t * P:(t + 1) * P], const.ident[:, :])
                    ins.then_inc(s_tok, 1)
                    gate(1, 0, False)
                    gate(2, 0, False)
                    pe.wait_ge(s_sp, START + n + 1)
                    for a, m in enumerate((const.within, const.to_half, const.upto, const.before)):
                        ins = pe.matmul(ps[:, F, a * P:(a + 1) * P], m[:, :], sp[:, :, :].rearrange("p t d -> p (t d)"), start=True, stop=True)
                    for t in range(TB):
                        ins = pe.matmul(ps[0:DK, A, D_COL + t:D_COL + t + 1], sp[:, t, :], const.ones[:, 0:1], start=True, stop=True)
                    ins.then_inc(s_sum, 1)
                    gate(3, 0, False)

                    def transpose_feats(t):
                        i = TB * n + t
                        pe.wait_ge(s_ft, START + 5 * n + 5)
                        pe.wait_ge(s_dec, START + 2 * n + 2)
                        pe.wait_ge(s_fts, START + i)
                        for a in range(4):
                            ins = pe.transpose(ps[0:DK, F, a * P:(a + 1) * P], feats[:, a, t, :], const.ident[:, :])
                        ins.then_inc(s_ftt, 1)

                    def scores(t):
                        i = TB * n + t
                        f = ft[t % 2]
                        pe.wait_ge(s_dexp, START + n + 1)
                        pe.wait_ge(s_at, START + i)
                        pe.wait_ge(s_fts, START + i + 1)
                        pe.matmul(ps[:, A, 0:HALF], f[:, KA, :], f[:, QH, 0:HALF], start=True, stop=True)
                        pe.matmul(ps[:, A, HALF:P], f[:, KB, :], f[:, QH, HALF:P], start=True, stop=True).then_inc(s_a, 1)
                        pe.wait_ge(s_s, START + i + b + 1)
                        pe.matmul(ps[0:DK, S, :], k_end[:, t, :], x_in[:, t, :], start=True, stop=True).then_inc(s_su, 1)

                    def outputs(t):
                        i = TB * n + t
                        f = ft[t % 2]
                        pe.wait_ge(s_at, START + i + 1)
                        pe.wait_ge(s_of, START + i)
                        for m in range(KC):
                            o = ps[:, O, m * P:(m + 1) * P]
                            pe.matmul(o, x_in[:, t, m * P:(m + 1) * P], at[t % 2][:, :], start=True, stop=False)
                            ins = pe.matmul(o, state[:, m * P:(m + 1) * P], f[:, QT, :], start=False, stop=True)
                        ins.then_inc(s_o, 1)

                    def sum_squares(t):
                        i = TB * n + t
                        pe.wait_ge(s_sq, START + i + 1)
                        for m in range(KC):
                            ins = pe.matmul(ps[:, A, SS_COL + t:SS_COL + t + 1], sq[:, m, :], const.ones[:, 0:1],
                                            start=(m == 0), stop=(m == KC - 1))
                        ins.then_inc(s_ss, 1)

                    transpose_feats(0)
                    scores(0)
                    for t in range(TB):
                        if t + 1 < TB:
                            transpose_feats(t + 1)
                        outputs(t)
                        if t:
                            sum_squares(t - 1)
                        if t + 1 < TB:
                            scores(t + 1)
                    pe.wait_ge(s_wlp, START + 1)
                    pe.wait_ge(s_ol, START + TB * n + TB)
                    gate(0, 1, True).then_inc(s_go, 1)
                    sum_squares(TB - 1)
                    for m in range(1, KC):
                        gate(m, 1, True).then_inc(s_go, 1)
                    pe.wait_ge(s_x[1 - h], START + 16 * (b + 1 + h))
                    pe.wait_ge(s_sg, START + KC * n + KC)
                    transposes(xs[1 - h])
                    pe.wait_ge(s_ph, START + KC * n + KC)
                    pe.wait_ge(s_pl, START + KC * n + KC)
                    pe.wait_ge(s_ms, START + n + 1)
                    pe.wait_ge(s_of, START + TB * n + TB)
                    pe.wait_ge(s_s, START + TB * n + TB + b + 1)
                    pe.wait_ge(s_wlp, START + 2)
                    for t in range(TB):
                        for c in range(KC):
                            ins = three_products(pe, ps[:, t, :], p_hi[:, c, t * P:(t + 1) * P], p_lo[:, c, t * P:(t + 1) * P],
                                                 w_hi[WO][:, c, :], w_lo[WO][:, c, :], c == 0, c == KC - 1)
                        ins.then_inc(s_y, 1)


D_FF = 2048
FT = D_FF // P
TOP = T // 2
NT8 = T // P


def routed_feed_forward(nc, x3, score, router_b, w1, b1, w2, b2, pairs, out, const):
    ctx, sems = ExitStack(), []
    ctx.callback(clear_semaphores, nc, sems)
    with ctx:
        def sb(name, shape, dt=F32):
            return ctx.enter_context(nc.sbuf_tensor(name, shape, dt))

        def sem(name):
            sems.append(nc.alloc_semaphore(name))
            return sems[-1]

        def sem_of_pool_dma(name):
            pool_sems.append(nc.alloc_semaphore(name))
            return pool_sems[-1]

        pool_sems = []
        ctx.callback(clear_semaphores, nc, pool_sems)

        W1, W2 = 0, 1
        NW = D_FF // 256
        chunks = [(W1, 0), (W1, 1)]
        for i in range(NW):
            chunks += [(W2, i)] + ([(W1, i + 2)] if i + 2 < NW else [])
        NCH = len(chunks)
        EARLY = 10
        BY_POOL = 5
        SLOTS = 3
        HS = 3

        w1_hi = sb("w1_hi", [P, KC, D_FF], F32R)
        w1_lo = sb("w1_lo", [P, KC, D_FF], F32R)
        w2_hi = sb("w2_hi", [P, FT, C], F32R)
        w2_lo = sb("w2_lo", [P, FT, C], F32R)
        w_raw = [sb(f"mw_raw{i}", [P, 2, C]) for i in range(SLOTS)]
        b1_sb = sb("b1_sb", [P, FT])
        b2_sb = sb("b2_sb", [P, C])
        rb_sb = sb("rb_sb", [P, 1])
        pair = sb("pair", [P, NB * NT8, 2])
        base = sb("base", [P, NB])
        scores = [sb(f"scores{b}", [P, T]) for b in range(NB)]
        junk = sb("junk", [P, T])
        counts = sb("counts", [P, 3, NT8])
        rank = sb("rank", [P, NT8])
        row = [sb(f"row{b}", [P, NT8], I32) for b in range(NB)]
        sel = [sb(f"sel{b}", [P, TB, 2]) for b in range(NB)]
        xsel = [sb(f"xsel{b}", [P, TB, C]) for b in range(NB)]
        xt_hi = sb("mxt_hi", [P, KC, BLK], F32R)
        xt_lo = sb("mxt_lo", [P, KC, BLK], F32R)
        diag = xsel[1][:, :, :].rearrange("p t (a n) -> p (t a) n", n=P)
        h = [sb(f"mh{i}", [P, BLK]) for i in range(2)]
        h_hi = [sb(f"mh_hi{i}", [P, BLK], F32R) for i in range(HS)]
        h_lo = [sb(f"mh_lo{i}", [P, BLK], F32R) for i in range(HS)]
        st = sb("mst", [P, TB, 6])
        mv = sb("mmv", [P, TB, 2])
        var = sb("mvar", [P, TB])
        rstd = sb("mrstd", [P, TB])
        p_st = sb("p_st", [P, 2, 6])
        p_mv = [sb(f"p_mv{i}", [P, 2, 2]) for i in range(2)]
        p_var = [sb(f"p_var{i}", [P, 2]) for i in range(2)]
        p_rstd = [sb(f"p_rstd{i}", [P, 2]) for i in range(2)]
        filler = sb("mfiller", [P, 1])

        ps = ctx.enter_context(nc.psum_tensor("ps_moe", [P, 8, 512], F32))
        Y, H = 0, 4

        s_rb = sem("router_bias_loaded")
        s_c = sem("biases_loaded")
        s_w = [sem(f"mw_loaded{i}") for i in range(SLOTS)]
        s_wh = sem("mw_hi_done")
        s_wlp = sem("mw_lo_done_by_pool")
        s_wld = sem("mw_lo_done_by_dve")
        s_id = sem("ids_ready")
        s_sc = sem("score_ready")
        s_sig = sem("weight_ready")
        s_diag = sem("score_diagonals_ready")
        s_bc = sem("scores_broadcast")
        s_sb = sem("scores_taken")
        s_cnt = sem("counted")
        s_rk = sem("rank_ready")
        s_row = sem("row_ready")
        s_pst = sem("plain_stats_done")
        s_pag = sem("plain_aggregated")
        s_pvar = sem("plain_var_ready")
        s_prstd = sem("plain_rstd_ready")
        s_px = [sem(f"plain_loaded{i}") for i in range(SLOTS)]
        s_pout = sem("plain_rows_ready")
        s_all = sem("plain_rows_stored")
        s_tp = sem("mx_transposed")
        s_xth = sem("mxt_hi_done")
        s_xtl = sem("mxt_lo_done")
        s_h1 = sem("mh_projected")
        s_g = sem("gelu_done")
        s_hh = sem("mh_hi_done")
        s_hl = sem("mh_lo_done")
        s_y = sem("my_added")
        s_b2 = sem("b2_weighted")
        s_r = sem("mresidual_added")
        s_st = sem("mstats_done")
        s_ag = sem("maggregated")
        s_var = sem("mvar_ready")
        s_rstd = sem("mrstd_ready")
        s_out = sem("mx_out_ready")
        s_scat = sem_of_pool_dma("pairs_scattered")
        s_pr = sem_of_pool_dma("selected_pairs_loaded")
        s_sel = sem_of_pool_dma("selected_gathered")
        s_fin = sem_of_pool_dma("selected_stored")

        start_semaphores(nc, sems)
        block = ctx.enter_context(nc.Block())

        NPL = NB * NT8 // 2

        def halves(n):
            kind, i = chunks[n]
            if kind == W1:
                return [w[:, :, 256 * i:256 * (i + 1)] for w in (w1_hi, w1_lo)]
            return [w[:, 2 * i:2 * i + 2, :] for w in (w2_hi, w2_lo)]

        def raw(n):
            w = w_raw[n % SLOTS][:, :, :]
            return w.rearrange("p a (k n) -> p (a k) n", n=256) if chunks[n][0] == W1 else w

        def lower_done(engine, n):
            if n < BY_POOL:
                engine.wait_ge(s_wlp, START + n + 1)
            else:
                engine.wait_ge(s_wld, START + n - BY_POOL + 1)

        def lower_half(engine, n):
            hi, lo = halves(n)
            engine.wait_ge(s_wh, START + n + 1)
            engine.tensor_tensor(lo, raw(n), hi.bitcast(F32), ALU.subtract).then_inc(s_wlp if n < BY_POOL else s_wld, 1)

        @block.sync
        def _(sp):
            sp.dma_start(rb_sb[:, :], router_b.to_broadcast([P, 1])).then_inc(s_rb, 16)
            for n in range(NCH):
                kind, i = chunks[n]
                if n >= SLOTS:
                    lower_done(sp, n - SLOTS)
                sp.dma_start(raw(n), w1[:, :, 256 * i:256 * (i + 1)] if kind == W1 else w2[:, 2 * i:2 * i + 2, :]).then_inc(s_w[n % SLOTS], 16)
                if n == 1:
                    sp.dma_start(b2_sb[:, :], b2.to_broadcast([P, C])).then_inc(s_c, 16)
                    sp.dma_start(b1_sb[:, :], b1).then_inc(s_c, 16)
            for k in range(NPL + 1):
                if k < NPL:
                    if k < SLOTS:
                        for n in range(NCH - SLOTS, NCH):
                            if n % SLOTS == k:
                                lower_done(sp, n)
                    else:
                        sp.wait_ge(s_all, START + 16 * (k - SLOTS + 1))
                    sp.dma_start(w_raw[k % SLOTS][:, :, :], x3[2 * k:2 * k + 2, :, :].rearrange("t p c -> p t c")).then_inc(s_px[k % SLOTS], 16)
                if k >= 1:
                    sp.wait_ge(s_pout, START + 2 * k)
                    sp.dma_start(out[2 * k - 2:2 * k, :, :].rearrange("t p c -> p t c"), w_raw[(k - 1) % SLOTS][:, :, :]).then_inc(s_all, 16)
            sp.wait_ge(s_all, START + 16 * NPL)

        @block.scalar
        def _(act):
            def upper_half(n):
                act.wait_ge(s_w[n % SLOTS], START + 16 * (n // SLOTS + 1))
                act.activation(halves(n)[0], raw(n), ACT.Copy).then_inc(s_wh, 1)

            act.wait_ge(s_sc, START + 1)
            act.activation(pair[:, :, 1], score, ACT.Sigmoid).then_inc(s_sig, 1)
            for b in range(NB):
                act.wait_ge(s_bc, START + b + 1)
                act.activation(scores[b][:, :].rearrange("p (a n) -> p a n", a=2), ps[:, H + 2 * b:H + 2 * b + 2, :], ACT.Copy).then_inc(s_sb, 1)
            for n in range(EARLY):
                upper_half(n)
            act.wait_ge(s_c, START + 32)
            late = list(range(EARLY, NCH))
            for b in range(NB):
                for c in range(KC):
                    act.wait_ge(s_tp, START + KC * b + c + 1)
                    act.activation(xt_hi[:, c, :], ps[:, H + c, :], ACT.Copy).then_inc(s_xth, 1)
                for j in range(FT + 1):
                    if j < FT:
                        act.wait_ge(s_h1, START + FT * b + j + 1)
                        act.wait_ge(s_hl, START + FT * b + max(0, j - 1))
                        act.activation(h[j % 2][:, :], ps[:, H + j % 4, :], ACT.Gelu_apprx_tanh, bias=b1_sb[:, j:j + 1]).then_inc(s_g, 1)
                        act.wait_ge(s_g, START + FT * b + j + 1)
                        act.wait_ge(s_y, START + FT * b + max(0, j - HS + 1))
                        act.activation(h_hi[j % HS][:, :], h[j % 2][:, :], ACT.Copy).then_inc(s_hh, 1)
                    for n in late[0:2]:
                        upper_half(n)
                    late = late[2:]

        @block.vector
        def _(dve):
            def ranks(b):
                k = (3 * NT8 - 1) * b
                for t in range(NT8):
                    s_t = score[:, NT8 * b + t:NT8 * b + t + 1]
                    todo = [(0, t * P, ALU.is_ge), (t * P, T, ALU.is_gt)] if t else [(0, T, ALU.is_gt)]
                    for a, (lo, hi, op) in enumerate(todo):
                        dve.tensor_scalar(junk[:, 0:hi - lo], scores[b][:, lo:hi], s_t, None, op, ALU.add,
                                          accum_out=counts[:, 1 - a if t else 0, t:t + 1]).then_inc(s_cnt, 1)
                        k += 1
                        dve.wait_ge(s_cnt, START + k)
                    dve.scalar_tensor_tensor(out=junk[:, 0:P], in0=scores[b][:, t * P:(t + 1) * P], scalar=s_t, in1=const.before[:, :],
                                             op0=ALU.is_equal, op1=ALU.mult, accum_out=counts[:, 2, t:t + 1]).then_inc(s_cnt, 1)
                    k += 1
                    dve.wait_ge(s_cnt, START + k)
                dve.tensor_tensor(rank[:, :], counts[:, 0, :], counts[:, 2, :], ALU.add).then_inc(s_rk, 1)
                dve.wait_ge(s_rk, START + 2 * b + 1)
                dve.tensor_tensor(rank[:, 1:NT8], rank[:, 1:NT8], counts[:, 1, 1:NT8], ALU.add).then_inc(s_rk, 1)
                dve.wait_ge(s_rk, START + 2 * b + 2)
                dve.tensor_tensor(row[b][:, :], rank[:, :], base[:, b:b + 1].to_broadcast([P, NT8]), ALU.add).then_inc(s_row, 1)

            def x_low(b):
                for c in range(KC):
                    dve.wait_ge(s_xth, START + KC * b + c + 1)
                    dve.tensor_tensor(xt_lo[:, c, :], ps[:, H + c, :], xt_hi[:, c, :].bitcast(F32), ALU.subtract).then_inc(s_xtl, 1)

            def plain_statistics(k):
                dve.wait_ge(s_px[k % SLOTS], START + 16 * (k // SLOTS + 1))
                dve.wait_ge(s_pag, START + 2 * k)
                dve.memset(filler[:, :], 0.0)
                for t in range(2):
                    dve.bn_stats(p_st[:, t, :], w_raw[k % SLOTS][:, t, :]).then_inc(s_pst, 1)
                dve.wait_ge(s_pst, START + 2 * k + 2)
                dve.memset(filler[:, :], 0.0)
                for t in range(2):
                    dve.bn_aggr(p_mv[k % 2][:, t, :], p_st[:, t, :]).then_inc(s_pag, 1)
                dve.wait_ge(s_pag, START + 2 * k + 2)
                dve.tensor_scalar(p_var[k % 2][:, :], p_mv[k % 2][:, :, 1], LN_EPS / 4, None, ALU.add).then_inc(s_pvar, 1)

            def plain_normalise(k):
                dve.wait_ge(s_prstd, START + k + 1)
                w = w_raw[k % SLOTS]
                for t in range(2):
                    dve.tensor_scalar(w[:, t, :], w[:, t, :], p_mv[k % 2][:, t, 0:1], p_rstd[k % 2][:, t:t + 1], ALU.subtract,
                                      ALU.mult).then_inc(s_pout, 1)

            def residual(b):
                dve.wait_ge(s_tp, START + KC * b + KC)
                for t in range(TB):
                    dve.tensor_scalar(xsel[b][:, t, :], xsel[b][:, t, :], 2.0, None, ALU.mult).then_inc(s_b2, 1)
                for t in range(TB):
                    dve.wait_ge(s_b2, START + 2 * TB * b + t + 1)
                    dve.scalar_tensor_tensor(out=xsel[b][:, t, :], in0=b2_sb[:, :], scalar=sel[b][:, t, 1:2], in1=xsel[b][:, t, :],
                                             op0=ALU.mult, op1=ALU.add).then_inc(s_b2, 1)

            def add_outputs(b):
                dve.wait_ge(s_y, START + FT * b + FT)
                for t in range(TB):
                    dve.wait_ge(s_b2, START + 2 * TB * b + TB + t + 1)
                    dve.scalar_tensor_tensor(out=xsel[b][:, t, :], in0=ps[:, Y + t, :], scalar=sel[b][:, t, 1:2], in1=xsel[b][:, t, :],
                                             op0=ALU.mult, op1=ALU.add).then_inc(s_r, 1)

            dve.wait_ge(s_rb, START + 16)
            dve.tensor_scalar(score, score, rb_sb[:, 0:1], None, ALU.add).then_inc(s_sc, 1)
            dve.wait_ge(s_sc, START + 1)
            dve.tensor_tensor(diag, const.ident[:, :].unsqueeze(1).to_broadcast([P, NB * NT8, P]),
                              score.unsqueeze(2).to_broadcast([P, NB * NT8, P]), ALU.mult).then_inc(s_diag, 1)
            dve.wait_ge(s_sb, START + 1)
            dve.wait_ge(s_id, START + 2)
            ranks(0)
            for n in range(BY_POOL, EARLY):
                lower_half(dve, n)
            x_low(0)
            for n in range(EARLY, NCH):
                lower_half(dve, n)
            dve.wait_ge(s_sb, START + 2)
            ranks(1)
            dve.wait_ge(s_c, START + 32)
            for k in range(NPL + 1):
                if k < NPL:
                    plain_statistics(k)
                if k >= 1:
                    plain_normalise(k - 1)
            for b in range(NB):
                residual(b)
                if b + 1 < NB:
                    x_low(b + 1)
                add_outputs(b)
                layer_norm_block(dve, b, xsel[b], st, mv, var, rstd, filler, s_r, s_st, s_ag, s_var, s_rstd, s_out)

        @block.gpsimd
        def _(pool):
            def scatter_pairs(b, t):
                pool.indirect_dma_start(pairs, bass.IndirectOffsetOnAxis(ap=row[b][:, t:t + 1], axis=0),
                                        pair[:, NT8 * b + t, :], None).then_inc(s_scat, 16)

            def load_selected(b):
                pool.wait_ge(s_scat, 16 * NT8 * (b + 1))
                pool.dma_start(sel[b][:, :, :], pairs[T * b:T * b + TOP, :].rearrange("(t p) c -> p t c", p=P)).then_inc(s_pr, 16)

            def gather(b, t):
                pool.indirect_dma_start(xsel[b][:, t, :], None, x3.rearrange("n p c -> (n p) c"),
                                        bass.IndirectOffsetOnAxis(ap=sel[b][:, t, 0:1].bitcast(I32), axis=0)).then_inc(s_sel, 16)

            def store_selected(b, t):
                pool.indirect_dma_start(out.rearrange("n p c -> (n p) c"), bass.IndirectOffsetOnAxis(ap=sel[b][:, t, 0:1].bitcast(I32), axis=0),
                                        xsel[b][:, t, :], None).then_inc(s_fin, 16)

            def plain_rstd(k):
                pool.wait_ge(s_pvar, START + k + 1)
                pool.tensor_tensor(p_rstd[k % 2][:, :], p_var[k % 2][:, :], const.minus_half[:, 0:2], ALU.pow).then_inc(s_prstd, 1)

            def selected_rstd(b):
                pool.wait_ge(s_var, START + b + 1)
                pool.tensor_tensor(rstd[:, :], var[:, :], const.minus_half[:, :], ALU.pow).then_inc(s_rstd, 1)

            def between(b, j):
                if b == 0:
                    if j == ROUTE:
                        pool.wait_ge(s_row, START + 2)
                    if ROUTE <= j < ROUTE + 4:
                        scatter_pairs(1, 2 * (j - ROUTE))
                        scatter_pairs(1, 2 * (j - ROUTE) + 1)
                    if j == ROUTE + 4:
                        load_selected(1)
                    if j == ROUTE + 5:
                        pool.wait_ge(s_pr, 32)
                    if ROUTE + 5 <= j < ROUTE + 7:
                        gather(1, 2 * (j - ROUTE - 5))
                        gather(1, 2 * (j - ROUTE - 5) + 1)
                    if ROUTE <= j < ROUTE + NPL:
                        plain_rstd(j - ROUTE)
                else:
                    if j == 2:
                        selected_rstd(0)
                    if j == 4:
                        pool.wait_ge(s_out, START + TB)
                        pool.wait_ge(s_all, START + 16 * NPL)
                    if 4 <= j < 4 + TB:
                        store_selected(0, j - 4)

            ROUTE = 7
            pool.iota(pair[:, :, 0].bitcast(I32), pattern=[[P, NB * NT8]], base=0, channel_multiplier=1).then_inc(s_id, 1)
            pool.iota(base[:, :], pattern=[[T, NB]], base=0, channel_multiplier=0,
                      allow_small_or_imprecise_dtypes=True).then_inc(s_id, 1)
            for n in range(BY_POOL):
                lower_half(pool, n)
            pool.wait_ge(s_sig, START + 1)
            pool.wait_ge(s_id, START + 2)
            pool.wait_ge(s_row, START + 1)
            for t in range(NT8):
                scatter_pairs(0, t)
            load_selected(0)
            pool.wait_ge(s_pr, 16)
            for t in range(TB):
                gather(0, t)
            for b in range(NB):
                for j in range(FT):
                    pool.wait_ge(s_hh, START + FT * b + j + 1)
                    pool.wait_ge(s_y, START + FT * b + max(0, j - HS + 1))
                    pool.tensor_tensor(h_lo[j % HS][:, :], h[j % 2][:, :], h_hi[j % HS][:, :].bitcast(F32), ALU.subtract).then_inc(s_hl, 1)
                    between(b, j)
            selected_rstd(1)
            pool.wait_ge(s_out, START + 2 * TB)
            for t in range(TB):
                store_selected(1, t)
            pool.wait_ge(s_fin, 16 * TB * NB)

        @block.tensor
        def _(pe):
            def transposes(b):
                pe.wait_ge(s_sel, 16 * TB * (b + 1))
                for c in range(KC):
                    pe.wait_ge(s_g, START + FT * b - KC * min(b, 1) + (c + 1) * min(b, 1))
                    for t in range(TB):
                        ins = pe.transpose(ps[:, H + c, t * P:(t + 1) * P], xsel[b][:, t, c * P:(c + 1) * P], const.ident[:, :])
                    ins.then_inc(s_tp, 1)

            def up(b, j):
                if j < 4:
                    pe.wait_ge(s_xtl, START + KC * b + KC)
                else:
                    pe.wait_ge(s_g, START + FT * b + j - 3)
                if b == 0:
                    lower_done(pe, chunks.index((W1, j // 2)))
                for c in range(KC):
                    ins = three_products(pe, ps[:, H + j % 4, :], w1_hi[:, c, j * P:(j + 1) * P], w1_lo[:, c, j * P:(j + 1) * P],
                                         xt_hi[:, c, :], xt_lo[:, c, :], c == 0, c == KC - 1)
                ins.then_inc(s_h1, 1)

            def down(b, j):
                pe.wait_ge(s_hh, START + FT * b + j + 1)
                pe.wait_ge(s_hl, START + FT * b + j + 1)
                if b == 0:
                    lower_done(pe, chunks.index((W2, j // 2)))
                for t in range(TB):
                    if j == 0 and b:
                        pe.wait_ge(s_r, START + TB * (b - 1) + t + 1)
                    ins = three_products(pe, ps[:, Y + t, :], h_hi[j % HS][:, t * P:(t + 1) * P], h_lo[j % HS][:, t * P:(t + 1) * P],
                                         w2_hi[:, j, :], w2_lo[:, j, :], j == 0, j == FT - 1)
                ins.then_inc(s_y, 1)

            pe.wait_ge(s_diag, START + 1)
            for b in range(NB):
                for a in range(2):
                    ins = pe.matmul(ps[:, H + 2 * b + a, :], const.ones[:, :],
                                    diag[:, NT8 * b + 4 * a:NT8 * b + 4 * a + 4, :].rearrange("p a n -> p (a n)"), start=True, stop=True)
                ins.then_inc(s_bc, 1)
            pe.wait_ge(s_sb, START + NB)
            transposes(0)
            for b in range(NB):
                up(b, 0)
                up(b, 1)
                for j in range(2, FT):
                    up(b, j)
                    down(b, j - 2)
                down(b, FT - 2)
                if b + 1 < NB:
                    transposes(b + 1)
                down(b, FT - 1)


def transformer_two_layers(nc, x, xT, wqT, wkT, wvT, woT, gu_packed, gu_scales, dn_packed, dn_scales,
                           wqkT, wogT, wigT, wo1T, norm_w, router_w, router_b, w1, b1, w2, b2, out):
    def tiles(a):
        return a.rearrange("(n p) c -> n p c", p=P)

    def contracted(a):
        return a.rearrange("(k p) n -> p k n", p=P)

    x1, x2, x3 = (tiles(nc.dram_tensor(name, [NB * T, C], F32).ap()) for name in ("x1", "x2", "x3"))
    pairs = nc.dram_tensor("routed_pairs", [NB * T, 2], F32).ap()
    with ExitStack() as ctx:
        const = Constants(nc, ctx)
        score = ctx.enter_context(nc.sbuf_tensor("score", [P, TB + NB * NT8], F32))
        linear_attention(nc, tiles(x), contracted(xT), [contracted(wkT), contracted(wvT), contracted(wqT)],
                         contracted(woT), x1, const)
        fp4_feed_forward(nc, x1, gu_packed.rearrange("(k w) o -> w k o", w=P // NIB), gu_scales, dn_packed, dn_scales,
                         x2, const)
        gated_linear_attention(nc, x2, contracted(wqkT), contracted(wogT), contracted(wigT), contracted(wo1T), norm_w,
                               router_w, x3, score, const)
        routed_feed_forward(nc, x3, score[:, TB:TB + NB * NT8], router_b, contracted(w1), b1, contracted(w2), b2, pairs, tiles(out), const)


def kernel(**inputs):
    import numpy as np
    import concourse.bacc as bacc
    from concourse.bass_utils import run_bass_kernel_spmd

    a = {name: np.asarray(value) for name, value in inputs.items()}
    x = a["L0_attn_x"].reshape(NB * T, C)
    laid_out = {
        "x": x,
        "xT": x.T,
        "wqT": a["L0_attn_Wq"].T,
        "wkT": a["L0_attn_Wk"].T,
        "wvT": a["L0_attn_Wv"].T,
        "woT": a["L0_attn_Wo"].T,
        "gate_up_packed": a["L0_ffn_gate_up_packed"].T,
        "gate_up_scales": a["L0_ffn_gate_up_scales"].reshape(KC, 2 * IT, P).transpose(2, 1, 0),
        "down_packed": a["L0_ffn_down_packed"].T,
        "down_scales": a["L0_ffn_down_scales"],
        "gla_wqkT": np.concatenate([a["L1_attn_Wq"], a["L1_attn_Wk"]]).T,
        "gla_wogT": a["L1_attn_Wog"].T,
        "gla_wigT": a["L1_attn_Wig"].T,
        "gla_woT": a["L1_attn_Wo"].T,
        "gla_norm_w": a["L1_attn_g_norm_w"].reshape(KC, P).T,
        "router_w": a["L1_ffn_router_weight"].reshape(1, C),
        "router_b": a["L1_ffn_router_bias"].reshape(1, 1),
        "w1": a["L1_ffn_w1"],
        "b1": a["L1_ffn_b1"].reshape(FT, P).T,
        "w2": a["L1_ffn_w2"],
        "b2": a["L1_ffn_b2"].reshape(1, C),
    }
    nc = bacc.Bacc("TRN2", target_bir_lowering=False, num_devices=1)
    arrays, args = {}, []
    for name, value in laid_out.items():
        arrays[f"in_{name}"] = np.ascontiguousarray(value)
        args.append(nc.dram_tensor(f"in_{name}", value.shape, mybir.dt.from_np(value.dtype), kind="ExternalInput").ap())
    args.append(nc.dram_tensor("out", (NB * T, C), F32, kind="ExternalOutput").ap())
    transformer_two_layers(nc, *args)
    result = run_bass_kernel_spmd(nc, [arrays], core_ids=[0])
    return result.results[0]["out"].reshape(NB, T, C)
```

```python
from contextlib import ExitStack

import concourse.bass as bass
from concourse import mybir

F32 = mybir.dt.float32
F32R = mybir.dt.float32r
F16 = mybir.dt.float16
I32 = mybir.dt.int32
U16 = mybir.dt.uint16
ALU = mybir.AluOpType
ACT = mybir.ActivationFunctionType
AX = mybir.AxisListType
ds = bass.ds

P = 128
NB = 2
T = 1024
C = 512
KC = C // P
BLK = 512
TB = BLK // P
NBLK = NB * T // BLK
HEADS = 16
DH = C // HEADS
HG = P // DH
LN_EPS = 1e-5
START = 1


class Steps:

    def __init__(self, engine, sem, per_turn):
        self.engine, self.sem, self.per_turn = engine, sem, per_turn

    def turn(self, it):
        self.base, self.k = it * self.per_turn, 0

    def done(self, ins):
        ins.then_inc(self.sem, 1)
        self.k += 1
        self.engine.wait_ge(self.sem, START + self.base + self.k)

    def end(self):
        assert self.k == self.per_turn, (self.k, self.per_turn)


def three_products(pe, out, lh, ll, rh, rl, first, last):
    pe.matmul(out, lh, rh, start=first, stop=False)
    pe.matmul(out, ll, rh, start=False, stop=False)
    return pe.matmul(out, lh, rl, start=False, stop=last)


def layer_norm_block(dve, n, r, st, mv, var, rstd, filler, s_r, s_st, s_ag, s_var, s_rstd, s_out):
    for t in range(TB):
        dve.wait_ge(s_r, START + TB * n + t + 1)
        dve.bn_stats(st[:, t, :], r[:, t, :]).then_inc(s_st, 1)
    dve.wait_ge(s_st, START + TB * n + TB)
    dve.memset(filler[:, :], 0.0)
    for t in range(TB):
        dve.bn_aggr(mv[:, t, :], st[:, t, :]).then_inc(s_ag, 1)
    dve.wait_ge(s_ag, START + TB * n + TB)
    dve.tensor_scalar(var[:, :], mv[:, :, 1], LN_EPS, None, ALU.add).then_inc(s_var, 1)
    dve.wait_ge(s_rstd, START + n + 1)
    for t in range(TB):
        dve.tensor_scalar(r[:, t, :], r[:, t, :], mv[:, t, 0:1], rstd[:, t:t + 1], ALU.subtract,
                          ALU.mult).then_inc(s_out, 1)


def start_semaphores(nc, sems):
    engines = [nc.gpsimd, nc.vector, nc.scalar, nc.tensor, nc.sync]
    for i, sem in enumerate(sems):
        engines[i % len(engines)].nop().then_inc(sem, START)
    nc.all_engine_barrier()


def clear_semaphores(nc, sems):
    nc.clear_and_free_semaphores(sems)
    nc.all_engine_barrier()


class Constants:

    def __init__(self, nc, ctx):
        def sb(name, shape, dt=F32):
            return ctx.enter_context(nc.sbuf_tensor(name, shape, dt))

        self.ident = sb("ident", [P, P])
        self.ones = sb("ones", [P, P])
        self.before = sb("before", [P, P])
        self.head_mask = sb("head_mask", [P, P])
        self.upto = sb("upto", [P, P])
        self.within = sb("within", [P, P])
        self.to_half = sb("to_half", [P, P])
        self.minus_half = sb("minus_half", [P, TB])
        self.steps = ctx.enter_context(nc.semaphore("const_steps"))
        self.ready = ctx.enter_context(nc.semaphore("const_ready"))

    def make(self, pool):
        k = 0

        def done(ins):
            nonlocal k
            k += 1
            ins.then_inc(self.steps, 1)
            pool.wait_ge(self.steps, k)

        h = P // 2
        pool.memset(self.minus_half[:, :], -0.5)
        pool.memset(self.ones[:, :], 1.0)
        pool.memset(self.to_half[:, :], 0.0)
        done(pool.memset(self.head_mask[:, :], 1.0))
        pool.affine_select(out=self.ident[:, :], in_=self.ones[:, :], compare_op=ALU.is_equal, fill=0.0,
                           base=0, pattern=[[-1, P]], channel_multiplier=1)
        pool.affine_select(out=self.before[:, :], in_=self.ones[:, :], compare_op=ALU.is_gt, fill=0.0,
                           base=0, pattern=[[-1, P]], channel_multiplier=1)
        for m in (self.within, self.upto):
            ins = pool.affine_select(out=m[:, :], in_=self.ones[:, :], compare_op=ALU.is_ge, fill=0.0,
                                     base=0, pattern=[[1, P]], channel_multiplier=-1)
        done(ins)
        done(pool.memset(self.within[0:h, h:P], 0.0))
        done(pool.tensor_copy(self.to_half[0:h, 0:h], self.before[0:h, 0:h]))
        done(pool.tensor_scalar(self.to_half[h:P, h:P], self.upto[h:P, h:P], -1.0, None, ALU.mult))
        v = self.head_mask[:, :].rearrange("p (h e) -> p h e", e=DH)
        done(pool.affine_select(out=v, in_=v, compare_op=ALU.is_ge, fill=0.0, base=0,
                                pattern=[[-DH, HG], [0, DH]], channel_multiplier=1))
        pool.affine_select(out=v, in_=v, compare_op=ALU.is_ge, fill=0.0, base=DH - 1,
                           pattern=[[DH, HG], [0, DH]], channel_multiplier=-1).then_inc(self.ready, 1)


def linear_attention(nc, x, xT, wT, woT, x1, const):
    ctx, sems = ExitStack(), []
    ctx.callback(clear_semaphores, nc, sems)
    with ctx:
        def sb(name, shape, dt=F32):
            return ctx.enter_context(nc.sbuf_tensor(name, shape, dt))

        def sem(name):
            sems.append(nc.alloc_semaphore(name))
            return sems[-1]

        NW = 4
        NT = T // P
        w_raw = [sb(f"w_raw{i}", [P, KC, C]) for i in range(2)]
        w_hi = [sb(f"w_hi{i}", [P, KC, C], F32R) for i in range(NW)]
        w_lo = [sb(f"w_lo{i}", [P, KC, C], F32R) for i in range(NW)]
        xt_raw = [sb(f"xt_raw{i}", [P, KC, BLK]) for i in range(2)]
        xt_hi = [sb(f"xt_hi{i}", [P, KC, BLK], F32R) for i in range(2)]
        xt_lo = [sb(f"xt_lo{i}", [P, KC, BLK], F32R) for i in range(2)]
        q = [sb(f"q{i}", [P, KC, BLK]) for i in range(2)]
        k = [sb(f"k{i}", [P, C]) for i in range(2)]
        v1 = [sb(f"v1_{i}", [P, KC, P + 1]) for i in range(2)]
        e_k = sb("e_k", [P, C])
        e_q = sb("e_q", [P, C])
        kvz = sb("kvz", [P, KC, P + HG])
        z = sb("z", [P, HEADS])
        zi = [sb(f"zi{i}", [P, HEADS]) for i in range(2)]
        att = [sb(f"att{i}", [P, C]) for i in range(2)]
        at_hi = [sb(f"at_hi{i}", [P, KC, P], F32R) for i in range(2)]
        at_lo = [sb(f"at_lo{i}", [P, KC, P], F32R) for i in range(2)]
        x_res = [sb(f"x_res{i}", [P, C]) for i in range(4)]
        r = [sb(f"r{i}", [P, C]) for i in range(3)]
        x_out = [sb(f"x_out{i}", [P, C]) for i in range(2)]
        st = [sb(f"st{i}", [P, 6]) for i in range(3)]
        mv = [sb(f"mv{i}", [P, 2]) for i in range(3)]
        filler = sb("filler", [P, 1])
        var = [sb(f"var{i}", [P, 1]) for i in range(2)]
        rstd = [sb(f"rstd{i}", [P, 1]) for i in range(2)]

        ps = ctx.enter_context(nc.psum_tensor("ps_attn", [P, 8, 512], F32))
        KV0, PROJ, QP, TP, YP = 0, 2, 6, 6, 0

        s_kv_w = [[sem(f"{name}_loaded{c}") for c in range(KC)] for name in ("wk", "wv")]
        s_kv_wh = [sem(f"{name}_hi_done") for name in ("wk", "wv")]
        s_kv_wl = [sem(f"{name}_lo_done") for name in ("wk", "wv")]
        s_x0 = [sem(f"first_xt_loaded{c}") for c in range(KC)]
        s_x0h = sem("first_xt_hi_done")
        s_x0l = sem("first_xt_lo_done")
        s_w = [sem(f"{name}_loaded") for name in ("wq", "wo")]
        s_wh = sem("w_hi_done")
        s_wl = sem("w_lo_done")
        s_xt = [sem(f"xt_loaded{i}") for i in range(2)]
        s_xth = sem("xt_hi_done")
        s_xtl = sem("xt_lo_done")
        s_proj = sem("k_v_projected")
        s_ek = sem("k_exp_done")
        s_k = sem("k_ready")
        s_v = sem("v_ready")
        s_ones = sem("ones_ready")
        s_kvt = sem("kv_tile_added")
        s_q = sem("q_projected")
        s_eq = sem("q_exp_done")
        s_qr = sem("q_ready")
        s_kv = sem("kv_masked")
        s_num = sem("num_done")
        s_att = sem("att_ready")
        s_tp = sem("att_transposed")
        s_ath = sem("att_hi_done")
        s_atl = sem("att_lo_done")
        s_y = sem("out_projected")
        s_xr = [sem(f"x_res_loaded{i}") for i in range(4)]
        s_r = sem("residual_added")
        s_var = sem("var_ready")
        s_rstd = sem("rstd_ready")
        s_out = sem("x_out_ready")
        s_st = [sem(f"x_out_stored{i}") for i in range(2)]
        s_dve = sem("dve_step_attn")

        start_semaphores(nc, sems)
        block = ctx.enter_context(nc.Block())

        @block.sync
        def _(sp):
            for c in range(KC):
                sp.dma_start(xt_raw[0][:, c, :], xT[:, c, 0:BLK]).then_inc(s_x0[c], 16)
                sp.dma_start(w_raw[0][:, c, :], wT[0][:, c, :]).then_inc(s_kv_w[0][c], 16)
            for c in range(KC):
                sp.dma_start(w_raw[1][:, c, :], wT[1][:, c, :]).then_inc(s_kv_w[1][c], 16)
            sp.dma_start(xt_raw[1][:, :, :], xT[:, :, BLK:2 * BLK]).then_inc(s_xt[1], 16)
            sp.wait_ge(s_kv_wl[0], START + KC)
            sp.dma_start(w_raw[0][:, :, :], wT[2]).then_inc(s_w[0], 16)
            sp.wait_ge(s_kv_wl[1], START + KC)
            sp.dma_start(w_raw[1][:, :, :], woT).then_inc(s_w[1], 16)
            with sp.Fori(0, NB) as b:
                for h in range(2):
                    if h == 0:
                        sp.wait_ge(s_x0l, START + KC)
                    sp.wait_ge(s_xth, START + 2 * b + h)
                    sp.wait_ge(s_xtl, START + 2 * b + h)
                    sp.dma_start(xt_raw[h][:, :, :], xT[:, :, ds((b * 2 + h + 2) % (NB * 2) * BLK, BLK)]).then_inc(s_xt[h], 16)
                for t in range(NT + 3):
                    if t < NT:
                        sp.wait_ge(s_r, START + b * NT + max(0, t - 3))
                        sp.dma_start(x_res[t % 4][:, :], x[b * NT + t, :, :]).then_inc(s_xr[t % 4], 16)
                    if t >= 3:
                        u = t - 3
                        sp.wait_ge(s_out, START + NT * b + u + 1)
                        sp.dma_start(x1[b * NT + u, :, :], x_out[u % 2][:, :]).then_inc(s_st[u % 2], 16)
            for i in range(2):
                sp.wait_ge(s_st[i], START + 16 * NB * NT // 2)

        @block.scalar
        def _(act):
            for c in range(KC):
                act.wait_ge(s_x0[c], START + 16)
                act.activation(xt_hi[0][:, c, :], xt_raw[0][:, c, :], ACT.Copy).then_inc(s_x0h, 1)
                act.wait_ge(s_kv_w[0][c], START + 16)
                act.activation(w_hi[0][:, c, :], w_raw[0][:, c, :], ACT.Copy).then_inc(s_kv_wh[0], 1)
            for c in range(KC):
                act.wait_ge(s_kv_w[1][c], START + 16)
                act.activation(w_hi[1][:, c, :], w_raw[1][:, c, :], ACT.Copy).then_inc(s_kv_wh[1], 1)
            with act.Fori(0, NB) as b:
                for h in range(2):
                    for t in range(TB):
                        n = TB * h + t
                        act.wait_ge(s_proj, START + NT * b + n + 1)
                        act.wait_ge(s_k, START + NT * b + n)
                        act.activation(e_k[:, :], ps[:, PROJ + 2 * (n % 2), :], ACT.Exp).then_inc(s_ek, 1)
                        act.wait_ge(s_kvt, START + NT * b + max(0, n - 1))
                        act.wait_ge(s_ones, START + 2)
                        act.activation(v1[n % 2][:, :, 0:P], ps[:, PROJ + 2 * (n % 2) + 1, :].rearrange("p (g e) -> p g e", g=KC),
                                       ACT.Copy).then_inc(s_v, 1)
                        if t == 1:
                            if h == 0:
                                act.wait_ge(s_xt[1], START + 16 * (b + 1))
                            else:
                                act.wait_ge(s_xt[0], START + 16 * (b + 1))
                            act.wait_ge(s_q, START + 8 * b + 4 * h)
                            act.activation(xt_hi[1 - h][:, :, :], xt_raw[1 - h][:, :, :], ACT.Copy).then_inc(s_xth, 1)
                    for m in range(KC):
                        act.wait_ge(s_q, START + 8 * b + 4 * h + m + 1)
                        act.wait_ge(s_qr, START + 8 * b + 4 * h + m)
                        act.activation(e_q[:, :], ps[:, QP + m % 2, :], ACT.Exp).then_inc(s_eq, 1)
                for t in range(NT):
                    act.wait_ge(s_tp, START + NT * b + t + 1)
                    act.wait_ge(s_y, START + NT * b + max(0, t - 1))
                    act.activation(at_hi[t % 2][:, :, :], ps[:, TP + t % 2, :].rearrange("p (k n) -> p k n", k=KC),
                                   ACT.Copy).then_inc(s_ath, 1)

        @block.vector
        def _(dve):
            steps = Steps(dve, s_dve, NT + 2 * KC + 4 * NT)

            def normalise(u, b):
                dve.wait_ge(s_rstd, START + NT * b + u + 1)
                dve.wait_ge(s_st[u % 2], START + 16 * (NT // 2 * b + u // 2))
                dve.tensor_scalar(x_out[u % 2][:, :], r[u % 3][:, :], mv[u % 3][:, 0:1], rstd[u % 2][:, :],
                                  ALU.subtract, ALU.mult).then_inc(s_out, 1)

            for i in range(2):
                dve.memset(v1[i][:, :, P:P + 1], 1.0).then_inc(s_ones, 1)
            for c in range(KC):
                dve.wait_ge(s_x0h, START + c + 1)
                dve.tensor_tensor(xt_lo[0][:, c, :], xt_raw[0][:, c, :], xt_hi[0][:, c, :].bitcast(F32), ALU.subtract).then_inc(s_x0l, 1)
                dve.wait_ge(s_kv_wh[0], START + c + 1)
                dve.tensor_tensor(w_lo[0][:, c, :], w_raw[0][:, c, :], w_hi[0][:, c, :].bitcast(F32),
                                  ALU.subtract).then_inc(s_kv_wl[0], 1)
            for c in range(KC):
                dve.wait_ge(s_kv_wh[1], START + c + 1)
                dve.tensor_tensor(w_lo[1][:, c, :], w_raw[1][:, c, :], w_hi[1][:, c, :].bitcast(F32),
                                  ALU.subtract).then_inc(s_kv_wl[1], 1)
            with dve.Fori(0, NB) as b:
                steps.turn(b)
                for h in range(2):
                    for t in range(TB):
                        n = TB * h + t
                        dve.wait_ge(s_ek, START + NT * b + n + 1)
                        dve.wait_ge(s_kvt, START + NT * b + max(0, n - 1))
                        steps.done(dve.tensor_scalar(e_k[:, :], e_k[:, :], 1.0, None, ALU.min))
                        dve.scalar_tensor_tensor(out=k[n % 2][:, :], in0=ps[:, PROJ + 2 * (n % 2), :], scalar=0.0,
                                                 in1=e_k[:, :], op0=ALU.max, op1=ALU.add).then_inc(s_k, 1)
                    for m in range(KC):
                        dve.wait_ge(s_eq, START + 8 * b + 4 * h + m + 1)
                        steps.done(dve.tensor_scalar(e_q[:, :], e_q[:, :], 1.0, None, ALU.min))
                        dve.scalar_tensor_tensor(out=q[h][:, m, :], in0=ps[:, QP + m % 2, :], scalar=0.0,
                                                 in1=e_q[:, :], op0=ALU.max, op1=ALU.add).then_inc(s_qr, 1)
                dve.wait_ge(const.ready, 1)
                dve.wait_ge(s_kvt, START + NT * b + NT)
                kvp = ps[:, KV0:KV0 + 2, 0:2 * (P + 1)].rearrange("p a (g e) -> p a g e", g=2)
                for a in range(2):
                    dve.tensor_tensor(kvz[:, 2 * a:2 * a + 2, 0:P], kvp[:, a, :, 0:P],
                                      const.head_mask[:, :].unsqueeze(1).to_broadcast([P, 2, P]), ALU.mult)
                    ins = dve.tensor_tensor(kvz[:, 2 * a:2 * a + 2, P:P + HG],
                                            kvp[:, a, :, P:P + 1].to_broadcast([P, 2, HG]),
                                            const.head_mask[:, 0:P:DH].unsqueeze(1).to_broadcast([P, 2, HG]), ALU.mult)
                ins.then_inc(s_kv, 1)
                for t in range(NT + 2):
                    if t < NT:
                        num = ps[:, PROJ + 2 * (t % 2):PROJ + 2 * (t % 2) + 2, 0:2 * (P + HG)].rearrange("p a (g e) -> p a g e", g=2)
                        dve.wait_ge(s_num, START + NT * b + t + 1)
                        dve.wait_ge(s_tp, START + NT * b + max(0, t - 1))
                        for a in range(2):
                            ins = dve.tensor_scalar(z[:, 8 * a:8 * a + 8].rearrange("p (g h) -> p g h", g=2), num[:, a, :, P:P + HG], 1e-6, None, ALU.add)
                        steps.done(ins)
                        steps.done(dve.reciprocal(zi[t % 2][:, :], z[:, :]))
                        for a in range(2):
                            ins = dve.tensor_tensor(
                                att[t % 2][:, 256 * a:256 * a + 256].rearrange("p (g h e) -> p g h e", g=2, h=HG),
                                num[:, a, :, 0:P].rearrange("p g (h e) -> p g h e", h=HG),
                                zi[t % 2][:, 8 * a:8 * a + 8].rearrange("p (g h) -> p g h", g=2).unsqueeze(3).to_broadcast([P, 2, HG, DH]),
                                ALU.mult)
                        ins.then_inc(s_att, 1)
                    if 1 <= t <= NT:
                        u = t - 1
                        dve.wait_ge(s_ath, START + NT * b + u + 1)
                        dve.wait_ge(s_y, START + NT * b + max(0, u - 1))
                        dve.tensor_tensor(at_lo[u % 2][:, :, :], ps[:, TP + u % 2, :].rearrange("p (k n) -> p k n", k=KC),
                                          at_hi[u % 2][:, :, :].bitcast(F32), ALU.subtract).then_inc(s_atl, 1)
                    if 2 <= t:
                        u = t - 2
                        dve.wait_ge(s_y, START + NT * b + u + 1)
                        dve.wait_ge(s_xr[u % 4], START + 16 * (NT // 4 * b + u // 4 + 1))
                        dve.wait_ge(s_out, START + NT * b + max(0, u - 2))
                        dve.tensor_tensor(r[u % 3][:, :], ps[:, YP + u % 2, :], x_res[u % 4][:, :], ALU.add).then_inc(s_r, 1)
                        dve.wait_ge(s_r, START + NT * b + u + 1)
                        steps.done(dve.bn_stats(st[u % 3][:, :], r[u % 3][:, :]))
                        dve.memset(filler[:, :], 0.0)
                        steps.done(dve.bn_aggr(mv[u % 3][:, :], st[u % 3][:, :]))
                        dve.tensor_scalar(var[u % 2][:, :], mv[u % 3][:, 1:2], LN_EPS, None, ALU.add).then_inc(s_var, 1)
                    if 3 <= t:
                        normalise(t - 3, b)
                normalise(NT - 1, b)
                steps.end()

        @block.gpsimd
        def _(pool):
            const.make(pool)
            for i in range(2, NW):
                pool.wait_ge(s_w[i - 2], START + 16)
                pool.tensor_copy(w_hi[i][:, :, :], w_raw[i % 2][:, :, :]).then_inc(s_wh, 1)
                pool.wait_ge(s_wh, START + i - 1)
                pool.tensor_tensor(w_lo[i][:, :, :], w_raw[i % 2][:, :, :], w_hi[i][:, :, :].bitcast(F32),
                                   ALU.subtract).then_inc(s_wl, 1)
            with pool.Fori(0, NB) as b:
                for h in range(2):
                    pool.wait_ge(s_xth, START + 2 * b + h + 1)
                    pool.wait_ge(s_q, START + 8 * b + 4 * h)
                    pool.tensor_tensor(xt_lo[1 - h][:, :, :], xt_raw[1 - h][:, :, :], xt_hi[1 - h][:, :, :].bitcast(F32),
                                       ALU.subtract).then_inc(s_xtl, 1)
                for t in range(NT):
                    pool.wait_ge(s_var, START + NT * b + t + 1)
                    pool.tensor_tensor(rstd[t % 2][:, :], var[t % 2][:, :], const.minus_half[:, 0:1], ALU.pow).then_inc(s_rstd, 1)

        @block.tensor
        def _(pe):
            with pe.Fori(0, NB) as b:
                def add_kv(n):
                    pe.wait_ge(s_k, START + NT * b + n + 1)
                    pe.wait_ge(s_v, START + NT * b + n + 1)
                    if n == 0:
                        pe.wait_ge(s_r, START + NT * b)
                    for g in range(KC):
                        ins = pe.matmul(ps[:, KV0 + g // 2, (g % 2) * (P + 1):(g % 2 + 1) * (P + 1)],
                                        k[n % 2][:, g * P:(g + 1) * P], v1[n % 2][:, g, :],
                                        start=(n == 0 and g % 2 == 0), stop=(n == NT - 1), skip_group_check=True)
                    ins.then_inc(s_kvt, 1)

                for h in range(2):
                    pe.wait_ge(s_xth, START + 2 * b + h)
                    pe.wait_ge(s_xtl, START + 2 * b + h)
                    for t in range(TB):
                        n = TB * h + t
                        bank = PROJ + 2 * (n % 2)
                        if n < 2:
                            pe.wait_ge(s_att, START + NT * b)
                        else:
                            pe.wait_ge(s_k, START + NT * b + n - 1)
                            pe.wait_ge(s_v, START + NT * b + n - 1)
                        for i in range(2):
                            for c in range(KC):
                                if n == 0:
                                    if i == 0:
                                        pe.wait_ge(s_x0l, START + c + 1)
                                    pe.wait_ge(s_kv_wl[i], START + c + 1)
                                ins = three_products(pe, ps[:, bank + i, :], xt_hi[h][:, c, t * P:(t + 1) * P],
                                                     xt_lo[h][:, c, t * P:(t + 1) * P], w_hi[i][:, c, :], w_lo[i][:, c, :],
                                                     c == 0, c == KC - 1)
                        ins.then_inc(s_proj, 1)
                        if n >= 1:
                            add_kv(n - 1)
                    for m in range(KC):
                        if m < 2 and h == 0:
                            pe.wait_ge(s_atl, START + NT * b)
                        else:
                            pe.wait_ge(s_qr, START + 8 * b + 4 * h + m - 1)
                        pe.wait_ge(s_wl, START + 1)
                        for c in range(KC):
                            ins = three_products(pe, ps[:, QP + m % 2, :], w_hi[2][:, c, m * P:(m + 1) * P],
                                                 w_lo[2][:, c, m * P:(m + 1) * P], xt_hi[h][:, c, :], xt_lo[h][:, c, :],
                                                 c == 0, c == KC - 1)
                        ins.then_inc(s_q, 1)
                        if h == 1 and m == 0:
                            add_kv(NT - 1)
                for t in range(NT + 2):
                    if t < NT:
                        h, col = t // TB, (t % TB) * P
                        if t == 0:
                            pe.wait_ge(s_kv, START + b + 1)
                        if t < 2:
                            pe.wait_ge(s_k, START + NT * b + NT)
                            pe.wait_ge(s_v, START + NT * b + NT)
                        else:
                            pe.wait_ge(s_att, START + NT * b + t - 1)
                        pe.wait_ge(s_qr, START + 8 * b + 4 * h + 4)
                        for g in range(KC):
                            ins = pe.matmul(ps[:, PROJ + 2 * (t % 2) + g // 2, (g % 2) * (P + HG):(g % 2 + 1) * (P + HG)],
                                            q[h][:, g, col:col + P], kvz[:, g, :], start=True, stop=True)
                        ins.then_inc(s_num, 1)
                    if 1 <= t <= NT:
                        u = t - 1
                        pe.wait_ge(s_att, START + NT * b + u + 1)
                        pe.wait_ge(const.ready, 1)
                        if u < 2:
                            pe.wait_ge(s_qr, START + 8 * b + 8)
                        else:
                            pe.wait_ge(s_atl, START + NT * b + u - 1)
                            pe.wait_ge(s_ath, START + NT * b + u - 1)
                        for m in range(KC):
                            ins = pe.transpose(ps[:, TP + u % 2, m * P:(m + 1) * P], att[u % 2][:, m * P:(m + 1) * P], const.ident[:, :])
                        ins.then_inc(s_tp, 1)
                    if t >= 2:
                        u = t - 2
                        pe.wait_ge(s_ath, START + NT * b + u + 1)
                        pe.wait_ge(s_atl, START + NT * b + u + 1)
                        if u < 2:
                            pe.wait_ge(s_kv, START + b + 1)
                        else:
                            pe.wait_ge(s_r, START + NT * b + u - 1)
                        pe.wait_ge(s_wl, START + 2)
                        for c in range(KC):
                            ins = three_products(pe, ps[:, YP + u % 2, :], at_hi[u % 2][:, c, :], at_lo[u % 2][:, c, :],
                                                 w_hi[3][:, c, :], w_lo[3][:, c, :], c == 0, c == KC - 1)
                        ins.then_inc(s_y, 1)


I_FF = 1408
IT = I_FF // P
NIB = 8
RMS_EPS = 1e-6
SIGN_AND_MAGNITUDE = -0x72000000
FP16_UNBIAS = 16384.0


class FinishRows:

    def __init__(self, nc, ctx, x1, x2, const):
        def sb(name, shape):
            return ctx.enter_context(nc.sbuf_tensor(name, shape, F32))

        self.sems = []

        def sem(name):
            self.sems.append(nc.alloc_semaphore(name))
            return self.sems[-1]

        self.x1, self.x2, self.const = x1, x2, const
        self.x_res = sb("fx_res", [P, TB, C])
        self.y = sb("y_sb", [P, TB, C])
        self.r = sb("fr", [P, TB, C])
        self.ss = sb("ss", [P, TB])
        self.ms = sb("fms", [P, TB])
        self.rms = sb("rms", [P, TB])
        self.st = sb("fst", [P, TB, 6])
        self.mv = sb("fmv", [P, TB, 2])
        self.var = sb("fvar", [P, TB])
        self.rstd = sb("frstd", [P, TB])
        self.filler = sb("ffiller", [P, 1])
        self.s_xr = sem("fx_res_loaded")
        self.s_ye = sem("y_copied")
        self.s_ss = sem("squares_summed")
        self.s_ms = sem("mean_square_ready")
        self.s_rms = sem("rms_ready")
        self.s_r = sem("fresidual_added")
        self.s_st = sem("fstats_done")
        self.s_ag = sem("faggregated")
        self.s_var = sem("fvar_ready")
        self.s_rstd = sem("frstd_ready")
        self.s_out = sem("fx_out_ready")
        self.s_sto = sem("fx_out_stored")

    def load_residual(self, sp, b):
        sp.wait_ge(self.s_r, START + TB * b)
        sp.dma_start(self.x_res[:, :, :], self.x1[ds(b * TB, TB), :, :].rearrange("t p c -> p t c")).then_inc(self.s_xr, 16)

    def store(self, sp, b):
        sp.wait_ge(self.s_out, START + TB * b + TB)
        sp.dma_start(self.x2[ds(TB * b, TB), :, :].rearrange("t p c -> p t c"), self.r[:, :, :]).then_inc(self.s_sto, 16)

    def take(self, act, b, y):
        act.wait_ge(self.s_r, START + TB * b)
        for t in range(TB):
            act.activation(self.y[:, t, :], y[:, t, :], ACT.Copy).then_inc(self.s_ye, 1)

    def squares(self, act, b):
        act.wait_ge(self.s_sto, START + 16 * b)
        act.wait_ge(self.s_ye, START + TB * b + TB)
        for t in range(TB):
            act.activation(self.r[:, t, :], self.y[:, t, :], ACT.Square, accum_out=self.ss[:, t:t + 1]).then_inc(self.s_ss, 1)

    def mean_square(self, dve, b):
        dve.wait_ge(self.s_ss, START + TB * b + TB)
        dve.tensor_scalar(self.ms[:, :], self.ss[:, :], 1.0 / C, RMS_EPS, ALU.mult, ALU.add).then_inc(self.s_ms, 1)

    def inverse_rms(self, pool, b):
        pool.wait_ge(self.s_ms, START + b + 1)
        pool.tensor_tensor(self.rms[:, :], self.ms[:, :], self.const.minus_half[:, :], ALU.pow).then_inc(self.s_rms, 1)

    def add_residual(self, dve, b, t):
        if t == 0:
            dve.wait_ge(self.s_rms, START + b + 1)
            dve.wait_ge(self.s_xr, START + 16 * (b + 1))
        dve.scalar_tensor_tensor(out=self.r[:, t, :], in0=self.y[:, t, :], scalar=self.rms[:, t:t + 1],
                                 in1=self.x_res[:, t, :], op0=ALU.mult, op1=ALU.add).then_inc(self.s_r, 1)
        dve.wait_ge(self.s_r, START + TB * b + t + 1)
        dve.memset(self.filler[:, :], 0.0)
        dve.bn_stats(self.st[:, t, :], self.r[:, t, :]).then_inc(self.s_st, 1)

    def variance(self, dve, b):
        dve.wait_ge(self.s_st, START + TB * b + TB)
        dve.memset(self.filler[:, :], 0.0)
        for t in range(TB):
            dve.bn_aggr(self.mv[:, t, :], self.st[:, t, :]).then_inc(self.s_ag, 1)
        dve.wait_ge(self.s_ag, START + TB * b + TB)
        dve.tensor_scalar(self.var[:, :], self.mv[:, :, 1], LN_EPS, None, ALU.add).then_inc(self.s_var, 1)

    def inverse_std(self, pool, b):
        pool.wait_ge(self.s_var, START + b + 1)
        pool.tensor_tensor(self.rstd[:, :], self.var[:, :], self.const.minus_half[:, :], ALU.pow).then_inc(self.s_rstd, 1)

    def normalise(self, dve, b, t):
        if t == 0:
            dve.wait_ge(self.s_rstd, START + b + 1)
        dve.tensor_scalar(self.r[:, t, :], self.r[:, t, :], self.mv[:, t, 0:1], self.rstd[:, t:t + 1], ALU.subtract,
                          ALU.mult).then_inc(self.s_out, 1)


def fp4_feed_forward(nc, x1, gu_packed, gu_scales, dn_packed, dn_scales, rows, const):
    ctx, sems = ExitStack(), []
    ctx.callback(clear_semaphores, nc, sems)
    with ctx:
        def sb(name, shape, dt=F32):
            return ctx.enter_context(nc.sbuf_tensor(name, shape, dt))

        def sem(name):
            sems.append(nc.alloc_semaphore(name))
            return sems[-1]

        SLOTS = 5
        gu_val = sb("gu_val", [P, 2 * IT, KC, P], F32R)
        dn_hi = sb("dn_hi", [P, IT, C], F32R)
        dn_lo = sb("dn_lo", [P, IT, C], F32R)
        gu_scale16 = sb("gu_scale16", [P, 2 * IT, KC], F16)
        gu_scale = sb("gu_scale", [P, 2 * IT, KC])
        packed = [sb(f"packed{i}", [P, C], I32) for i in range(SLOTS)]
        nib = [sb(f"nib{i}", [P, C], I32) for i in range(SLOTS)]
        scale = [sb(f"scale{i}", [P, C], F16) for i in range(2)]
        scale_hi = [sb(f"scale_hi{i}", [P, C], F16) for i in range(2)]
        scale_lo = [sb(f"scale_lo{i}", [P, C], F16) for i in range(2)]
        dn_val = [sb(f"dn_val{i}", [P, C]) for i in range(2)]
        shift = sb("shift", [P, 1], I32)
        lane = sb("lane", [P, 1], I32)
        xs = sb("xs", [P, TB, C])
        xt_hi = sb("fxt_hi", [P, KC, BLK], F32R)
        xt_lo = sb("fxt_lo", [P, KC, BLK], F32R)
        acc = [[sb(f"acc{part}_{i}", [P, BLK]) for i in range(2)] for part in range(2)]
        sg = [sb(f"sg{i}", [P, BLK]) for i in range(2)]
        h = [sb(f"h{i}", [P, BLK]) for i in range(2)]
        HS = 3
        h_hi = [sb(f"h_hi{i}", [P, BLK], F32R) for i in range(HS)]
        h_lo = [sb(f"h_lo{i}", [P, BLK], F32R) for i in range(HS)]

        ps = ctx.enter_context(nc.psum_tensor("ps_fp4", [P, 8, 512], F32))
        Y, G = 0, 4

        s_ln = sem("lane_ready")
        s_sh = sem("shift_ready")
        s_gs = sem("gu_scales_loaded")
        s_gsc = sem("gu_scales_widened")
        s_pk = [sem(f"packed_loaded{i}") for i in range(SLOTS)]
        s_sc = [sem(f"scale_loaded{i}") for i in range(2)]
        s_n1 = sem("nibble_shifted")
        s_n2 = sem("nibble_masked")
        s_s1 = sem("scale_hi_done")
        s_s2 = sem("scale_lo_done")
        s_v = sem("gate_up_values_done")
        s_dv = sem("down_values_done")
        s_dh = sem("down_hi_done")
        s_dl = sem("down_lo_done")
        s_x = sem("xs_loaded")
        s_tp = sem("x_transposed")
        s_xth = sem("fxt_hi_done")
        s_xtl = sem("fxt_lo_done")
        s_gu = sem("group_projected")
        s_g0 = sem("first_group_scaled")
        s_acc = sem("group_added")
        s_sg = sem("silu_done")
        s_h = sem("h_ready")
        s_hh = sem("h_hi_done")
        s_hl = sem("h_lo_done")
        s_dn = sem("down_added")

        start_semaphores(nc, rows.sems + sems)
        block = ctx.enter_context(nc.Block())

        DOWN = 2
        chunks = [(0, 0), (0, 1)]
        for j in range(IT):
            chunks += [(j + 1, 0), (j + 1, 1)] if j + 1 < IT else []
            chunks.append((j, DOWN))
        NCH = len(chunks)

        def loads(n):
            return 1 if chunks[n][1] == DOWN else KC

        @block.sync
        def _(sp):
            sp.dma_start(xs[:, :, :], x1[0:TB, :, :].rearrange("t p c -> p t c")).then_inc(s_x, 16)
            sp.dma_start(gu_scale16[:, :, :], gu_scales).then_inc(s_gs, 16)
            for n in range(NCH):
                j, part = chunks[n]
                if n >= SLOTS:
                    sp.wait_ge(s_n1, START + n - SLOTS + 1)
                if part == DOWN:
                    if j >= 2:
                        sp.wait_ge(s_s2, START + j - 1)
                    sp.dma_start(packed[n % SLOTS][:, :], dn_packed[j * (P // NIB):(j + 1) * (P // NIB), :].unsqueeze(1)
                                 .to_broadcast([P // NIB, NIB, C])).then_inc(s_pk[n % SLOTS], 16)
                    sp.dma_start(scale[j % 2][:, :], dn_scales[j:j + 1, :].to_broadcast([P, C])).then_inc(s_sc[j % 2], 16)
                else:
                    o = part * IT + j
                    for kk in range(KC):
                        sp.dma_start(packed[n % SLOTS][:, kk * P:(kk + 1) * P], gu_packed[:, kk, o * P:(o + 1) * P]
                                     .unsqueeze(1).to_broadcast([P // NIB, NIB, P])).then_inc(s_pk[n % SLOTS], 16)

            def load(b, nxt):
                sp.wait_ge(s_tp, START + KC * b + KC)
                sp.dma_start(xs[:, :, :], x1[ds(nxt * TB, TB), :, :].rearrange("t p c -> p t c")).then_inc(s_x, 16)

            load(0, 1)
            rows.load_residual(sp, 0)
            with sp.Fori(1, NBLK) as b:
                load(b, (b + 1) % NBLK)
                rows.store(sp, b - 1)
                rows.load_residual(sp, b)
            sp.wait_ge(rows.s_sto, START + 16 * (NBLK - 1))
            sp.wait_ge(s_x, START + 16 * (NBLK + 1))

        @block.scalar
        def _(act):
            act.wait_ge(s_gs, START + 16)
            act.activation(gu_scale[:, :, :], gu_scale16[:, :, :], ACT.Copy).then_inc(s_gsc, 1)
            act.wait_ge(s_gsc, START + 1)

            def x_high(n):
                for c in range(KC):
                    act.wait_ge(s_tp, START + KC * n + c + 1)
                    act.activation(xt_hi[:, c, :], ps[:, G + c, :], ACT.Copy).then_inc(s_xth, 1)

            def values(j, part):
                n = chunks.index((j, part))
                act.wait_ge(s_n2, START + n + 1)
                act.activation(gu_val[:, part * IT + j, :, :].rearrange("p k o -> p (k o)"),
                               nib[n % SLOTS][:, :].bitcast(F16)[:, 1:2 * C:2], ACT.Copy, scale=FP16_UNBIAS).then_inc(s_v, 1)

            def down_values(j):
                n = chunks.index((j, DOWN))
                act.wait_ge(s_n2, START + n + 1)
                if j >= 2:
                    act.wait_ge(s_dh, START + j - 1)
                    act.wait_ge(s_dl, START + j - 1)
                act.activation(dn_val[j % 2][:, :], nib[n % SLOTS][:, :].bitcast(F16)[:, 1:2 * C:2], ACT.Copy,
                               scale=FP16_UNBIAS).then_inc(s_dv, 1)

            def first_group(b, j, part):
                u = 2 * (IT * b + j) + part
                act.wait_ge(s_gu, START + KC * u + 1)
                if part == 0:
                    act.wait_ge(s_sg, START + IT * b + max(0, j - 1))
                else:
                    act.wait_ge(s_h, START + IT * b + max(0, j - 1))
                act.activation(acc[part][j % 2][:, :], ps[:, G, :], ACT.Copy,
                               scale=gu_scale[:, part * IT + j, 0:1]).then_inc(s_g0, 1)

            def silu(b, j):
                act.wait_ge(s_acc, START + 3 * (2 * (IT * b + j)) + 3)
                act.wait_ge(s_h, START + IT * b + max(0, j - 1))
                act.activation(sg[j % 2][:, :], acc[0][j % 2][:, :], ACT.Silu).then_inc(s_sg, 1)

            def h_high(b, j):
                act.wait_ge(s_h, START + IT * b + j + 1)
                act.wait_ge(s_dn, START + IT * b + max(0, j - HS + 1))
                act.activation(h_hi[j % HS][:, :], h[j % 2][:, :], ACT.Copy).then_inc(s_hh, 1)

            def run(b, first):
                for j in range(IT):
                    first_group(b, j, 0)
                    if not first and j == 0:
                        take(b - 1)
                    if first and j:
                        down_values(j - 1)
                    if j:
                        h_high(b, j - 1)
                    first_group(b, j, 1)
                    if first and j + 1 < IT:
                        values(j + 1, 0)
                    silu(b, j)
                    if first and j + 1 < IT:
                        values(j + 1, 1)
                    if not first and j == 1:
                        rows.squares(act, b - 1)
                if first:
                    down_values(IT - 1)
                h_high(b, IT - 1)
                x_high(b + 1)

            def take(b):
                act.wait_ge(s_dn, START + IT * b + IT)
                rows.take(act, b, ps[:, Y:Y + TB, :])

            x_high(0)
            values(0, 0)
            values(0, 1)
            run(0, True)
            with act.Fori(1, NBLK) as b:
                run(b, False)
            take(NBLK - 1)

        @block.vector
        def _(dve):
            dve.wait_ge(s_ln, START + 1)
            dve.tensor_scalar(lane[:, :], lane[:, :], NIB - 1, 2, ALU.bitwise_and, ALU.logical_shift_left).then_inc(s_sh, 1)
            dve.wait_ge(s_sh, START + 1)
            dve.tensor_scalar(shift[:, :], lane[:, :], -1.0, 28.0, ALU.mult, ALU.add).then_inc(s_sh, 1)
            dve.wait_ge(s_sh, START + 2)

            def nibbles(n):
                j, part = chunks[n]
                i = n % SLOTS
                dve.wait_ge(s_pk[i], START + 16 * sum(loads(m) for m in range(i, n + 1, SLOTS)))
                if n >= SLOTS:
                    held, held_part = chunks[n - SLOTS]
                    if held_part == DOWN:
                        dve.wait_ge(s_dv, START + held + 1)
                    else:
                        dve.wait_ge(s_v, START + 2 * held + held_part + 1)
                dve.tensor_scalar(nib[i][:, :], packed[i][:, :], shift[:, 0:1], 3, ALU.logical_shift_left,
                                  ALU.arith_shift_right).then_inc(s_n1, 1)
                dve.wait_ge(s_n1, START + n + 1)
                dve.tensor_scalar(nib[i][:, :], nib[i][:, :], SIGN_AND_MAGNITUDE, None, ALU.bitwise_and).then_inc(s_n2, 1)

            def down_scales(j):
                i = j % 2
                dve.wait_ge(s_sc[i], START + 16 * (j // 2 + 1))
                if j >= 2:
                    dve.wait_ge(s_s2, START + j - 1)
                    dve.wait_ge(s_dh, START + j - 1)
                dve.tensor_scalar(scale_hi[i][:, :].bitcast(U16), scale[i][:, :].bitcast(U16), 0xFFFE, None,
                                  ALU.bitwise_and).then_inc(s_s1, 1)

            def x_low(n):
                for c in range(KC):
                    dve.wait_ge(s_xth, START + KC * n + c + 1)
                    dve.tensor_tensor(xt_lo[:, c, :], ps[:, G + c, :], xt_hi[:, c, :].bitcast(F32), ALU.subtract).then_inc(s_xtl, 1)

            def groups(b, j, part):
                u = 2 * (IT * b + j) + part
                a = acc[part][j % 2]
                for c in range(1, KC):
                    dve.wait_ge(s_gu, START + KC * u + c + 1)
                    if c == 1:
                        dve.wait_ge(s_g0, START + u + 1)
                    else:
                        dve.wait_ge(s_acc, START + 3 * u + c - 1)
                    dve.scalar_tensor_tensor(out=a[:, :], in0=ps[:, G + c, :], scalar=gu_scale[:, part * IT + j, c:c + 1],
                                             in1=a[:, :], op0=ALU.mult, op1=ALU.add).then_inc(s_acc, 1)

            def run(b, first):
                for j in range(IT):
                    groups(b, j, 0)
                    if first and j + 1 < IT:
                        nibbles(chunks.index((j + 1, 0)))
                    groups(b, j, 1)
                    if first:
                        if j + 1 < IT:
                            nibbles(chunks.index((j + 1, 1)))
                        down_scales(j)
                        nibbles(chunks.index((j, DOWN)))
                    else:
                        if j == 2:
                            rows.mean_square(dve, b - 1)
                        if 3 <= j < 3 + TB:
                            rows.add_residual(dve, b - 1, j - 3)
                        if j == 2 + TB:
                            rows.variance(dve, b - 1)
                        if j >= IT - TB:
                            rows.normalise(dve, b - 1, j - (IT - TB))
                x_low(b + 1)

            nibbles(0)
            nibbles(1)
            x_low(0)
            dve.wait_ge(s_gsc, START + 1)
            run(0, True)
            with dve.Fori(1, NBLK) as b:
                run(b, False)

        @block.gpsimd
        def _(pool):
            pool.iota(lane[:, :], pattern=[[0, 1]], base=0, channel_multiplier=1).then_inc(s_ln, 1)

            def down_weights(j):
                i = j % 2
                pool.wait_ge(s_s1, START + j + 1)
                pool.tensor_tensor(scale_lo[i][:, :], scale[i][:, :], scale_hi[i][:, :], ALU.subtract).then_inc(s_s2, 1)
                pool.wait_ge(s_dv, START + j + 1)
                pool.tensor_tensor(dn_hi[:, j, :], dn_val[i][:, :], scale_hi[i][:, :], ALU.mult).then_inc(s_dh, 1)
                pool.wait_ge(s_s2, START + j + 1)
                pool.tensor_tensor(dn_lo[:, j, :], dn_val[i][:, :], scale_lo[i][:, :], ALU.mult).then_inc(s_dl, 1)

            def product(b, j):
                pool.wait_ge(s_sg, START + IT * b + j + 1)
                pool.wait_ge(s_acc, START + 3 * (2 * (IT * b + j) + 1) + 3)
                pool.wait_ge(s_hl, START + IT * b + max(0, j - 1))
                pool.wait_ge(s_hh, START + IT * b + max(0, j - 1))
                pool.tensor_tensor(h[j % 2][:, :], sg[j % 2][:, :], acc[1][j % 2][:, :], ALU.mult).then_inc(s_h, 1)

            def h_low(b, j):
                pool.wait_ge(s_hh, START + IT * b + j + 1)
                pool.wait_ge(s_dn, START + IT * b + max(0, j - HS + 1))
                pool.tensor_tensor(h_lo[j % HS][:, :], h[j % 2][:, :], h_hi[j % HS][:, :].bitcast(F32), ALU.subtract).then_inc(s_hl, 1)

            for j in range(IT):
                product(0, j)
                down_weights(j)
                h_low(0, j)
            with pool.Fori(1, NBLK) as b:
                for j in range(IT):
                    product(b, j)
                    h_low(b, j)
                    if j == 2:
                        rows.inverse_rms(pool, b - 1)
                    if j == 2 + TB:
                        rows.inverse_std(pool, b - 1)

        @block.tensor
        def _(pe):
            def bank_left(u, c):
                if c == 0:
                    pe.wait_ge(s_g0, START + u)
                else:
                    pe.wait_ge(s_acc, START + 3 * (u - 1) + c)

            def transposes(n, first=False):
                pe.wait_ge(s_x, START + 16 * (n + 1))
                for c in range(KC):
                    if not first:
                        bank_left(2 * IT * n, c)
                    for t in range(TB):
                        ins = pe.transpose(ps[:, G + c, t * P:(t + 1) * P], xs[:, t, c * P:(c + 1) * P], const.ident[:, :])
                    ins.then_inc(s_tp, 1)

            def project(b, j, part, first):
                u = 2 * (IT * b + j) + part
                o = part * IT + j
                if first:
                    pe.wait_ge(s_v, START + 2 * j + part + 1)
                for c in range(KC):
                    if j == 0 and part == 0:
                        pe.wait_ge(s_xtl, START + KC * b + c + 1)
                    else:
                        bank_left(u, c)
                    pe.matmul(ps[:, G + c, :], gu_val[:, o, c, :], xt_hi[:, c, :], start=True, stop=False)
                    pe.matmul(ps[:, G + c, :], gu_val[:, o, c, :], xt_lo[:, c, :], start=False, stop=True).then_inc(s_gu, 1)

            def down(b, j, half, first):
                if half == 0:
                    pe.wait_ge(s_hh, START + IT * b + j + 1)
                    pe.wait_ge(s_hl, START + IT * b + j + 1)
                    if first:
                        pe.wait_ge(s_dh, START + j + 1)
                        pe.wait_ge(s_dl, START + j + 1)
                for t in range(2 * half, 2 * half + 2):
                    if j == 0 and not first:
                        pe.wait_ge(rows.s_ye, START + TB * (b - 1) + t + 1)
                    ins = three_products(pe, ps[:, Y + t, :], h_hi[j % HS][:, t * P:(t + 1) * P], h_lo[j % HS][:, t * P:(t + 1) * P],
                                         dn_hi[:, j, :], dn_lo[:, j, :], j == 0, j == IT - 1)
                if half == 1:
                    ins.then_inc(s_dn, 1)

            def run(b, first):
                for j in range(IT):
                    project(b, j, 0, first)
                    if j >= 2:
                        down(b, j - 2, 0, first)
                    project(b, j, 1, first)
                    if j >= 2:
                        down(b, j - 2, 1, first)
                down(b, IT - 2, 0, first)
                down(b, IT - 2, 1, first)
                transposes(b + 1)
                down(b, IT - 1, 0, first)
                down(b, IT - 1, 1, first)

            transposes(0, first=True)
            run(0, True)
            with pe.Fori(1, NBLK) as b:
                run(b, False)


HALF = 64
DK = 32
GLA_EPS = 1e-5


def gated_linear_attention(nc, x2, wqkT, wogT, wigT, woT, norm_w, router_w, router_b, x3, score, rows, const):
    ctx, sems = ExitStack(), []
    ctx.callback(clear_semaphores, nc, sems)
    ctx.callback(clear_semaphores, nc, rows.sems)
    with ctx:
        def sb(name, shape, dt=F32):
            return ctx.enter_context(nc.sbuf_tensor(name, shape, dt))

        def sem(name):
            sems.append(nc.alloc_semaphore(name))
            return sems[-1]

        WQK, WIG, WOG, WO = range(4)
        NW = 4
        w_cols = [P, C, C, C]
        w_raw = [sb(f"gw_raw{i}", [P, KC, w_cols[i]]) for i in range(NW - 1)]
        w_raw.append(w_raw[WIG])
        w_hi = [sb(f"gw_hi{i}", [P, KC, w_cols[i]], F32R) for i in range(NW)]
        w_lo = [sb(f"gw_lo{i}", [P, KC, w_cols[i]], F32R) for i in range(NW)]
        nw = sb("norm_w_sb", [P, KC])
        xs = [sb(f"gxs{i}", [P, TB, C]) for i in range(2)]
        xt_hi = sb("gxt_hi", [P, KC, BLK], F32R)
        xt_lo = sb("gxt_lo", [P, KC, BLK], F32R)
        qk_f = sb("qk_f", [P, BLK])
        q_max = sb("q_max", [P, TB])
        q_sum = sb("q_sum", [P, TB])
        q_inv = sb("q_inv", [P, TB])
        qx = sb("qx", [P, TB, DK])
        qs = sb("qs", [P, TB, DK])
        kx = sb("kx", [P, TB, DK])
        ks = sb("ks", [P, TB, DK])
        sp = sb("sp", [P, TB, DK])
        decay = sb("decay", [P, 4, TB, DK])
        grow = sb("grow", [P, TB, DK])
        QH, QT, KA, KB = range(4)
        feats = sb("feats", [P, 4, TB, DK])
        k_end = sb("k_end", [P, TB, DK])
        ft = [sb(f"ft{i}", [DK, 4, P]) for i in range(2)]
        at = [sb(f"gat{i}", [P, P]) for i in range(2)]
        state = sb("state", [DK, C])
        dec = sb("dec", [DK, TB])
        o_f = sb("o_f", [P, KC, BLK])
        o_hi = sb("o_hi", [P, KC, BLK], F32R)
        o_lo = sb("o_lo", [P, KC, BLK], F32R)
        sq = sb("sq", [P, KC, P])
        sq2 = sb("sq2", [P, 2, P])
        sq1 = [sb(f"sq1_{i}", [P, P]) for i in range(2)]
        sg = [sb(f"gsg{i}", [P, BLK]) for i in range(2)]
        p_hi = sb("p_hi", [P, KC, BLK], F32R)
        p_lo = sb("p_lo", [P, KC, BLK], F32R)
        ms = sb("ms", [P, TB])
        rms = sb("grms", [P, TB])
        r = sb("gr", [P, TB, C])
        st = sb("gst", [P, TB, 6])
        mv = sb("gmv", [P, TB, 2])
        var = sb("gvar", [P, TB])
        rstd = sb("grstd", [P, TB])
        filler = sb("gfiller", [P, 1])
        rw_sb = sb("rw_sb", [P, C])
        rb_sb = sb("rb_sb", [P, 1])
        junk = sb("gjunk", [P, C])
        dot = sb("dot", [P, TB])
        table = sb("table", [P, 1])

        ps = ctx.enter_context(nc.psum_tensor("ps_gla", [P, 8, 512], F32))
        F, A, S, O, GO = 0, 1, 2, 3, 4
        D_COL, SS_COL = 128, 132

        s_nw = sem("norm_w_loaded")
        s_w = [sem(f"gw_loaded{i}") for i in range(NW)]
        s_fold = sem("norm_w_folded")
        s_wh = sem("gw_hi_done")
        s_wl = sem("gw_lo_done_by_dve")
        s_wlp = sem("gw_lo_done_by_pool")
        s_zero = sem("table_and_rows_zeroed")
        s_table = sem("exp_table_loaded")
        s_x = [sem(f"gx_loaded{i}") for i in range(2)]
        s_tp = sem("gx_transposed")
        s_xth = sem("gxt_hi_done")
        s_xtl = sem("gxt_lo_done")
        s_qk = sem("qk_projected")
        s_qkf = sem("qk_taken")
        s_tok = sem("qk_transposed")
        s_qx = sem("q_shifted")
        s_qe = sem("q_exp_done_gla")
        s_ke = sem("k_exp_done_gla")
        s_ks = sem("k_sigmoid_done")
        s_k2 = sem("k_exp2_done")
        s_sp = sem("softplus_done")
        s_sum = sem("gate_sums_done")
        s_dec = sem("decays_done")
        s_ft = sem("feats_ready")
        s_ftt = sem("feats_transposed")
        s_fts = sem("feats_taken")
        s_a = sem("scores_done")
        s_at = sem("scores_masked")
        s_su = sem("state_update_done")
        s_dexp = sem("state_decay_ready")
        s_s = sem("state_ready")
        s_o = sem("o_done")
        s_of = sem("o_copied")
        s_sq = sem("o_squared")
        s_sq2 = sem("squares_paired")
        s_sq1 = sem("squares_of_tile_added")
        s_oh = sem("o_hi_done")
        s_ol = sem("o_lo_done")
        s_ss = sem("o_squares_summed")
        s_go = sem("go_done")
        s_sg = sem("gsilu_done")
        s_p = sem("p_ready")
        s_ph = sem("p_hi_done")
        s_pl = sem("p_lo_done")
        s_y = sem("gy_done")
        s_ms = sem("gmean_square_ready")
        s_rms = sem("grms_ready")
        s_r = sem("gresidual_added")
        s_st = sem("gstats_done")
        s_ag = sem("gaggregated")
        s_var = sem("gvar_ready")
        s_rstd = sem("grstd_ready")
        s_out = sem("gx_out_ready")
        s_sto = sem("gx_out_stored")
        s_rw = sem("router_w_loaded")
        s_sc = sem("scores_kept")
        s_dot = sem("score_dot_done")
        s_dve = sem("dve_step_gla")

        start_semaphores(nc, sems)
        block = ctx.enter_context(nc.Block())

        @block.sync
        def _(sp_):
            sp_.dma_start(w_raw[WQK][:, :, 0:2 * DK], wqkT).then_inc(s_w[WQK], 16)
            sp_.dma_start(w_raw[WQK][:, :, 2 * DK:P], wqkT).then_inc(s_w[WQK], 16)
            sp_.dma_start(xs[0][:, :, :], x2[0:TB, :, :].rearrange("t p c -> p t c")).then_inc(s_x[0], 16)
            sp_.dma_start(w_raw[WIG][:, :, :], wigT).then_inc(s_w[WIG], 16)
            sp_.dma_start(w_raw[WOG][:, :, :], wogT).then_inc(s_w[WOG], 16)
            sp_.dma_start(nw[:, :], norm_w).then_inc(s_nw, 16)
            sp_.dma_start(rw_sb[:, :], router_w.to_broadcast([P, C])).then_inc(s_rw, 16)
            sp_.dma_start(rb_sb[:, :], router_b.to_broadcast([P, 1])).then_inc(s_rw, 16)
            sp_.wait_ge(s_wl, START + 2)
            sp_.dma_start(w_raw[WO][:, :, :], woT).then_inc(s_w[WO], 16)
            rows.store(sp_, NBLK - 1)
            sp_.wait_ge(rows.s_sto, START + 16 * NBLK)
            with sp_.Fori(0, NB) as b:
                for h in range(2):
                    n = 2 * b + h
                    sp_.wait_ge(s_r, START + TB * n)
                    sp_.dma_start(xs[1 - h][:, :, :], x2[ds((n + 1) % NBLK * TB, TB), :, :].rearrange("t p c -> p t c")).then_inc(s_x[1 - h], 16)
                    for t in range(TB):
                        sp_.wait_ge(s_out, START + TB * n + t + 1)
                        sp_.dma_start(x3[TB * n + t, :, :], r[:, t, :]).then_inc(s_sto, 16)
            sp_.wait_ge(s_sto, START + 16 * TB * NBLK)
            sp_.wait_ge(s_x[0], START + 16 * (NB + 1))

        @block.scalar
        def _(act):
            def weight_high(i):
                act.wait_ge(s_w[i], START + (32 if i == WQK else 16))
                act.activation(w_hi[i][:, :, :], w_raw[i][:, :, :], ACT.Copy).then_inc(s_wh, 1)

            def x_high(n):
                for c in range(KC):
                    act.wait_ge(s_tp, START + KC * n + c + 1)
                    act.activation(xt_hi[:, c, :], ps[:, GO + c, :], ACT.Copy).then_inc(s_xth, 1)

            rows.squares(act, NBLK - 1)
            act.wait_ge(s_zero, START + 2)
            weight_high(WQK)
            x_high(0)
            weight_high(WIG)
            weight_high(WOG)
            with act.Fori(0, NB) as b:
                for h in range(2):
                    n = 2 * b + h
                    act.wait_ge(s_qk, START + n + 1)
                    act.activation(qk_f[:, :], ps[:, F, :], ACT.Copy).then_inc(s_qkf, 1)
                    tok = ps[:, A, :].rearrange("p (t f) -> p t f", t=TB)
                    act.wait_ge(s_qx, START + n + 1)
                    act.activation(kx[:, :, :], tok[:, :, DK:2 * DK], ACT.Exp, scale=-1.0).then_inc(s_ke, 1)
                    act.activation(qx[:, :, :], qx[:, :, :], ACT.Exp).then_inc(s_qe, 1)
                    act.wait_ge(s_ks, START + n + 1)
                    act.activation(kx[:, :, :], ks[:, :, :], ACT.Exp).then_inc(s_k2, 1)
                    act.wait_ge(s_k2, START + n + 1)
                    act.activation(sp[:, :, :], kx[:, :, :], ACT.Ln, bias=1.0).then_inc(s_sp, 1)
                    act.activation(table[:, :], table[:, :], ACT.Exp, scale=0.0).then_inc(s_table, 1)
                    act.wait_ge(s_table, START + n + 1)
                    act.wait_ge(s_sum, START + n + 1)
                    act.wait_ge(s_ft, START + 5 * n)
                    act.activation(decay[:, :, :, :].rearrange("p a t d -> p (a t d)"), ps[:, F, :], ACT.Exp, scale=-1.0).then_inc(s_dec, 1)
                    act.activation(grow[:, :, :].rearrange("p t d -> p (t d)"), ps[:, F, 0:P], ACT.Exp).then_inc(s_dec, 1)
                    act.wait_ge(s_s, START + 2 * TB * b + TB * h + b + 1)
                    act.activation(dec[:, :], ps[0:DK, A, D_COL:D_COL + TB], ACT.Exp, scale=-1.0).then_inc(s_dexp, 1)

                    def take_feats(t):
                        i = TB * n + t
                        act.wait_ge(s_ftt, START + i + 1)
                        act.wait_ge(s_o, START + TB * n + max(0, t - 1))
                        act.activation(ft[t % 2][:, :, :].rearrange("d a n -> d (a n)"), ps[0:DK, F, :], ACT.Copy).then_inc(s_fts, 1)

                    take_feats(0)
                    for t in range(TB):
                        i = TB * n + t
                        if t + 1 < TB:
                            take_feats(t + 1)
                        act.wait_ge(s_o, START + i + 1)
                        o = ps[:, O, :].rearrange("p (m n) -> p m n", m=KC)
                        o_t = o_f[:, :, t * P:(t + 1) * P]
                        act.activation(o_t, o, ACT.Copy).then_inc(s_of, 1)
                        act.wait_ge(s_of, START + i + 1)
                        act.activation(o_hi[:, :, t * P:(t + 1) * P], o_t, ACT.Copy).then_inc(s_oh, 1)
                        act.wait_ge(s_sq2, START + i)
                        act.activation(sq[:, :, :], o_t, ACT.Square).then_inc(s_sq, 1)
                    for m in range(KC):
                        act.wait_ge(s_go, START + KC * n + m + 1)
                        act.wait_ge(s_pl, START + KC * n + max(0, m - 1))
                        act.activation(sg[m % 2][:, :], ps[:, GO + m, :], ACT.Silu).then_inc(s_sg, 1)
                        act.wait_ge(s_p, START + KC * n + m + 1)
                        act.activation(p_hi[:, m, :], sg[m % 2][:, :], ACT.Copy).then_inc(s_ph, 1)
                    x_high(n + 1)

        @block.vector
        def _(dve):
            def x_low(n):
                for c in range(KC):
                    dve.wait_ge(s_xth, START + KC * n + c + 1)
                    dve.tensor_tensor(xt_lo[:, c, :], ps[:, GO + c, :], xt_hi[:, c, :].bitcast(F32), ALU.subtract).then_inc(s_xtl, 1)

            def weight_low(i):
                dve.wait_ge(s_wh, START + i + 1)
                dve.tensor_tensor(w_lo[i][:, :, :], w_raw[i][:, :, :], w_hi[i][:, :, :].bitcast(F32), ALU.subtract).then_inc(s_wl, 1)

            def score_tile(n, t):
                dve.wait_ge(s_out, START + TB * n)
                dve.wait_ge(s_dot, START + TB * n + t)
                dve.tensor_tensor_reduce(out=junk[:, :], in0=r[:, t, :], in1=rw_sb[:, :], scale=1.0, scalar=0.0,
                                         op0=ALU.mult, op1=ALU.add, accum_out=dot[:, t:t + 1]).then_inc(s_dot, 1)

            def keep_scores(n):
                dve.wait_ge(s_dot, START + TB * n + TB)
                dve.tensor_scalar(score[:, ds(TB * n, TB)], dot[:, :], rb_sb[:, 0:1], None, ALU.add).then_inc(s_sc, 1)

            steps = Steps(dve, s_dve, 2 * 5)
            rows.mean_square(dve, NBLK - 1)
            for t in range(TB):
                rows.add_residual(dve, NBLK - 1, t)
            rows.variance(dve, NBLK - 1)
            weight_low(WQK)
            x_low(0)
            for t in range(TB):
                rows.normalise(dve, NBLK - 1, t)
            weight_low(WIG)
            dve.wait_ge(s_rw, START + 32)
            dve.wait_ge(s_zero, START + 2)
            with dve.Fori(0, NB) as b:
                steps.turn(b)
                dve.wait_ge(s_o, START + 2 * TB * b)
                dve.memset(state[:, :], 0.0).then_inc(s_s, 1)
                for h in range(2):
                    n = 2 * b + h
                    dve.wait_ge(s_tok, START + n + 1)
                    tok = ps[:, A, :].rearrange("p (t f) -> p t f", t=TB)
                    steps.done(dve.tensor_reduce(q_max[:, :], tok[:, :, 0:DK], AX.X, ALU.max))
                    dve.tensor_tensor(qx[:, :, :], tok[:, :, 0:DK], q_max[:, :].unsqueeze(2).to_broadcast([P, TB, DK]),
                                      ALU.subtract).then_inc(s_qx, 1)
                    dve.wait_ge(s_ke, START + n + 1)
                    steps.done(dve.tensor_scalar(kx[:, :, :], kx[:, :, :], 1.0, None, ALU.add))
                    dve.reciprocal(ks[:, :, :], kx[:, :, :]).then_inc(s_ks, 1)
                    dve.wait_ge(s_qe, START + n + 1)
                    steps.done(dve.tensor_reduce(q_sum[:, :], qx[:, :, :], AX.X, ALU.add))
                    steps.done(dve.reciprocal(q_inv[:, :], q_sum[:, :]))
                    steps.done(dve.tensor_tensor(qs[:, :, :], qx[:, :, :], q_inv[:, :].unsqueeze(2).to_broadcast([P, TB, DK]), ALU.mult))
                    dve.wait_ge(s_dec, START + 2 * n + 2)
                    dve.wait_ge(s_su, START + TB * n)
                    dve.wait_ge(s_ks, START + n + 1)
                    dve.tensor_tensor(feats[:, QH, :, :], qs[:, :, :], decay[:, 0, :, :], ALU.mult).then_inc(s_ft, 1)
                    dve.tensor_tensor(feats[:, KA, :, :], ks[:, :, :], grow[:, :, :], ALU.mult).then_inc(s_ft, 1)
                    dve.tensor_tensor(feats[:, KB, :, :], ks[:, :, :], decay[:, 1, :, :], ALU.mult).then_inc(s_ft, 1)
                    dve.tensor_tensor(feats[:, QT, :, :], qs[:, :, :], decay[:, 2, :, :], ALU.mult).then_inc(s_ft, 1)
                    dve.tensor_tensor(k_end[:, :, :], ks[:, :, :], decay[:, 3, :, :], ALU.mult).then_inc(s_ft, 1)

                    def mask(t):
                        i = TB * n + t
                        dve.wait_ge(s_a, START + i + 1)
                        dve.tensor_tensor(at[t % 2][:, :], ps[:, A, 0:P], const.upto[:, :], ALU.mult).then_inc(s_at, 1)

                    mask(0)
                    dve.wait_ge(s_sc, START + n)
                    for t in range(TB):
                        i = TB * n + t
                        dve.wait_ge(s_dexp, START + n + 1)
                        dve.wait_ge(s_su, START + i + 1)
                        dve.wait_ge(s_o, START + i + 1)
                        dve.scalar_tensor_tensor(out=state[:, :], in0=state[:, :], scalar=dec[:, t:t + 1],
                                                 in1=ps[0:DK, S, :], op0=ALU.mult, op1=ALU.add).then_inc(s_s, 1)
                        if t + 1 < TB:
                            mask(t + 1)
                        dve.wait_ge(s_oh, START + i + 1)
                        dve.tensor_tensor(o_lo[:, :, t * P:(t + 1) * P], o_f[:, :, t * P:(t + 1) * P],
                                          o_hi[:, :, t * P:(t + 1) * P].bitcast(F32), ALU.subtract).then_inc(s_ol, 1)
                        score_tile(n, t)
                    keep_scores(n)
                    dve.wait_ge(s_ss, START + TB * n + TB)
                    dve.tensor_scalar(ms[:, :], ps[:, A, SS_COL:SS_COL + TB], 1.0 / C, GLA_EPS, ALU.mult, ALU.add).then_inc(s_ms, 1)
                    for m in range(KC):
                        dve.wait_ge(s_sg, START + KC * n + m + 1)
                        dve.tensor_tensor(sg[m % 2][:, :], sg[m % 2][:, :], o_f[:, m, :], ALU.mult).then_inc(s_p, 1)
                    x_low(n + 1)
                    dve.wait_ge(s_rms, START + n + 1)
                    dve.wait_ge(s_sto, START + 16 * TB * n)
                    dve.wait_ge(s_dot, START + TB * n + TB)
                    for t in range(TB):
                        dve.wait_ge(s_y, START + TB * n + t + 1)
                        dve.scalar_tensor_tensor(out=r[:, t, :], in0=ps[:, t, :], scalar=rms[:, t:t + 1], in1=xs[h][:, t, :],
                                                 op0=ALU.mult, op1=ALU.add).then_inc(s_r, 1)
                        dve.wait_ge(s_r, START + TB * n + t + 1)
                        dve.memset(filler[:, :], 0.0)
                        dve.bn_stats(st[:, t, :], r[:, t, :]).then_inc(s_st, 1)
                    dve.wait_ge(s_st, START + TB * n + TB)
                    dve.memset(filler[:, :], 0.0)
                    for t in range(TB):
                        dve.bn_aggr(mv[:, t, :], st[:, t, :]).then_inc(s_ag, 1)
                    dve.wait_ge(s_ag, START + TB * n + TB)
                    dve.tensor_scalar(var[:, :], mv[:, :, 1], LN_EPS, None, ALU.add).then_inc(s_var, 1)
                    dve.wait_ge(s_rstd, START + n + 1)
                    for t in range(TB):
                        dve.tensor_scalar(r[:, t, :], r[:, t, :], mv[:, t, 0:1], rstd[:, t:t + 1], ALU.subtract,
                                          ALU.mult).then_inc(s_out, 1)
                steps.end()
            dve.wait_ge(s_out, START + TB * NBLK)
            dve.wait_ge(s_sc, START + NBLK)
            for t in range(TB):
                score_tile(NBLK, t)
            keep_scores(NBLK)

        @block.gpsimd
        def _(pool):
            pool.memset(table[:, :], 0.0).then_inc(s_zero, 1)
            pool.memset(r[:, :, :], 0.0).then_inc(s_zero, 1)
            rows.inverse_rms(pool, NBLK - 1)
            rows.inverse_std(pool, NBLK - 1)
            pool.wait_ge(s_wh, START + WOG + 1)
            pool.tensor_tensor(w_lo[WOG][:, :, :], w_raw[WOG][:, :, :], w_hi[WOG][:, :, :].bitcast(F32), ALU.subtract).then_inc(s_wlp, 1)
            pool.wait_ge(s_nw, START + 16)
            pool.wait_ge(s_w[WO], START + 16)
            pool.tensor_tensor(w_raw[WO][:, :, :], w_raw[WO][:, :, :], nw[:, :].unsqueeze(2).to_broadcast([P, KC, C]), ALU.mult).then_inc(s_fold, 1)
            pool.wait_ge(s_fold, START + 1)
            pool.tensor_copy(w_hi[WO][:, :, :], w_raw[WO][:, :, :]).then_inc(s_fold, 1)
            pool.wait_ge(s_fold, START + 2)
            pool.tensor_tensor(w_lo[WO][:, :, :], w_raw[WO][:, :, :], w_hi[WO][:, :, :].bitcast(F32), ALU.subtract).then_inc(s_wlp, 1)
            with pool.Fori(0, NB) as b:
                for h in range(2):
                    n = 2 * b + h
                    for t in range(TB):
                        i = TB * n + t
                        pool.wait_ge(s_sq, START + i + 1)
                        pool.wait_ge(s_sq1, START + i)
                        pool.tensor_tensor(sq2[:, :, :], sq[:, 0:2, :], sq[:, 2:4, :], ALU.add).then_inc(s_sq2, 1)
                        pool.wait_ge(s_sq2, START + i + 1)
                        pool.wait_ge(s_ss, START + TB * n + max(0, t - 1))
                        pool.tensor_tensor(sq1[t % 2][:, :], sq2[:, 0, :], sq2[:, 1, :], ALU.add).then_inc(s_sq1, 1)
                    pool.wait_ge(s_ms, START + n + 1)
                    pool.tensor_tensor(rms[:, :], ms[:, :], const.minus_half[:, :], ALU.pow).then_inc(s_rms, 1)
                    for m in range(KC):
                        pool.wait_ge(s_ph, START + KC * n + m + 1)
                        pool.tensor_tensor(p_lo[:, m, :], sg[m % 2][:, :], p_hi[:, m, :].bitcast(F32), ALU.subtract).then_inc(s_pl, 1)
                    pool.wait_ge(s_var, START + n + 1)
                    pool.tensor_tensor(rstd[:, :], var[:, :], const.minus_half[:, :], ALU.pow).then_inc(s_rstd, 1)

        @block.tensor
        def _(pe):
            def transposes(x_in, n):
                for c in range(KC):
                    if n is not None:
                        pe.wait_ge(s_sg, START + KC * n + c + 1)
                    for t in range(TB):
                        ins = pe.transpose(ps[:, GO + c, t * P:(t + 1) * P], x_in[:, t, c * P:(c + 1) * P], const.ident[:, :])
                    ins.then_inc(s_tp, 1)

            pe.wait_ge(s_x[0], START + 16)
            transposes(xs[0], None)
            with pe.Fori(0, NB) as b:
                for h in range(2):
                    n = 2 * b + h
                    x_in = xs[h]

                    def gate(m, half, last):
                        w, hi, lo = ((WIG, xt_hi, xt_lo), (WOG, o_hi, o_lo))[half]
                        for c in range(KC):
                            ins = three_products(pe, ps[:, GO + m, :], w_hi[w][:, c, m * P:(m + 1) * P], w_lo[w][:, c, m * P:(m + 1) * P],
                                                 hi[:, c, :], lo[:, c, :], half == 0 and c == 0, last and c == KC - 1)
                        return ins

                    pe.wait_ge(s_xtl, START + KC * n + KC)
                    pe.wait_ge(s_r, START + TB * n)
                    pe.wait_ge(s_wl, START + 1)
                    for c in range(KC):
                        ins = three_products(pe, ps[:, F, :], w_hi[WQK][:, c, :], w_lo[WQK][:, c, :], xt_hi[:, c, :], xt_lo[:, c, :],
                                             c == 0, c == KC - 1)
                    ins.then_inc(s_qk, 1)
                    pe.wait_ge(s_wl, START + 2)
                    gate(0, 0, False)
                    pe.wait_ge(s_qkf, START + n + 1)
                    pe.wait_ge(s_ms, START + n)
                    for t in range(TB):
                        ins = pe.transpose(ps[:, A, t * P:(t + 1) * P], qk_f[:, t * P:(t + 1) * P], const.ident[:, :])
                    ins.then_inc(s_tok, 1)
                    gate(1, 0, False)
                    gate(2, 0, False)
                    pe.wait_ge(s_sp, START + n + 1)
                    for a, m in enumerate((const.within, const.to_half, const.upto, const.before)):
                        ins = pe.matmul(ps[:, F, a * P:(a + 1) * P], m[:, :], sp[:, :, :].rearrange("p t d -> p (t d)"), start=True, stop=True)
                    for t in range(TB):
                        ins = pe.matmul(ps[0:DK, A, D_COL + t:D_COL + t + 1], sp[:, t, :], const.ones[:, 0:1], start=True, stop=True)
                    ins.then_inc(s_sum, 1)
                    gate(3, 0, False)

                    def transpose_feats(t):
                        i = TB * n + t
                        pe.wait_ge(s_ft, START + 5 * n + 5)
                        pe.wait_ge(s_dec, START + 2 * n + 2)
                        pe.wait_ge(s_fts, START + i)
                        for a in range(4):
                            ins = pe.transpose(ps[0:DK, F, a * P:(a + 1) * P], feats[:, a, t, :], const.ident[:, :])
                        ins.then_inc(s_ftt, 1)

                    def scores(t):
                        i = TB * n + t
                        f = ft[t % 2]
                        pe.wait_ge(s_dexp, START + n + 1)
                        pe.wait_ge(s_at, START + i)
                        pe.wait_ge(s_fts, START + i + 1)
                        pe.matmul(ps[:, A, 0:HALF], f[:, KA, :], f[:, QH, 0:HALF], start=True, stop=True)
                        pe.matmul(ps[:, A, HALF:P], f[:, KB, :], f[:, QH, HALF:P], start=True, stop=True).then_inc(s_a, 1)
                        pe.wait_ge(s_s, START + i + b + 1)
                        pe.matmul(ps[0:DK, S, :], k_end[:, t, :], x_in[:, t, :], start=True, stop=True).then_inc(s_su, 1)

                    def outputs(t):
                        i = TB * n + t
                        f = ft[t % 2]
                        pe.wait_ge(s_at, START + i + 1)
                        pe.wait_ge(s_of, START + i)
                        for m in range(KC):
                            o = ps[:, O, m * P:(m + 1) * P]
                            pe.matmul(o, x_in[:, t, m * P:(m + 1) * P], at[t % 2][:, :], start=True, stop=False)
                            ins = pe.matmul(o, state[:, m * P:(m + 1) * P], f[:, QT, :], start=False, stop=True)
                        ins.then_inc(s_o, 1)

                    def sum_squares(t):
                        i = TB * n + t
                        pe.wait_ge(s_sq1, START + i + 1)
                        pe.matmul(ps[:, A, SS_COL + t:SS_COL + t + 1], sq1[t % 2][:, :], const.ones[:, 0:1],
                                  start=True, stop=True).then_inc(s_ss, 1)

                    transpose_feats(0)
                    scores(0)
                    for t in range(TB):
                        if t + 1 < TB:
                            transpose_feats(t + 1)
                        outputs(t)
                        if t:
                            sum_squares(t - 1)
                        if t + 1 < TB:
                            scores(t + 1)
                    pe.wait_ge(s_wlp, START + 1)
                    pe.wait_ge(s_ol, START + TB * n + TB)
                    gate(0, 1, True).then_inc(s_go, 1)
                    sum_squares(TB - 1)
                    for m in range(1, KC):
                        gate(m, 1, True).then_inc(s_go, 1)
                    pe.wait_ge(s_x[1 - h], START + 16 * (b + 1 + h))
                    transposes(xs[1 - h], n)
                    pe.wait_ge(s_ms, START + n + 1)
                    pe.wait_ge(s_of, START + TB * n + TB)
                    pe.wait_ge(s_s, START + TB * n + TB + b + 1)
                    pe.wait_ge(s_wlp, START + 2)
                    for t in range(TB):
                        for c in range(KC):
                            if t == 0:
                                pe.wait_ge(s_ph, START + KC * n + c + 1)
                                pe.wait_ge(s_pl, START + KC * n + c + 1)
                            ins = three_products(pe, ps[:, t, :], p_hi[:, c, t * P:(t + 1) * P], p_lo[:, c, t * P:(t + 1) * P],
                                                 w_hi[WO][:, c, :], w_lo[WO][:, c, :], c == 0, c == KC - 1)
                        ins.then_inc(s_y, 1)


D_FF = 2048
FT = D_FF // P
TOP = T // 2
NT8 = T // P


def routed_feed_forward(nc, x3, score, w1, b1, w2, b2, pairs, out, const):
    ctx, sems = ExitStack(), []
    ctx.callback(clear_semaphores, nc, sems)
    with ctx:
        def sb(name, shape, dt=F32):
            return ctx.enter_context(nc.sbuf_tensor(name, shape, dt))

        def sem(name):
            sems.append(nc.alloc_semaphore(name))
            return sems[-1]

        def sem_of_pool_dma(name):
            pool_sems.append(nc.alloc_semaphore(name))
            return pool_sems[-1]

        pool_sems = []
        ctx.callback(clear_semaphores, nc, pool_sems)

        W1, W2 = 0, 1
        NW = D_FF // 256
        chunks = [(W1, 0), (W1, 1)]
        for i in range(NW):
            chunks += [(W2, i)] + ([(W1, i + 2)] if i + 2 < NW else [])
        NCH = len(chunks)
        EARLY = 8
        BY_POOL = 1
        SLOTS = 3
        HS = 3

        w1_hi = sb("w1_hi", [P, KC, D_FF], F32R)
        w1_lo = sb("w1_lo", [P, KC, D_FF], F32R)
        w2_hi = sb("w2_hi", [P, FT, C], F32R)
        w2_lo = sb("w2_lo", [P, FT, C], F32R)
        w_raw = [sb(f"mw_raw{i}", [P, 2, C]) for i in range(SLOTS)]
        b1_sb = sb("b1_sb", [P, FT])
        b2_sb = sb("b2_sb", [P, C])
        pair = sb("pair", [P, NB * NT8, 2])
        scores = [sb(f"scores{b}", [P, T]) for b in range(NB)]
        junk = sb("junk", [P, T])
        junk_own = sb("junk_own", [P, P])
        counts = sb("counts", [P, 3, NT8])
        row = [sb(f"row{b}", [P, NT8], I32) for b in range(NB)]
        sel = [sb(f"sel{b}", [P, TB, 2]) for b in range(NB)]
        xsel = [sb(f"xsel{b}", [P, TB, C]) for b in range(NB)]
        xt_hi = sb("mxt_hi", [P, KC, BLK], F32R)
        xt_lo = sb("mxt_lo", [P, KC, BLK], F32R)
        diag = xsel[1][:, :, :].rearrange("p t (a n) -> p (t a) n", n=P)
        h = [sb(f"mh{i}", [P, BLK]) for i in range(2)]
        h_hi = [sb(f"mh_hi{i}", [P, BLK], F32R) for i in range(HS)]
        h_lo = [sb(f"mh_lo{i}", [P, BLK], F32R) for i in range(HS)]
        st = sb("mst", [P, TB, 6])
        mv = sb("mmv", [P, TB, 2])
        var = sb("mvar", [P, TB])
        rstd = sb("mrstd", [P, TB])
        p_st = sb("p_st", [P, 2, 6])
        p_mv = [sb(f"p_mv{i}", [P, 2, 2]) for i in range(2)]
        p_var = [sb(f"p_var{i}", [P, 2]) for i in range(2)]
        p_rstd = [sb(f"p_rstd{i}", [P, 2]) for i in range(2)]
        filler = sb("mfiller", [P, 1])

        ps = ctx.enter_context(nc.psum_tensor("ps_moe", [P, 8, 512], F32))
        Y, H = 0, 4

        s_c = sem("biases_loaded")
        s_w = [sem(f"mw_loaded{i}") for i in range(SLOTS)]
        s_wh = sem("mw_hi_done")
        s_wlp = sem("mw_lo_done_by_pool")
        s_wld = sem("mw_lo_done_by_dve")
        s_id = sem("ids_ready")
        s_sig = sem("weight_ready")
        s_diag = sem("score_diagonals_ready")
        s_bc = sem("scores_broadcast")
        s_sb = sem("scores_taken")
        s_cnt = sem("counted")
        s_zero = sem("counts_zeroed")
        s_row = sem("row_ready")
        s_pst = sem("plain_stats_done")
        s_pag = sem("plain_aggregated")
        s_pvar = sem("plain_var_ready")
        s_prstd = sem("plain_rstd_ready")
        s_px = [sem(f"plain_loaded{i}") for i in range(SLOTS)]
        s_pout = sem("plain_rows_ready")
        s_all = [sem(f"plain_rows_stored{i}") for i in range(SLOTS)]
        s_tp = sem("mx_transposed")
        s_xth = sem("mxt_hi_done")
        s_xtl = sem("mxt_lo_done")
        s_h1 = sem("mh_projected")
        s_g = sem("gelu_done")
        s_hh = sem("mh_hi_done")
        s_hl = sem("mh_lo_done")
        s_y = sem("my_added")
        s_yt = sem("my_tile_whole")
        s_b2 = sem("b2_weighted")
        s_r = sem("mresidual_added")
        s_st = sem("mstats_done")
        s_ag = sem("maggregated")
        s_var = sem("mvar_ready")
        s_rstd = sem("mrstd_ready")
        s_out = sem("mx_out_ready")
        s_scat = sem_of_pool_dma("pairs_scattered")
        s_pr0 = sem("batch_0_pairs_loaded")
        s_pr = sem_of_pool_dma("batch_1_pairs_loaded")
        s_sel = sem_of_pool_dma("selected_gathered")
        s_fin = sem_of_pool_dma("selected_stored")

        start_semaphores(nc, sems)
        block = ctx.enter_context(nc.Block())

        NPL = NB * NT8 // 2
        NPB = NPL // NB

        def halves(n):
            kind, i = chunks[n]
            if kind == W1:
                return [w[:, :, 256 * i:256 * (i + 1)] for w in (w1_hi, w1_lo)]
            return [w[:, 2 * i:2 * i + 2, :] for w in (w2_hi, w2_lo)]

        def raw(n):
            w = w_raw[n % SLOTS][:, :, :]
            return w.rearrange("p a (k n) -> p (a k) n", n=256) if chunks[n][0] == W1 else w

        def lower_done(engine, n):
            if n < BY_POOL:
                engine.wait_ge(s_wlp, START + n + 1)
            else:
                engine.wait_ge(s_wld, START + n - BY_POOL + 1)

        def lower_half(engine, n):
            hi, lo = halves(n)
            engine.wait_ge(s_wh, START + n + 1)
            engine.tensor_tensor(lo, raw(n), hi.bitcast(F32), ALU.subtract).then_inc(s_wlp if n < BY_POOL else s_wld, 1)

        def plain_stored(engine, n):
            for i in range(SLOTS):
                engine.wait_ge(s_all[i], START + 16 * len(range(i, n, SLOTS)))

        def selected(b):
            return pairs[b][0:TOP, :].rearrange("(t p) c -> p t c", p=P)

        @block.sync
        def _(sp):
            for n in range(NCH):
                kind, i = chunks[n]
                if n >= SLOTS:
                    lower_done(sp, n - SLOTS)
                sp.dma_start(raw(n), w1[:, :, 256 * i:256 * (i + 1)] if kind == W1 else w2[:, 2 * i:2 * i + 2, :]).then_inc(s_w[n % SLOTS], 16)
                if n == SLOTS + 1:
                    sp.wait_ge(s_scat, 16 * NT8)
                    sp.dma_start(sel[0][:, :, :], selected(0)).then_inc(s_pr0, 16)
                if n == 1:
                    sp.dma_start(b2_sb[:, :], b2.to_broadcast([P, C])).then_inc(s_c, 16)
                    sp.dma_start(b1_sb[:, :], b1).then_inc(s_c, 16)
            for k in range(NPL + 1):
                if k < NPL:
                    if k < SLOTS:
                        for n in range(NCH - SLOTS, NCH):
                            if n % SLOTS == k:
                                lower_done(sp, n)
                    else:
                        sp.wait_ge(s_all[k % SLOTS], START + 16 * (k // SLOTS))
                    sp.dma_start(w_raw[k % SLOTS][:, :, :], x3[2 * k:2 * k + 2, :, :].rearrange("t p c -> p t c")).then_inc(s_px[k % SLOTS], 16)
                if k >= 1:
                    sp.wait_ge(s_pout, START + 2 * k)
                    sp.dma_start(out[2 * k - 2:2 * k, :, :].rearrange("t p c -> p t c"), w_raw[(k - 1) % SLOTS][:, :, :]).then_inc(s_all[(k - 1) % SLOTS], 16)
            plain_stored(sp, NPL)

        @block.scalar
        def _(act):
            def upper_half(n):
                act.wait_ge(s_w[n % SLOTS], START + 16 * (n // SLOTS + 1))
                act.activation(halves(n)[0], raw(n), ACT.Copy).then_inc(s_wh, 1)

            act.activation(pair[:, :, 1], score, ACT.Sigmoid).then_inc(s_sig, 1)
            for b in range(NB):
                act.wait_ge(s_bc, START + b + 1)
                act.activation(scores[b][:, :].rearrange("p (a n) -> p a n", a=2), ps[:, H + 2 * b:H + 2 * b + 2, :], ACT.Copy).then_inc(s_sb, 1)
            for n in range(EARLY):
                upper_half(n)
            act.wait_ge(s_c, START + 32)
            late = list(range(EARLY, NCH))
            for b in range(NB):
                for c in range(KC):
                    act.wait_ge(s_tp, START + KC * b + c + 1)
                    act.activation(xt_hi[:, c, :], ps[:, H + c, :], ACT.Copy).then_inc(s_xth, 1)
                for j in range(FT + 1):
                    if j < FT:
                        act.wait_ge(s_h1, START + FT * b + j + 1)
                        act.wait_ge(s_hl, START + FT * b + max(0, j - 1))
                        act.activation(h[j % 2][:, :], ps[:, H + j % 4, :], ACT.Gelu_apprx_tanh, bias=b1_sb[:, j:j + 1]).then_inc(s_g, 1)
                        act.wait_ge(s_g, START + FT * b + j + 1)
                        act.wait_ge(s_y, START + (FT - 1) * b + max(0, j - HS + 1))
                        if j == 0:
                            act.wait_ge(s_yt, START + TB * b)
                        act.activation(h_hi[j % HS][:, :], h[j % 2][:, :], ACT.Copy).then_inc(s_hh, 1)
                    for n in late[0:2]:
                        upper_half(n)
                    late = late[2:]

        @block.vector
        def _(dve):
            def ranks(b):
                k = (3 * NT8 - 1) * b
                for t in range(NT8):
                    s_t = score[:, NT8 * b + t:NT8 * b + t + 1]
                    todo = [(0, t * P, ALU.is_ge), (t * P, T, ALU.is_gt)] if t else [(0, T, ALU.is_gt)]
                    if t:
                        dve.wait_ge(s_cnt, START + k - 1)
                    for a, (lo, hi, op) in enumerate(todo):
                        dve.tensor_scalar(junk[:, lo:hi], scores[b][:, lo:hi], s_t, None, op, ALU.add,
                                          accum_out=counts[:, len(todo) - 1 - a, t:t + 1]).then_inc(s_cnt, 1)
                    k += len(todo)
                    if t:
                        dve.wait_ge(s_cnt, START + k - 2)
                    dve.scalar_tensor_tensor(out=junk_own[:, :], in0=scores[b][:, t * P:(t + 1) * P], scalar=s_t, in1=const.before[:, :],
                                             op0=ALU.is_equal, op1=ALU.mult, accum_out=counts[:, 2, t:t + 1]).then_inc(s_cnt, 1)
                    k += 1
                    dve.wait_ge(s_cnt, START + k)
                    dve.scalar_tensor_tensor(out=row[b][:, t:t + 1], in0=counts[:, 0, t:t + 1], scalar=counts[:, 1, t:t + 1],
                                             in1=counts[:, 2, t:t + 1], op0=ALU.add, op1=ALU.add).then_inc(s_row, 1)

            def x_low(b):
                for c in range(KC):
                    dve.wait_ge(s_xth, START + KC * b + c + 1)
                    dve.tensor_tensor(xt_lo[:, c, :], ps[:, H + c, :], xt_hi[:, c, :].bitcast(F32), ALU.subtract).then_inc(s_xtl, 1)

            def plain_statistics(k):
                dve.wait_ge(s_px[k % SLOTS], START + 16 * (k // SLOTS + 1))
                dve.wait_ge(s_pag, START + 2 * k)
                dve.memset(filler[:, :], 0.0)
                for t in range(2):
                    dve.bn_stats(p_st[:, t, :], w_raw[k % SLOTS][:, t, :]).then_inc(s_pst, 1)
                dve.wait_ge(s_pst, START + 2 * k + 2)
                dve.memset(filler[:, :], 0.0)
                for t in range(2):
                    dve.bn_aggr(p_mv[k % 2][:, t, :], p_st[:, t, :]).then_inc(s_pag, 1)
                dve.wait_ge(s_pag, START + 2 * k + 2)
                dve.tensor_scalar(p_var[k % 2][:, :], p_mv[k % 2][:, :, 1], LN_EPS / 4, None, ALU.add).then_inc(s_pvar, 1)

            def plain_normalise(k):
                dve.wait_ge(s_prstd, START + k + 1)
                w = w_raw[k % SLOTS]
                for t in range(2):
                    dve.tensor_scalar(w[:, t, :], w[:, t, :], p_mv[k % 2][:, t, 0:1], p_rstd[k % 2][:, t:t + 1], ALU.subtract,
                                      ALU.mult).then_inc(s_pout, 1)

            def residual(b):
                dve.wait_ge(s_tp, START + KC * b + KC)
                for t in range(TB):
                    dve.tensor_scalar(xsel[b][:, t, :], xsel[b][:, t, :], 2.0, None, ALU.mult).then_inc(s_b2, 1)
                for t in range(TB):
                    dve.wait_ge(s_b2, START + 2 * TB * b + t + 1)
                    dve.scalar_tensor_tensor(out=xsel[b][:, t, :], in0=b2_sb[:, :], scalar=sel[b][:, t, 1:2], in1=xsel[b][:, t, :],
                                             op0=ALU.mult, op1=ALU.add).then_inc(s_b2, 1)

            def add_outputs(b):
                for t in range(TB):
                    dve.wait_ge(s_yt, START + TB * b + t + 1)
                    dve.wait_ge(s_b2, START + 2 * TB * b + TB + t + 1)
                    dve.scalar_tensor_tensor(out=xsel[b][:, t, :], in0=ps[:, Y + t, :], scalar=sel[b][:, t, 1:2], in1=xsel[b][:, t, :],
                                             op0=ALU.mult, op1=ALU.add).then_inc(s_r, 1)

            dve.memset(counts[:, 1, :], 0.0).then_inc(s_zero, 1)
            for b in range(NB):
                tiles = slice(NT8 * b, NT8 * (b + 1))
                dve.tensor_tensor(diag[:, tiles, :], const.ident[:, :].unsqueeze(1).to_broadcast([P, NT8, P]),
                                  score[:, tiles].unsqueeze(2).to_broadcast([P, NT8, P]), ALU.mult).then_inc(s_diag, 1)
            dve.wait_ge(s_sb, START + 1)
            dve.wait_ge(s_zero, START + 1)
            ranks(0)
            for n in range(BY_POOL, EARLY):
                lower_half(dve, n)
            x_low(0)
            for n in range(EARLY, NCH):
                lower_half(dve, n)
            dve.wait_ge(s_sb, START + 2)
            ranks(1)
            dve.wait_ge(s_c, START + 32)
            for b in range(NB):
                for k in range(NPB * b, NPB * (b + 1) + 1):
                    if k < NPB * (b + 1):
                        plain_statistics(k)
                    if k > NPB * b:
                        plain_normalise(k - 1)
                residual(b)
                if b + 1 < NB:
                    x_low(b + 1)
                add_outputs(b)
                layer_norm_block(dve, b, xsel[b], st, mv, var, rstd, filler, s_r, s_st, s_ag, s_var, s_rstd, s_out)

        @block.gpsimd
        def _(pool):
            def scatter_pairs(b, t):
                pool.indirect_dma_start(pairs[b], bass.IndirectOffsetOnAxis(ap=row[b][:, t:t + 1], axis=0),
                                        pair[:, NT8 * b + t, :], None).then_inc(s_scat, 16)

            def load_selected(b):
                pool.wait_ge(s_scat, 16 * NT8 * (b + 1))
                pool.dma_start(sel[b][:, :, :], selected(b)).then_inc(s_pr, 16)

            def gather(b, t):
                pool.indirect_dma_start(xsel[b][:, t, :], None, x3.rearrange("n p c -> (n p) c"),
                                        bass.IndirectOffsetOnAxis(ap=sel[b][:, t, 0:1].bitcast(I32), axis=0)).then_inc(s_sel, 16)

            def store_selected(b, t):
                pool.indirect_dma_start(out.rearrange("n p c -> (n p) c"), bass.IndirectOffsetOnAxis(ap=sel[b][:, t, 0:1].bitcast(I32), axis=0),
                                        xsel[b][:, t, :], None).then_inc(s_fin, 16)

            def plain_rstd(k):
                pool.wait_ge(s_pvar, START + k + 1)
                pool.tensor_tensor(p_rstd[k % 2][:, :], p_var[k % 2][:, :], const.minus_half[:, 0:2], ALU.pow).then_inc(s_prstd, 1)

            def selected_rstd(b):
                pool.wait_ge(s_var, START + b + 1)
                pool.tensor_tensor(rstd[:, :], var[:, :], const.minus_half[:, :], ALU.pow).then_inc(s_rstd, 1)

            def between(b, j):
                if b == 0:
                    if j == ROUTE:
                        pool.wait_ge(s_row, START + 2 * NT8)
                    if ROUTE <= j < ROUTE + 4:
                        scatter_pairs(1, 2 * (j - ROUTE))
                        scatter_pairs(1, 2 * (j - ROUTE) + 1)
                    if j == ROUTE + 4:
                        load_selected(1)
                    if j == ROUTE + 5:
                        pool.wait_ge(s_pr, 16)
                    if ROUTE + 5 <= j < ROUTE + 7:
                        gather(1, 2 * (j - ROUTE - 5))
                        gather(1, 2 * (j - ROUTE - 5) + 1)
                    if PLAIN <= j < PLAIN + NPB:
                        plain_rstd(j - PLAIN)
                else:
                    if j == 2:
                        selected_rstd(0)
                    if j == 4:
                        pool.wait_ge(s_out, START + TB)
                        plain_stored(pool, NPB)
                    if 4 <= j < 4 + TB:
                        store_selected(0, j - 4)
                    if PLAIN <= j < PLAIN + NPB:
                        plain_rstd(NPB + j - PLAIN)

            PLAIN = 10
            ROUTE = 7
            pool.iota(pair[:, :, 0].bitcast(I32), pattern=[[P, NB * NT8]], base=0, channel_multiplier=1).then_inc(s_id, 1)
            for n in range(BY_POOL):
                lower_half(pool, n)
            pool.wait_ge(s_sig, START + 1)
            pool.wait_ge(s_id, START + 1)
            for t in range(NT8):
                pool.wait_ge(s_row, START + t + 1)
                scatter_pairs(0, t)
            pool.wait_ge(s_pr0, START + 16)
            for t in range(TB):
                gather(0, t)
            for b in range(NB):
                for j in range(FT):
                    pool.wait_ge(s_hh, START + FT * b + j + 1)
                    pool.wait_ge(s_y, START + (FT - 1) * b + max(0, j - HS + 1))
                    if j == 0:
                        pool.wait_ge(s_yt, START + TB * b)
                    pool.tensor_tensor(h_lo[j % HS][:, :], h[j % 2][:, :], h_hi[j % HS][:, :].bitcast(F32), ALU.subtract).then_inc(s_hl, 1)
                    between(b, j)
            selected_rstd(1)
            plain_stored(pool, NPL)
            for t in range(TB):
                pool.wait_ge(s_out, START + TB + t + 1)
                store_selected(1, t)
            pool.wait_ge(s_fin, 16 * TB * NB)

        @block.tensor
        def _(pe):
            def transposes(b):
                pe.wait_ge(s_sel, 16 * TB * (b + 1))
                for c in range(KC):
                    pe.wait_ge(s_g, START + FT * b - KC * min(b, 1) + (c + 1) * min(b, 1))
                    for t in range(TB):
                        ins = pe.transpose(ps[:, H + c, t * P:(t + 1) * P], xsel[b][:, t, c * P:(c + 1) * P], const.ident[:, :])
                    ins.then_inc(s_tp, 1)

            def up(b, j):
                if j < 4:
                    pe.wait_ge(s_xtl, START + KC * b + KC)
                else:
                    pe.wait_ge(s_g, START + FT * b + j - 3)
                if b == 0:
                    lower_done(pe, chunks.index((W1, j // 2)))
                for c in range(KC):
                    ins = three_products(pe, ps[:, H + j % 4, :], w1_hi[:, c, j * P:(j + 1) * P], w1_lo[:, c, j * P:(j + 1) * P],
                                         xt_hi[:, c, :], xt_lo[:, c, :], c == 0, c == KC - 1)
                ins.then_inc(s_h1, 1)

            def down(b, j):
                pe.wait_ge(s_hh, START + FT * b + j + 1)
                pe.wait_ge(s_hl, START + FT * b + j + 1)
                if b == 0:
                    lower_done(pe, chunks.index((W2, j // 2)))
                for t in range(TB):
                    if j == 0 and b:
                        pe.wait_ge(s_r, START + TB * (b - 1) + t + 1)
                    ins = three_products(pe, ps[:, Y + t, :], h_hi[j % HS][:, t * P:(t + 1) * P], h_lo[j % HS][:, t * P:(t + 1) * P],
                                         w2_hi[:, j, :], w2_lo[:, j, :], j == 0, j == FT - 1)
                    if j == FT - 1:
                        ins.then_inc(s_yt, 1)
                if j < FT - 1:
                    ins.then_inc(s_y, 1)

            for b in range(NB):
                pe.wait_ge(s_diag, START + b + 1)
                for a in range(2):
                    ins = pe.matmul(ps[:, H + 2 * b + a, :], const.ones[:, :],
                                    diag[:, NT8 * b + 4 * a:NT8 * b + 4 * a + 4, :].rearrange("p a n -> p (a n)"), start=True, stop=True)
                ins.then_inc(s_bc, 1)
            pe.wait_ge(s_sb, START + NB)
            transposes(0)
            for b in range(NB):
                up(b, 0)
                up(b, 1)
                for j in range(2, FT):
                    up(b, j)
                    down(b, j - 2)
                down(b, FT - 2)
                if b + 1 < NB:
                    transposes(b + 1)
                down(b, FT - 1)


def transformer_two_layers(nc, x, xT, wqT, wkT, wvT, woT, gu_packed, gu_scales, dn_packed, dn_scales,
                           wqkT, wogT, wigT, wo1T, norm_w, router_w, router_b, w1, b1, w2, b2, out):
    def tiles(a):
        return a.rearrange("(n p) c -> n p c", p=P)

    def contracted(a):
        return a.rearrange("(k p) n -> p k n", p=P)

    x1, x2, x3 = (tiles(nc.dram_tensor(name, [NB * T, C], F32).ap()) for name in ("x1", "x2", "x3"))
    pairs = [nc.dram_tensor(f"routed_pairs{b}", [T, 2], F32).ap() for b in range(NB)]
    with ExitStack() as ctx:
        const = Constants(nc, ctx)
        score = ctx.enter_context(nc.sbuf_tensor("score", [P, TB + NB * NT8], F32))
        linear_attention(nc, tiles(x), contracted(xT), [contracted(wkT), contracted(wvT), contracted(wqT)],
                         contracted(woT), x1, const)
        with ExitStack() as carried:
            rows = FinishRows(nc, carried, x1, x2, const)
            fp4_feed_forward(nc, x1, gu_packed.rearrange("(k w) o -> w k o", w=P // NIB), gu_scales, dn_packed,
                             dn_scales, rows, const)
            gated_linear_attention(nc, x2, contracted(wqkT), contracted(wogT), contracted(wigT), contracted(wo1T),
                                   norm_w, router_w, router_b, x3, score, rows, const)
        routed_feed_forward(nc, x3, score[:, TB:TB + NB * NT8], contracted(w1), b1, contracted(w2), b2, pairs,
                            tiles(out), const)


def kernel(**inputs):
    import numpy as np
    import concourse.bacc as bacc
    from concourse.bass_utils import run_bass_kernel_spmd

    a = {name: np.asarray(value) for name, value in inputs.items()}
    x = a["L0_attn_x"].reshape(NB * T, C)
    laid_out = {
        "x": x,
        "xT": x.T,
        "wqT": a["L0_attn_Wq"].T,
        "wkT": a["L0_attn_Wk"].T,
        "wvT": a["L0_attn_Wv"].T,
        "woT": a["L0_attn_Wo"].T,
        "gate_up_packed": a["L0_ffn_gate_up_packed"].T,
        "gate_up_scales": a["L0_ffn_gate_up_scales"].reshape(KC, 2 * IT, P).transpose(2, 1, 0),
        "down_packed": a["L0_ffn_down_packed"].T,
        "down_scales": a["L0_ffn_down_scales"],
        "gla_wqkT": np.concatenate([a["L1_attn_Wq"], a["L1_attn_Wk"]]).T,
        "gla_wogT": a["L1_attn_Wog"].T,
        "gla_wigT": a["L1_attn_Wig"].T,
        "gla_woT": a["L1_attn_Wo"].T,
        "gla_norm_w": a["L1_attn_g_norm_w"].reshape(KC, P).T,
        "router_w": a["L1_ffn_router_weight"].reshape(1, C),
        "router_b": a["L1_ffn_router_bias"].reshape(1, 1),
        "w1": a["L1_ffn_w1"],
        "b1": a["L1_ffn_b1"].reshape(FT, P).T,
        "w2": a["L1_ffn_w2"],
        "b2": a["L1_ffn_b2"].reshape(1, C),
    }
    nc = bacc.Bacc("TRN2", target_bir_lowering=False, num_devices=1)
    arrays, args = {}, []
    for name, value in laid_out.items():
        arrays[f"in_{name}"] = np.ascontiguousarray(value)
        args.append(nc.dram_tensor(f"in_{name}", value.shape, mybir.dt.from_np(value.dtype), kind="ExternalInput").ap())
    args.append(nc.dram_tensor("out", (NB * T, C), F32, kind="ExternalOutput").ap())
    transformer_two_layers(nc, *args)
    result = run_bass_kernel_spmd(nc, [arrays], core_ids=[0])
    return result.results[0]["out"].reshape(NB, T, C)
```
